# Optimizing a Trainium2 kernel written in Bass

```python
import numpy as np
import jax
import jax.numpy as jnp

def _softmax(x, axis=-1):
    return jax.nn.softmax(x, axis=axis)

def _gelu(x):
    return jax.nn.gelu(x, approximate=True)

def _silu(x):
    return jax.nn.silu(x)

def _sigmoid(x):
    return jax.nn.sigmoid(x)

def _layernorm(x, axis=-1, eps=1e-05):
    m = jnp.mean(x, axis=axis, keepdims=True)
    v = jnp.var(x, axis=axis, keepdims=True)
    return (x - m) / jnp.sqrt(v + eps)

def _scatter_add(tgt, idx, src, axis=0):
    return tgt.at[idx].add(src)

def _segment_sum(src, seg, n):
    return jax.ops.segment_sum(src, seg, n)
kernel_name = 'mk_adj_ffn_d4_adj_r2_62e2bc'

def setup_inputs(seed: int=0):
    np.random.seed(seed)
    _w = jnp.asarray

    def _rec_inputs():
        import jax
        import jax.numpy as jnp
        _gk = jax.random.key(seed)
        x = -2.104e-05 + 0.9999 * jax.random.normal(jax.random.fold_in(_gk, 1), (16, 512, 128), jnp.float32)
        _w = (1.0 + jnp.arange(512, dtype=jnp.float32)) ** (-0.5)
        _w = _w / _w.mean()
        _pij = jnp.clip(0.00390625 * _w[:, None] * _w[None, :], 0.0, 1.0)
        _a = jax.random.uniform(jax.random.fold_in(_gk, 2), (512, 512)) < _pij
        _a = jnp.logical_or(_a, jnp.swapaxes(_a, -1, -2))
        _af = _a.astype(jnp.float32)
        _af = _af / jnp.maximum(_af.sum(-1, keepdims=True), 1.0)
        adj = _af
        return (x, adj)
    x, adj = _rec_inputs()

    def _L0_gnn_setup():
        import jax, jax.numpy as jnp
        import numpy as np
        N = 3445
        B = 32
        IN_DIM = 128
        HID_DIM = 128

        def _make_adj(key):
            a = jax.random.uniform(key, (N, N), dtype=jnp.float32)
            a = (a < 0.001).astype(jnp.float32)
            a = jnp.maximum(a, a.T)
            deg = jnp.sum(a, axis=1, keepdims=True)
            return a / jnp.maximum(deg, 1.0)

        def _graph_conv(x, adj, w_loop, w_neigh, b):
            loop = jnp.einsum('bnd,dh->bnh', x, w_loop)
            neigh = jnp.einsum('nm,bmh->bnh', adj, jnp.einsum('bnd,dh->bnh', x, w_neigh))
            return loop + neigh + b
        key = jax.random.key(seed)
        k = jax.random.split(key, 8)
        s1 = 1.0 / np.sqrt(IN_DIM)
        s2 = 1.0 / np.sqrt(HID_DIM)
        return {'x': jax.random.normal(k[0], (B, N, IN_DIM), dtype=jnp.float32), 'adj': _make_adj(k[1]), 'w1_loop': jax.random.normal(k[2], (IN_DIM, HID_DIM), dtype=jnp.float32) * s1, 'w1_neigh': jax.random.normal(k[3], (IN_DIM, HID_DIM), dtype=jnp.float32) * s1, 'b1': jnp.zeros((HID_DIM,), dtype=jnp.float32), 'w2_loop': jax.random.normal(k[4], (HID_DIM, IN_DIM), dtype=jnp.float32) * s2, 'w2_neigh': jax.random.normal(k[5], (HID_DIM, IN_DIM), dtype=jnp.float32) * s2, 'b2': jnp.zeros((IN_DIM,), dtype=jnp.float32)}
    _L0_gnn_all = _L0_gnn_setup()
    _L0_gnn_in = {k: v for k, v in _L0_gnn_all.items() if k in ('w1_loop', 'w1_neigh', 'b1', 'w2_loop', 'w2_neigh', 'b2')}
    del _L0_gnn_all

    def _L0_ffn_setup():
        import jax, jax.numpy as jnp
        import numpy as np
        D_MODEL = 128
        EXPERT_DIM = 256
        NUM_EXPERTS = 8
        TOP_K = 2
        SEQ_LEN = 1024
        BATCH = 2
        key = jax.random.key(seed)
        ks = jax.random.split(key, 8)
        s = 0.02
        x = jax.random.normal(ks[0], (SEQ_LEN, BATCH, D_MODEL), dtype=jnp.float32)
        Wg = jax.random.normal(ks[1], (D_MODEL, NUM_EXPERTS), dtype=jnp.float32) * s
        bg = jax.random.normal(ks[2], (NUM_EXPERTS,), dtype=jnp.float32) * s
        bias = jnp.zeros((NUM_EXPERTS,), dtype=jnp.float32)
        W1 = jax.random.normal(ks[3], (NUM_EXPERTS, D_MODEL, EXPERT_DIM), dtype=jnp.float32) * s
        b1 = jax.random.normal(ks[4], (NUM_EXPERTS, EXPERT_DIM), dtype=jnp.float32) * s
        W2 = jax.random.normal(ks[5], (NUM_EXPERTS, EXPERT_DIM, D_MODEL), dtype=jnp.float32) * s
        b2 = jax.random.normal(ks[6], (NUM_EXPERTS, D_MODEL), dtype=jnp.float32) * s
        return {'x': x, 'Wg': Wg, 'bg': bg, 'bias': bias, 'W1': W1, 'b1': b1, 'W2': W2, 'b2': b2}
    _L0_ffn_all = _L0_ffn_setup()
    _L0_ffn_in = {k: v for k, v in _L0_ffn_all.items() if k in ('Wg', 'bg', 'bias', 'W1', 'b1', 'W2', 'b2')}
    del _L0_ffn_all

    def _L1_gnn_setup():
        import jax, jax.numpy as jnp
        import numpy as np
        B, N, C, D = (8, 1024, 128, 128)
        NEG = -1e+16
        key = jax.random.key(seed)
        k1, k2, k3, k4, k5 = jax.random.split(key, 5)
        inputs = jax.random.normal(k1, (B, N, C), dtype=jnp.float32)
        graph = jax.random.bernoulli(k2, 0.5, (N, N)).astype(jnp.float32)
        W = jax.random.normal(k3, (C, D), dtype=jnp.float32) * (1.0 / np.sqrt(C))
        b_lin = jax.random.normal(k4, (D,), dtype=jnp.float32) * 0.02
        b = jax.random.normal(k5, (D,), dtype=jnp.float32)
        return {'inputs': inputs, 'graph': graph, 'W': W, 'b_lin': b_lin, 'b': b}
    _L1_gnn_all = _L1_gnn_setup()
    _L1_gnn_in = {k: v for k, v in _L1_gnn_all.items() if k in ('W', 'b_lin', 'b')}
    del _L1_gnn_all

    def _L1_ffn_setup():
        import jax, jax.numpy as jnp
        import numpy as np
        NUM_EXPERTS = 8
        TOP_K = 2
        B, S, D = (8, 4096, 128)

        def _moe(tokens, router_w, w1, b1, w2, b2):
            N = tokens.shape[0]
            E = router_w.shape[0]
            logits = tokens.astype(jnp.float32) @ router_w.astype(jnp.float32).T
            probs = jax.nn.softmax(logits, axis=-1)
            rw, re = jax.lax.top_k(probs, TOP_K)
            if TOP_K > 1:
                rw = rw / jnp.maximum(rw.sum(-1, keepdims=True), 1e-12)
            rw = rw.astype(tokens.dtype)
            combine = jnp.zeros((N, E), tokens.dtype).at[jnp.arange(N)[:, None], re].set(rw)
            out = tokens
            for e in range(E):
                h = jax.nn.gelu(tokens @ w1[e] + b1[e], approximate=False)
                y = h @ w2[e] + b2[e]
                out = out + combine[:, e:e + 1] * y
            return out
        key = jax.random.key(seed)
        ks = jax.random.split(key, 4)
        scale = 1.0 / np.sqrt(D).astype(np.float32)
        return {'input_embeddings': jax.random.normal(ks[0], (B, S, D), jnp.float32), 'router_w': jax.random.normal(ks[1], (NUM_EXPERTS, D), jnp.float32) * scale, 'w1': jax.random.normal(ks[2], (NUM_EXPERTS, D, D), jnp.float32) * scale, 'b1': jnp.zeros((NUM_EXPERTS, D), jnp.float32), 'w2': jax.random.normal(ks[3], (NUM_EXPERTS, D, D), jnp.float32) * scale, 'b2': jnp.zeros((NUM_EXPERTS, D), jnp.float32)}
    _L1_ffn_all = _L1_ffn_setup()
    _L1_ffn_in = {k: v for k, v in _L1_ffn_all.items() if k in ('router_w', 'w1', 'b1', 'w2', 'b2')}
    del _L1_ffn_all

    def _L2_gnn_setup():
        import jax, jax.numpy as jnp
        import numpy as np
        N_STEPS = 8
        SPATIAL_SCALE = 1.0
        key = jax.random.key(seed)
        ks = jax.random.split(key, 6)
        B, N, D = (32, 512, 128)
        x = jax.random.normal(ks[0], (B, N, D), dtype=jnp.float32)
        adj_mx = jax.random.uniform(ks[1], (N, N), dtype=jnp.float32) / N
        alpha_train = jnp.ones((N,), dtype=jnp.float32)
        w = jnp.eye(D, dtype=jnp.float32) + 0.01 * jax.random.normal(ks[2], (D, D), dtype=jnp.float32)
        d = jax.random.uniform(ks[3], (D,), dtype=jnp.float32)
        fc_in_w = jax.random.normal(ks[4], (D, D), dtype=jnp.float32) * (1.0 / np.sqrt(D))
        fc_in_b = jnp.zeros((D,), dtype=jnp.float32)
        return {'x': x, 'adj_mx': adj_mx, 'alpha_train': alpha_train, 'w': w, 'd': d, 'fc_in_w': fc_in_w, 'fc_in_b': fc_in_b, 'vt': 0}
    _L2_gnn_all = _L2_gnn_setup()
    _L2_gnn_in = {k: v for k, v in _L2_gnn_all.items() if k in ('alpha_train', 'w', 'd', 'fc_in_w', 'fc_in_b')}
    del _L2_gnn_all

    def _L2_ffn_setup():
        import jax, jax.numpy as jnp
        import numpy as np
        B, T, D, H, L = (16, 2048, 128, 128, 2)

        def _lstm(x, W_ih, W_hh, b_ih, b_hh):
            x_proj = jnp.einsum('btd,gd->btg', x, W_ih) + b_ih + b_hh
            h0 = jnp.zeros((x.shape[0], W_hh.shape[1]), x.dtype)
            c0 = jnp.zeros_like(h0)

            def step(carry, xp):
                h, c = carry
                gates = xp + h @ W_hh.T
                i, f, g, o = jnp.split(gates, 4, axis=-1)
                c = jax.nn.sigmoid(f) * c + jax.nn.sigmoid(i) * jnp.tanh(g)
                h = jax.nn.sigmoid(o) * jnp.tanh(c)
                return ((h, c), h)
            _, hs = jax.lax.scan(step, (h0, c0), jnp.swapaxes(x_proj, 0, 1))
            return jnp.swapaxes(hs, 0, 1)
        key = jax.random.key(seed)
        ks = jax.random.split(key, 9)
        s = 1.0 / np.sqrt(H)
        u = lambda k, shape: jax.random.uniform(k, shape, jnp.float32, -s, s)
        return {'x': jax.random.normal(ks[0], (B, T, D), jnp.float32), 'W_ih': u(ks[1], (4 * H, D)), 'W_hh': u(ks[2], (4 * H, H)), 'b_ih': u(ks[3], (4 * H,)), 'b_hh': u(ks[4], (4 * H,)), 'W_lin': u(ks[5], (L, H)), 'b_lin': u(ks[6], (L,)), 'fw_att': jnp.full((1, H), 0.001, jnp.float32), 'bw_att': jnp.full((1, H), 0.001, jnp.float32)}
    _L2_ffn_all = _L2_ffn_setup()
    _L2_ffn_in = {k: v for k, v in _L2_ffn_all.items() if k in ('W_ih', 'W_hh', 'b_ih', 'b_hh', 'W_lin', 'b_lin', 'fw_att', 'bw_att')}
    del _L2_ffn_all

    def _L3_gnn_setup():
        import jax, jax.numpy as jnp
        import numpy as np
        B, T, D, H = (64, 1024, 128, 128)
        MAX_SKIP = 4

        def _lstm_last(Wih, Whh, bih, bhh, xs):
            N, _, Hd = xs.shape
            bias = bih + bhh

            def step(carry, x_t):
                h, c = carry
                g = x_t @ Wih.T + h @ Whh.T + bias
                i, f, gg, o = jnp.split(g, 4, axis=-1)
                c = jax.nn.sigmoid(f) * c + jax.nn.sigmoid(i) * jnp.tanh(gg)
                h = jax.nn.sigmoid(o) * jnp.tanh(c)
                return ((h, c), None)
            init = (jnp.zeros((N, Hd), xs.dtype), jnp.zeros((N, Hd), xs.dtype))
            (h_last, _), _ = jax.lax.scan(step, init, jnp.swapaxes(xs, 0, 1))
            return h_last
        key = jax.random.key(seed)
        ks = jax.random.split(key, 8)
        s = 0.05
        x = jax.random.normal(ks[0], (B, T, D), jnp.float32)
        adj = jax.random.uniform(ks[1], (T, T), jnp.float32) / T
        Wg0 = jax.random.normal(ks[2], (D, H), jnp.float32) * s
        bg0 = jnp.zeros((H,), jnp.float32)
        Wg1 = jax.random.normal(ks[3], (H, H), jnp.float32) * s
        bg1 = jnp.zeros((H,), jnp.float32)
        Wih = jax.random.normal(ks[4], (MAX_SKIP, 4 * H, H), jnp.float32) * s
        Whh = jax.random.normal(ks[5], (MAX_SKIP, 4 * H, H), jnp.float32) * s
        bih = jax.random.normal(ks[6], (MAX_SKIP, 4 * H), jnp.float32) * s
        bhh = jax.random.normal(ks[7], (MAX_SKIP, 4 * H), jnp.float32) * s
        return dict(x=x, adj=adj, Wg0=Wg0, bg0=bg0, Wg1=Wg1, bg1=bg1, Wih=Wih, Whh=Whh, bih=bih, bhh=bhh)
    _L3_gnn_all = _L3_gnn_setup()
    _L3_gnn_in = {k: v for k, v in _L3_gnn_all.items() if k in ('Wg0', 'bg0', 'Wg1', 'bg1', 'Wih', 'Whh', 'bih', 'bhh')}
    del _L3_gnn_all

    def _L3_ffn_setup():
        import jax, jax.numpy as jnp
        import numpy as np
        B, T, C = (64, 192, 128)
        NH, NKV = (4, 2)
        HD = C // NH
        NREP = NH // NKV
        NE, TOPK = (8, 2)
        HID = int(8 / 3 * C)
        EPS_RMS = 1e-06

        def _rope_tables(t_len):
            inv_freq = 1.0 / 10000.0 ** (np.arange(0, HD, 2, dtype=np.float32) / HD)
            t = np.arange(t_len, dtype=np.float32)
            freqs = np.outer(t, inv_freq)
            emb = np.concatenate([freqs, freqs], axis=-1)
            return (jnp.asarray(np.cos(emb)), jnp.asarray(np.sin(emb)))

        def _rotate_half(x):
            h = x.shape[-1] // 2
            return jnp.concatenate([-x[..., h:], x[..., :h]], axis=-1)

        def _rmsnorm(v, w):
            return v * jax.lax.rsqrt(jnp.mean(v * v, axis=-1, keepdims=True) + EPS_RMS) * w
        key = jax.random.key(seed)
        ks = jax.random.split(key, 10)
        s = lambda k, shape: jax.random.normal(k, shape, jnp.float32) * 0.02
        return {'x': jax.random.normal(ks[0], (B, T, C), jnp.float32), 'ln1_w': jnp.ones((C,), jnp.float32), 'ln2_w': jnp.ones((C,), jnp.float32), 'wq': s(ks[1], (NH * HD, C)), 'wk': s(ks[2], (NKV * HD, C)), 'wv': s(ks[3], (NKV * HD, C)), 'wo': s(ks[4], (C, C)), 'router_w': s(ks[5], (NE, C)), 'w1': s(ks[6], (NE, HID, C)), 'w2': s(ks[7], (NE, C, HID)), 'w3': s(ks[8], (NE, HID, C))}
    _L3_ffn_all = _L3_ffn_setup()
    _L3_ffn_in = {k: v for k, v in _L3_ffn_all.items() if k in ('ln1_w', 'ln2_w', 'wq', 'wk', 'wv', 'wo', 'router_w', 'w1', 'w2', 'w3')}
    del _L3_ffn_all
    return {'x': x, 'adj': adj, 'L0_gnn_w1_loop': _L0_gnn_in['w1_loop'], 'L0_gnn_w1_neigh': _L0_gnn_in['w1_neigh'], 'L0_gnn_b1': _L0_gnn_in['b1'], 'L0_gnn_w2_loop': _L0_gnn_in['w2_loop'], 'L0_gnn_w2_neigh': _L0_gnn_in['w2_neigh'], 'L0_gnn_b2': _L0_gnn_in['b2'], 'L0_ffn_Wg': _L0_ffn_in['Wg'], 'L0_ffn_bg': _L0_ffn_in['bg'], 'L0_ffn_bias': _L0_ffn_in['bias'], 'L0_ffn_W1': _L0_ffn_in['W1'], 'L0_ffn_b1': _L0_ffn_in['b1'], 'L0_ffn_W2': _L0_ffn_in['W2'], 'L0_ffn_b2': _L0_ffn_in['b2'], 'L1_gnn_W': _L1_gnn_in['W'], 'L1_gnn_b_lin': _L1_gnn_in['b_lin'], 'L1_gnn_b': _L1_gnn_in['b'], 'L1_ffn_router_w': _L1_ffn_in['router_w'], 'L1_ffn_w1': _L1_ffn_in['w1'], 'L1_ffn_b1': _L1_ffn_in['b1'], 'L1_ffn_w2': _L1_ffn_in['w2'], 'L1_ffn_b2': _L1_ffn_in['b2'], 'L2_gnn_alpha_train': _L2_gnn_in['alpha_train'], 'L2_gnn_w': _L2_gnn_in['w'], 'L2_gnn_d': _L2_gnn_in['d'], 'L2_gnn_fc_in_w': _L2_gnn_in['fc_in_w'], 'L2_gnn_fc_in_b': _L2_gnn_in['fc_in_b'], 'L2_ffn_W_ih': _L2_ffn_in['W_ih'], 'L2_ffn_W_hh': _L2_ffn_in['W_hh'], 'L2_ffn_b_ih': _L2_ffn_in['b_ih'], 'L2_ffn_b_hh': _L2_ffn_in['b_hh'], 'L2_ffn_W_lin': _L2_ffn_in['W_lin'], 'L2_ffn_b_lin': _L2_ffn_in['b_lin'], 'L2_ffn_fw_att': _L2_ffn_in['fw_att'], 'L2_ffn_bw_att': _L2_ffn_in['bw_att'], 'L3_gnn_Wg0': _L3_gnn_in['Wg0'], 'L3_gnn_bg0': _L3_gnn_in['bg0'], 'L3_gnn_Wg1': _L3_gnn_in['Wg1'], 'L3_gnn_bg1': _L3_gnn_in['bg1'], 'L3_gnn_Wih': _L3_gnn_in['Wih'], 'L3_gnn_Whh': _L3_gnn_in['Whh'], 'L3_gnn_bih': _L3_gnn_in['bih'], 'L3_gnn_bhh': _L3_gnn_in['bhh'], 'L3_ffn_ln1_w': _L3_ffn_in['ln1_w'], 'L3_ffn_ln2_w': _L3_ffn_in['ln2_w'], 'L3_ffn_wq': _L3_ffn_in['wq'], 'L3_ffn_wk': _L3_ffn_in['wk'], 'L3_ffn_wv': _L3_ffn_in['wv'], 'L3_ffn_wo': _L3_ffn_in['wo'], 'L3_ffn_router_w': _L3_ffn_in['router_w'], 'L3_ffn_w1': _L3_ffn_in['w1'], 'L3_ffn_w2': _L3_ffn_in['w2'], 'L3_ffn_w3': _L3_ffn_in['w3']}

def reference(x, adj, L0_gnn_w1_loop, L0_gnn_w1_neigh, L0_gnn_b1, L0_gnn_w2_loop, L0_gnn_w2_neigh, L0_gnn_b2, L0_ffn_Wg, L0_ffn_bg, L0_ffn_bias, L0_ffn_W1, L0_ffn_b1, L0_ffn_W2, L0_ffn_b2, L1_gnn_W, L1_gnn_b_lin, L1_gnn_b, L1_ffn_router_w, L1_ffn_w1, L1_ffn_b1, L1_ffn_w2, L1_ffn_b2, L2_gnn_alpha_train, L2_gnn_w, L2_gnn_d, L2_gnn_fc_in_w, L2_gnn_fc_in_b, L2_ffn_W_ih, L2_ffn_W_hh, L2_ffn_b_ih, L2_ffn_b_hh, L2_ffn_W_lin, L2_ffn_b_lin, L2_ffn_fw_att, L2_ffn_bw_att, L3_gnn_Wg0, L3_gnn_bg0, L3_gnn_Wg1, L3_gnn_bg1, L3_gnn_Wih, L3_gnn_Whh, L3_gnn_bih, L3_gnn_bhh, L3_ffn_ln1_w, L3_ffn_ln2_w, L3_ffn_wq, L3_ffn_wk, L3_ffn_wv, L3_ffn_wo, L3_ffn_router_w, L3_ffn_w1, L3_ffn_w2, L3_ffn_w3):
    import jax
    import jax.numpy as jnp

    def _L0_gnn_ref(x, adj, w1_loop, w1_neigh, b1, w2_loop, w2_neigh, b2):
        import jax, jax.numpy as jnp
        import numpy as np
        N = 3445
        B = 32
        IN_DIM = 128
        HID_DIM = 128

        def _make_adj(key):
            a = jax.random.uniform(key, (N, N), dtype=jnp.float32)
            a = (a < 0.001).astype(jnp.float32)
            a = jnp.maximum(a, a.T)
            deg = jnp.sum(a, axis=1, keepdims=True)
            return a / jnp.maximum(deg, 1.0)

        def _graph_conv(x, adj, w_loop, w_neigh, b):
            loop = jnp.einsum('bnd,dh->bnh', x, w_loop)
            neigh = jnp.einsum('nm,bmh->bnh', adj, jnp.einsum('bnd,dh->bnh', x, w_neigh))
            return loop + neigh + b
        h = jax.nn.relu(_graph_conv(x, adj, w1_loop, w1_neigh, b1))
        h = jax.nn.relu(_graph_conv(h, adj, w2_loop, w2_neigh, b2))
        return (x + h) * 0.5

    def _L0_ffn_ref(x, Wg, bg, bias, W1, b1, W2, b2):
        import jax, jax.numpy as jnp
        import numpy as np
        D_MODEL = 128
        EXPERT_DIM = 256
        NUM_EXPERTS = 8
        TOP_K = 2
        SEQ_LEN = 1024
        BATCH = 2
        x_flat = x.reshape(-1, D_MODEL)
        gate_logits = x_flat @ Wg + bg + bias
        topk_vals, topk_idx = jax.lax.top_k(gate_logits, TOP_K)
        topk_w = jax.nn.softmax(topk_vals, axis=-1)
        combine = (jax.nn.one_hot(topk_idx, NUM_EXPERTS, dtype=x.dtype) * topk_w[..., None]).sum(axis=1)
        h = jax.nn.relu(jnp.einsum('td,edh->teh', x_flat, W1) + b1)
        y = jnp.einsum('teh,ehd->ted', h, W2) + b2
        out = jnp.einsum('ted,te->td', y, combine)
        return out.reshape(x.shape)

    def _L1_gnn_ref(inputs, graph, W, b_lin, b):
        import jax, jax.numpy as jnp
        import numpy as np
        B, N, C, D = (8, 1024, 128, 128)
        NEG = -1e+16
        h = jnp.einsum('bnc,cd->bnd', inputs, W) + b_lin
        scores = jnp.einsum('bnd,bmd->bnm', h, h) * graph[None, :, :]
        scores = jnp.where(scores == 0.0, NEG, scores)
        attention = jax.nn.softmax(scores, axis=2)
        return jnp.einsum('bnm,bmd->bnd', attention, h) + b

    def _L1_ffn_ref(input_embeddings, router_w, w1, b1, w2, b2):
        import jax, jax.numpy as jnp
        import numpy as np
        NUM_EXPERTS = 8
        TOP_K = 2
        B, S, D = (8, 4096, 128)

        def _moe(tokens, router_w, w1, b1, w2, b2):
            N = tokens.shape[0]
            E = router_w.shape[0]
            logits = tokens.astype(jnp.float32) @ router_w.astype(jnp.float32).T
            probs = jax.nn.softmax(logits, axis=-1)
            rw, re = jax.lax.top_k(probs, TOP_K)
            if TOP_K > 1:
                rw = rw / jnp.maximum(rw.sum(-1, keepdims=True), 1e-12)
            rw = rw.astype(tokens.dtype)
            combine = jnp.zeros((N, E), tokens.dtype).at[jnp.arange(N)[:, None], re].set(rw)
            out = tokens
            for e in range(E):
                h = jax.nn.gelu(tokens @ w1[e] + b1[e], approximate=False)
                y = h @ w2[e] + b2[e]
                out = out + combine[:, e:e + 1] * y
            return out
        b, s, d = input_embeddings.shape
        tokens = input_embeddings.reshape(b * s, d)
        return _moe(tokens, router_w, w1, b1, w2, b2).reshape(b, s, d)

    def _L2_gnn_ref(x, adj_mx, alpha_train, w, d, fc_in_w, fc_in_b, vt):
        import jax, jax.numpy as jnp
        import numpy as np
        N_STEPS = 8
        SPATIAL_SCALE = 1.0
        x0 = jax.lax.stop_gradient(x)
        h = jnp.einsum('bnd,ed->bne', x, fc_in_w) + fc_in_b
        alph = jax.nn.sigmoid(alpha_train)[:, None]
        d_clamped = jnp.clip(d, 0.0, 1.0)
        w_eff = w * d_clamped @ w.T
        dt = jnp.float32(SPATIAL_SCALE / N_STEPS)

        def euler_step(h, _):
            ax = jnp.einsum('nm,bmd->bnd', adj_mx, h)
            f = alph * 0.5 * (ax - h) + h @ w_eff - h + x0
            return (h + dt * f, None)
        h, _ = jax.lax.scan(euler_step, h, None, length=N_STEPS)
        return h

    def _L2_ffn_ref(x, W_ih, W_hh, b_ih, b_hh, W_lin, b_lin, fw_att, bw_att):
        import jax, jax.numpy as jnp
        import numpy as np
        B, T, D, H, L = (16, 2048, 128, 128, 2)

        def _lstm(x, W_ih, W_hh, b_ih, b_hh):
            x_proj = jnp.einsum('btd,gd->btg', x, W_ih) + b_ih + b_hh
            h0 = jnp.zeros((x.shape[0], W_hh.shape[1]), x.dtype)
            c0 = jnp.zeros_like(h0)

            def step(carry, xp):
                h, c = carry
                gates = xp + h @ W_hh.T
                i, f, g, o = jnp.split(gates, 4, axis=-1)
                c = jax.nn.sigmoid(f) * c + jax.nn.sigmoid(i) * jnp.tanh(g)
                h = jax.nn.sigmoid(o) * jnp.tanh(c)
                return ((h, c), h)
            _, hs = jax.lax.scan(step, (h0, c0), jnp.swapaxes(x_proj, 0, 1))
            return jnp.swapaxes(hs, 0, 1)
        lstm_out = _lstm(x, W_ih, W_hh, b_ih, b_hh)
        logits = jnp.einsum('bth,lh->btl', lstm_out, W_lin) + b_lin
        g = jax.lax.stop_gradient(jnp.argmax(logits, axis=-1).astype(lstm_out.dtype))[..., None]
        w = g * lstm_out
        inc = jnp.cumsum(w, axis=1)
        prefix = inc - w
        suffix = inc[:, -1:, :] - inc
        return 2.0 * lstm_out + prefix * fw_att + suffix * bw_att

    def _L3_gnn_ref(x, adj, Wg0, bg0, Wg1, bg1, Wih, Whh, bih, bhh):
        import jax, jax.numpy as jnp
        import numpy as np
        B, T, D, H = (64, 1024, 128, 128)
        MAX_SKIP = 4

        def _lstm_last(Wih, Whh, bih, bhh, xs):
            N, _, Hd = xs.shape
            bias = bih + bhh

            def step(carry, x_t):
                h, c = carry
                g = x_t @ Wih.T + h @ Whh.T + bias
                i, f, gg, o = jnp.split(g, 4, axis=-1)
                c = jax.nn.sigmoid(f) * c + jax.nn.sigmoid(i) * jnp.tanh(gg)
                h = jax.nn.sigmoid(o) * jnp.tanh(c)
                return ((h, c), None)
            init = (jnp.zeros((N, Hd), xs.dtype), jnp.zeros((N, Hd), xs.dtype))
            (h_last, _), _ = jax.lax.scan(step, init, jnp.swapaxes(xs, 0, 1))
            return h_last
        h = jax.nn.relu(jnp.einsum('ts,bsh->bth', adj, x @ Wg0 + bg0))
        h = jax.nn.relu(jnp.einsum('ts,bsh->bth', adj, h @ Wg1 + bg1))
        Bv, Tv, Hd = h.shape
        for p in range(1, MAX_SKIP + 1):
            nw = Tv // p
            wins = h[:, :nw * p, :].reshape(Bv * nw, p, Hd)
            last = _lstm_last(Wih[p - 1], Whh[p - 1], bih[p - 1], bhh[p - 1], wins)
            idx = jnp.arange(nw) * p + (p - 1)
            h = h.at[:, idx, :].set(last.reshape(Bv, nw, Hd))
        return h

    def _L3_ffn_ref(x, ln1_w, ln2_w, wq, wk, wv, wo, router_w, w1, w2, w3):
        import jax, jax.numpy as jnp
        import numpy as np
        B, T, C = (64, 192, 128)
        NH, NKV = (4, 2)
        HD = C // NH
        NREP = NH // NKV
        NE, TOPK = (8, 2)
        HID = int(8 / 3 * C)
        EPS_RMS = 1e-06

        def _rope_tables(t_len):
            inv_freq = 1.0 / 10000.0 ** (np.arange(0, HD, 2, dtype=np.float32) / HD)
            t = np.arange(t_len, dtype=np.float32)
            freqs = np.outer(t, inv_freq)
            emb = np.concatenate([freqs, freqs], axis=-1)
            return (jnp.asarray(np.cos(emb)), jnp.asarray(np.sin(emb)))

        def _rotate_half(x):
            h = x.shape[-1] // 2
            return jnp.concatenate([-x[..., h:], x[..., :h]], axis=-1)

        def _rmsnorm(v, w):
            return v * jax.lax.rsqrt(jnp.mean(v * v, axis=-1, keepdims=True) + EPS_RMS) * w
        Bx, Tx, Cx = x.shape
        h = _rmsnorm(x, ln1_w)
        q = (h @ wq.T).reshape(Bx, Tx, NH, HD).transpose(0, 2, 1, 3)
        k = (h @ wk.T).reshape(Bx, Tx, NKV, HD).transpose(0, 2, 1, 3)
        v = (h @ wv.T).reshape(Bx, Tx, NKV, HD).transpose(0, 2, 1, 3)
        cos, sin = _rope_tables(Tx)
        cos, sin = (cos[None, None], sin[None, None])
        q = q * cos + _rotate_half(q) * sin
        k = k * cos + _rotate_half(k) * sin
        k = jnp.repeat(k, NREP, axis=1)
        v = jnp.repeat(v, NREP, axis=1)
        scores = jnp.einsum('bhtd,bhsd->bhts', q, k) / jnp.sqrt(jnp.float32(HD))
        causal = jnp.tril(jnp.ones((Tx, Tx), dtype=bool))
        scores = jnp.where(causal[None, None], scores, jnp.float32(-1e+30))
        att = jax.nn.softmax(scores, axis=-1)
        y = jnp.einsum('bhts,bhsd->bhtd', att, v).transpose(0, 2, 1, 3).reshape(Bx, Tx, Cx)
        x = x + y @ wo.T
        flat = _rmsnorm(x, ln2_w).reshape(-1, Cx)
        probs = jax.nn.softmax(flat @ router_w.T, axis=-1)
        tp, ti = jax.lax.top_k(probs, TOPK)
        tp = tp / (jnp.sum(tp, axis=-1, keepdims=True) + 1e-09)
        weights = jnp.sum(tp[..., None] * jax.nn.one_hot(ti, NE, dtype=flat.dtype), axis=1)
        out = jnp.zeros_like(flat)
        for e in range(NE):
            hh = jax.nn.silu(flat @ w1[e].T) * (flat @ w3[e].T)
            out = out + weights[:, e:e + 1] * (hh @ w2[e].T)
        return x + out.reshape(Bx, Tx, Cx)
    x = x + _L0_gnn_ref(_layernorm(x, axis=-1), adj, L0_gnn_w1_loop, L0_gnn_w1_neigh, L0_gnn_b1, L0_gnn_w2_loop, L0_gnn_w2_neigh, L0_gnn_b2)
    x = x + _L0_ffn_ref(_layernorm(x, axis=-1), L0_ffn_Wg, L0_ffn_bg, L0_ffn_bias, L0_ffn_W1, L0_ffn_b1, L0_ffn_W2, L0_ffn_b2)
    x = x + _L1_gnn_ref(_layernorm(x, axis=-1), adj, L1_gnn_W, L1_gnn_b_lin, L1_gnn_b)
    x = x + _L1_ffn_ref(_layernorm(x, axis=-1), L1_ffn_router_w, L1_ffn_w1, L1_ffn_b1, L1_ffn_w2, L1_ffn_b2)
    x = x + _L2_gnn_ref(_layernorm(x, axis=-1), adj, L2_gnn_alpha_train, L2_gnn_w, L2_gnn_d, L2_gnn_fc_in_w, L2_gnn_fc_in_b, 0)
    x = x + _L2_ffn_ref(_layernorm(x, axis=-1), L2_ffn_W_ih, L2_ffn_W_hh, L2_ffn_b_ih, L2_ffn_b_hh, L2_ffn_W_lin, L2_ffn_b_lin, L2_ffn_fw_att, L2_ffn_bw_att)
    x = x + _L3_gnn_ref(_layernorm(x, axis=-1), adj, L3_gnn_Wg0, L3_gnn_bg0, L3_gnn_Wg1, L3_gnn_bg1, L3_gnn_Wih, L3_gnn_Whh, L3_gnn_bih, L3_gnn_bhh)
    x = x + _L3_ffn_ref(_layernorm(x, axis=-1), L3_ffn_ln1_w, L3_ffn_ln2_w, L3_ffn_wq, L3_ffn_wk, L3_ffn_wv, L3_ffn_wo, L3_ffn_router_w, L3_ffn_w1, L3_ffn_w2, L3_ffn_w3)
    return x

_drawn_inputs = setup_inputs


def setup_inputs(seed=0):
    import zlib

    import numpy as np

    out = dict(_drawn_inputs(seed))
    spreads = {'L0_gnn_b1': (0.0, 0.276),
     'L0_gnn_b2': (0.0, 0.275),
     'L0_ffn_bias': (0.0, 0.293),
     'L1_ffn_b1': (0.0, 0.483),
     'L1_ffn_b2': (0.0, 0.323),
     'L2_gnn_alpha_train': (1.0, 0.6),
     'L2_gnn_fc_in_b': (0.0, 0.464),
     'L2_ffn_fw_att': (0.0010000000474974513, 0.6),
     'L2_ffn_bw_att': (0.0010000000474974513, 0.6),
     'L3_gnn_bg0': (0.0, 0.8),
     'L3_gnn_bg1': (0.0, 0.8),
     'L3_ffn_ln1_w': (1.0, 0.6),
     'L3_ffn_ln2_w': (1.0, 0.6)}
    factors = {'L0_ffn_bg': 6.838,
     'L0_ffn_b1': 8.0,
     'L0_ffn_b2': 3.689,
     'L1_gnn_b_lin': 3.144,
     'L2_ffn_W_hh': 2.926,
     'L2_ffn_b_ih': 4.382,
     'L2_ffn_b_hh': 4.255,
     'L2_ffn_W_lin': 8.0,
     'L2_ffn_b_lin': 8.0,
     'L3_gnn_Wg0': 8.0,
     'L3_gnn_Wg1': 8.0,
     'L3_gnn_Wih': 8.0,
     'L3_gnn_Whh': 8.0,
     'L3_gnn_bih': 8.0,
     'L3_gnn_bhh': 8.0,
     'L3_ffn_wq': 8.0,
     'L3_ffn_wk': 8.0,
     'L3_ffn_wv': 8.0,
     'L3_ffn_wo': 8.0,
     'L3_ffn_router_w': 8.0,
     'L3_ffn_w1': 8.0,
     'L3_ffn_w2': 8.0,
     'L3_ffn_w3': 8.0}
    for name, (base, spread) in spreads.items():
        noise = np.random.default_rng([zlib.crc32(name.encode()), seed]).standard_normal(out[name].shape)
        drawn = base * np.exp(spread * noise) if base else spread * noise
        out[name] = jnp.asarray(drawn.astype(out[name].dtype))
    for name, factor in factors.items():
        out[name] = (out[name] * factor).astype(out[name].dtype)
    return out
```

```python
from contextlib import ExitStack

import concourse.bass as bass
from concourse import mybir

F32 = mybir.dt.float32
U32 = mybir.dt.uint32
ALU = mybir.AluOpType
ACT = mybir.ActivationFunctionType
AX = mybir.AxisListType.X

P = 128
B, N, D = 16, 512, 128
T = N // P
E = 8
HEADS, HD = 4, 32
FILLERS = 5
EPS_LN = 1e-05
EPS_RMS = 1e-06


class Stage(ExitStack):

    def __init__(self, nc):
        super().__init__()
        self.nc, self.sems, self.counts = nc, [], []

    def sem(self, name):
        self.sems.append(self.nc.alloc_semaphore(name))
        return self.sems[-1]

    def __exit__(self, *what):
        if self.sems and what[0] is None:
            self.nc.clear_and_free_semaphores(self.sems)
            self.nc.all_engine_barrier()
        return super().__exit__(*what)


class Count:

    def __init__(self, ctx, nc, name, per=1, credit=0):
        self.sem = ctx.sem(name)
        ctx.counts.append(self)
        self.per = per
        self.credit = credit
        self.name = name

    def done(self, b, k=None):
        return b * self.per + (self.per if k is None else k) + self.credit

    def freed(self, b, k=None):
        return b * self.per + (self.per if k is None else k)


class Chain:

    def __init__(self, ctx, nc, name, per):
        self.count = Count(ctx, nc, name, per)
        self.k = 0

    def begin(self, b):
        self.b, self.k = b, 0

    def link(self, eng, ins):
        self.k += 1
        ins.then_inc(self.count.sem, 1)
        eng.wait_ge(self.count.sem, self.count.done(self.b, self.k))

    def end(self):
        assert self.k == self.count.per, (self.count.name, self.k)


def hold(eng, res):
    eng.sem_inc(res["holds"], 1)


class Front:

    def __init__(self, ctx, nc, res, src, pt_bank, kind="layernorm", weight=None, tag=""):
        self.res = res
        self.src, self.pt, self.kind, self.weight = src, pt_bank, kind, weight
        self.ident, self.eps, self.nhalf = res["ident"], res["eps_" + kind], res["nhalf"]
        self.z, self.zF, self.st, self.mv, self.ve, self.rstd = (
            res["front_" + n] for n in ("z", "zF", "st", "mv", "ve", "rstd"))
        c = lambda n, **k: Count(ctx, nc, tag + n, **k)
        self.stats = c("ln_stats")
        self.moments = c("ln_moments")
        self.eps_added = c("ln_eps_added")
        self.rstd_ready = c("ln_rstd_ready")
        self.z_ready = c("z_ready")
        self.z_turned = c("z_turned")
        self.zF_ready = c("zF_ready", credit=1)

    def vector_stats(self, v, b, q):
        if self.kind == "layernorm":
            for t in range(T):
                ins = v.bn_stats(self.st[q][:, t, :], self.src[:, b, t, :])
            ins.then_inc(self.stats.sem, 1)
            v.wait_ge(self.stats.sem, self.stats.done(b))
            hold(v, self.res)
            for t in range(T):
                ins = v.bn_aggr(self.mv[q][:, t, :], self.st[q][:, t, :])
            ins.then_inc(self.moments.sem, 1)
        else:
            for t in range(T):
                ins = v.scalar_tensor_tensor(out=self.z[q][:, t, :], in0=self.src[:, b, t, :], scalar=1.0,
                                             in1=self.src[:, b, t, :], op0=ALU.mult, op1=ALU.mult,
                                             accum_out=self.mv[q][:, t, 1:2])
            ins.then_inc(self.moments.sem, 1)

    def gpsimd(self, g, b, q):
        g.wait_ge(self.moments.sem, self.moments.done(b))
        g.tensor_tensor(self.ve[q][:, :], self.mv[q][:, :, 1], self.eps[:, :], ALU.add)\
            .then_inc(self.eps_added.sem, 1)
        g.wait_ge(self.eps_added.sem, self.eps_added.done(b))
        g.tensor_tensor(self.rstd[q][:, :], self.ve[q][:, :], self.nhalf[:, :], ALU.pow)\
            .then_inc(self.rstd_ready.sem, 1)

    def vector_apply(self, v, b, q):
        v.wait_ge(self.rstd_ready.sem, self.rstd_ready.done(b))
        for t in range(T):
            if self.kind == "layernorm":
                ins = v.tensor_scalar(self.z[q][:, t, :], self.src[:, b, t, :], self.mv[q][:, t, 0:1],
                                      self.rstd[q][:, t:t + 1], ALU.subtract, ALU.mult)
            else:
                ins = v.tensor_scalar(self.z[q][:, t, :], self.src[:, b, t, :],
                                      self.rstd[q][:, t:t + 1], float(D) ** 0.5, ALU.mult, ALU.mult)
        ins.then_inc(self.z_ready.sem, 1)

    def tensor(self, pe, b, q, frees_z=False):
        pe.wait_ge(self.z_ready.sem, self.z_ready.done(b))
        pe.wait_ge(self.zF_ready.sem, self.zF_ready.freed(b))
        for t in range(T):
            ins = pe.transpose(self.pt[:, t * P:(t + 1) * P], self.z[q][:, t, :], self.ident[:, :])
        ins.then_inc(self.z_turned.sem, 1)

    def scalar(self, a, b, q):
        a.wait_ge(self.z_turned.sem, self.z_turned.done(b))
        if self.weight is None:
            a.activation(self.zF[q][:, :], self.pt[:, :], ACT.Copy).then_inc(self.zF_ready.sem, 1)
        else:
            a.activation(self.zF[q][:, :], self.pt[:, :], ACT.Copy, scale=self.weight)\
                .then_inc(self.zF_ready.sem, 1)


def run_front_and_main(eng, front, main):
    front(0, 0)
    with eng.Fori(0, B // 2 - 1) as j:
        main(j * 2, 0, (j * 2 + 1, 1))
        main(j * 2 + 1, 1, (j * 2 + 2, 0))
    main(B - 2, 0, (B - 1, 1))
    main(B - 1, 1, None)


def credit(eng, stage):
    for c in stage.counts:
        if c.credit:
            eng.sem_inc(c.sem, c.credit)



def load_all(late, early, nc, ap):
    res = {"holds": late.enter_context(nc.semaphore("holds"))}

    def sb(name, shape, ctx=late):
        res[name] = ctx.enter_context(nc.sbuf_tensor("r_" + name, shape, F32))
        return res[name]

    res["psum"] = late.enter_context(nc.psum_tensor("psum", [P, 8, N], F32))
    res["bank"] = [res["psum"][:, i, :] for i in range(8)]
    for n, shape in (("z", [P, T, D]), ("zF", [P, N]), ("st", [P, T, 6]), ("mv", [P, T, 2]),
                     ("ve", [P, T]), ("rstd", [P, T])):
        res["front_" + n] = [late.enter_context(nc.sbuf_tensor(f"front_{n}{q}", shape, F32))
                             for q in range(2)]
    X = sb("X", [P, B, T, D])
    ident = sb("ident", [P, P])
    nhalf = sb("nhalf", [P, T])
    eps_ln, eps_rms = sb("eps_layernorm", [P, T]), sb("eps_rms", [P, T])
    iota = sb("iota", [P, T, E])
    adj_t = sb("adj_t", [P, T, N])
    tri = sb("tri", [P, N])
    plan = []

    def weight(name, shape, src, ctx=late):
        dst = sb(name, shape, ctx)
        plan.append((dst[(slice(None),) * len(shape)], src))

    row = lambda a, n: a.rearrange("(a d) -> a d", a=1).broadcast_to([P, n])
    fold = lambda a: a.rearrange("(t p) m -> p t m", p=P)
    col = lambda a: a.rearrange("(a p) -> p a", p=P)
    plan.append((adj_t[:, :, :], fold(ap["adj_t"])))
    for n in ("L3_gnn_Wg0", "L3_gnn_Wg1", "woT"):
        weight(n, [P, D], ap[n])
    for n in ("ln1_w", "ln2_w"):
        weight(n, [P, 1], col(ap[n]))
    for n in ("L3_gnn_bg0", "L3_gnn_bg1"):
        weight("row_" + n, [P, D], row(ap[n], D))
    weight("WihT", [P, 4, 4 * D], ap["WihT"])
    weight("WhhT", [P, 4, 4 * D], ap["WhhT"])
    weight("bih", [P, 4, 4], ap["bihc"])
    weight("bhh", [P, 4, 4], ap["bhhc"])
    for n in ("wqT", "wqrT", "wkT", "wkrT"):
        weight(n, [P, D], ap[n])
    weight("wvT", [P, 64], ap["wvT"])
    weight("cos", [P, N], ap["cos_table"])
    weight("sin", [P, N], ap["sin_table"])
    weight("L3_Wg", [P, E], ap["L3_router_wT"])
    HID = ap["L3_w1T"].shape[2]
    weight("L3_W1", [P, E, HID], ap["L3_w1T"])
    weight("L3_W3", [P, E, HID], ap["L3_w3T"])
    w2 = sb("L3_W2", [P, E, 3, D])
    for e in range(E):
        plan.append((w2[:, e, 0:2, :], ap["L3_w2T"][e, 0:256, :].rearrange("(c p) d -> p c d", p=P)))
        plan.append((w2[0:HID - 256, e, 2, :], ap["L3_w2T"][e, 256:HID, :]))
    adj_n = sb("adj_n", [P, T, N], early)
    plan.append((adj_n[:, :, :], fold(ap["adj"])))
    for n in ("L0_gnn_w1_loop", "L0_gnn_w1_neigh", "L0_gnn_w2_loop", "L0_gnn_w2_neigh", "L1_gnn_W",
              "L2_gnn_wT", "fc_in_wT"):
        weight(n, [P, D], ap[n], early)
    for n in ("L0_gnn_b1", "L1_gnn_b_lin", "L2_gnn_d", "L2_gnn_fc_in_b", "fw_att", "bw_att"):
        weight(n, [P, 1], col(ap[n]), early)
    for n in ("L0_gnn_b2", "L1_gnn_b_lin", "L1_gnn_b"):
        weight("row_" + n, [P, D], row(ap[n], D), early)
    weight("alpha", [P, T], ap["alpha"], early)
    weight("L0_Wg", [P, E], ap["L0_ffn_Wg"], early)
    for n in ("bg", "bias"):
        weight("L0_" + n, [P, E], row(ap["L0_ffn_" + n], E), early)
    weight("L0_W1", [P, E, 256], ap["L0_ffn_W1"].rearrange("e d h -> d e h"), early)
    weight("L0_b1", [P, E, 2], ap["L0_b1c"], early)
    weight("L0_W2", [P, E, 2, D], ap["L0_ffn_W2"].rearrange("e (c p) d -> p e c d", p=P), early)
    weight("L0_b2", [E, D], ap["L0_ffn_b2"], early)
    weight("L1_Wg", [P, E], ap["L1_router_wT"], early)
    weight("L1_W1", [P, E, D], ap["L1_ffn_w1"].rearrange("e d h -> d e h"), early)
    weight("L1_b1", [P, E, 1], ap["L1_b1c"], early)
    weight("L1_W2", [P, E, 1, D], ap["L1_ffn_w2"].rearrange("e (c p) d -> p e c d", p=P), early)
    weight("L1_b2", [E, D], ap["L1_ffn_b2"], early)
    weight("W_ihT", [P, 4 * D], ap["W_ihT"], early)
    weight("W_hhT", [P, 4 * D], ap["W_hhT"], early)
    weight("b_ih", [1, 4 * D], ap["L2_ffn_b_ih"].rearrange("(a d) -> a d", a=1), early)
    weight("b_hh", [1, 4 * D], ap["L2_ffn_b_hh"].rearrange("(a d) -> a d", a=1), early)
    weight("W_linT", [P, 2], ap["W_linT"], early)
    weight("b_lin", [P, 2], row(ap["L2_ffn_b_lin"], 2), early)

    x_in = ap["x"].rearrange("b (t p) d -> p b t d", p=P)
    with Stage(nc) as ctx, nc.Block() as block:
        x_loaded, w_loaded, const_set = ctx.sem("x_loaded"), ctx.sem("w_loaded"), ctx.sem("const_set")

        @block.sync
        def _(sp):
            for b in range(B):
                sp.dma_start(X[:, b, :, :], x_in[:, b, :, :]).then_inc(x_loaded, 16)
            for dst, src in plan[1::2]:
                sp.dma_start(dst, src).then_inc(w_loaded, 16)
            sp.wait_ge(x_loaded, 16 * B)
            sp.wait_ge(w_loaded, 16 * len(plan))

        @block.scalar
        def _(a):
            for dst, src in plan[0::2]:
                a.dma_start(dst, src).then_inc(w_loaded, 16)

        @block.gpsimd
        def _(g):
            g.memset(ident[:, :], 0.0).then_inc(const_set, 1)
            g.memset(tri[:, :], 0.0).then_inc(const_set, 1)
            g.memset(nhalf[:, :], -0.5)
            g.memset(eps_ln[:, :], EPS_LN)
            g.memset(eps_rms[:, :], EPS_RMS * D)
            g.iota(iota[:, :, :], [[0, T], [1, E]], base=0, channel_multiplier=0,
                   allow_small_or_imprecise_dtypes=True)
            g.wait_ge(const_set, 2)
            g.affine_select(out=ident[:, :], in_=ident[:, :], compare_op=ALU.not_equal, fill=1.0, base=0,
                            pattern=[[-1, P]], channel_multiplier=1)
            g.affine_select(out=tri[:, N - P:N], in_=tri[:, N - P:N], compare_op=ALU.is_ge, fill=-1e30,
                            base=0, pattern=[[-1, P]], channel_multiplier=1)
    return res



def graph_convolution(nc, res, adj_t, X):
    with Stage(nc) as ctx:
        bank = res["bank"]
        sb = lambda n, s: ctx.enter_context(nc.sbuf_tensor("g0_" + n, s, F32))
        c = lambda n, **k: Count(ctx, nc, "g0_" + n, **k)
        fr = Front(ctx, nc, res, X, bank[0])
        mixed, h1F, n2 = sb("mixed", [P, N]), sb("h1F", [P, N]), sb("n2", [P, T, D])
        out = [sb(f"out{i}", [P, T, D]) for i in range(2)]
        az_ready, az_copied = c("az_ready"), c("az_copied", credit=1)
        h1_ready, h1_copied = c("h1_ready", credit=1), c("h1_copied", credit=1)
        n2_ready, n2_copied = c("n2_ready"), c("n2_copied", credit=1)
        y_ready, y_read = c("y_ready", credit=1), c("y_read", credit=1)
        y_rectified, x_done = c("y_rectified"), c("x_done")
        w = lambda n: res["L0_gnn_" + n]
        AZ, H1, N2, Y = bank[1], bank[2], bank[3], [bank[4], bank[5]]

        with nc.Block() as block:
            @block.tensor
            def _(pe):
                def main(b, q, nxt):
                    pe.wait_ge(fr.z_ready.sem, fr.z_ready.done(b))
                    pe.wait_ge(az_copied.sem, az_copied.freed(b))
                    for m in range(T):
                        ins = pe.matmul(AZ[:, :], fr.z[q][:, m, :], adj_t[:, m, :],
                                        start=(m == 0), stop=(m == T - 1))
                    ins.then_inc(az_ready.sem, 1)
                    if nxt:
                        fr.tensor(pe, *nxt)
                    pe.wait_ge(fr.zF_ready.sem, fr.zF_ready.done(b))
                    pe.wait_ge(h1_copied.sem, h1_copied.freed(b))
                    pe.matmul(H1[:, :], w("w1_loop")[:, :], fr.zF[q][:, :], start=True, stop=False)
                    pe.wait_ge(az_copied.sem, az_copied.done(b))
                    pe.matmul(H1[:, :], w("w1_neigh")[:, :], mixed[:, :], start=False, stop=True)\
                        .then_inc(h1_ready.sem, 1)
                    pe.wait_ge(h1_copied.sem, h1_copied.done(b))
                    pe.wait_ge(n2_copied.sem, n2_copied.freed(b))
                    for t in range(T):
                        ins = pe.matmul(N2[:, t * P:(t + 1) * P], h1F[:, t * P:(t + 1) * P],
                                        w("w2_neigh")[:, :], start=True, stop=True)
                    ins.then_inc(n2_ready.sem, 1)
                    pe.wait_ge(n2_copied.sem, n2_copied.done(b))
                    pe.wait_ge(y_read.sem, y_read.freed(b))
                    for t in range(T):
                        o = Y[q][:, t * P:(t + 1) * P]
                        pe.matmul(o, h1F[:, t * P:(t + 1) * P], w("w2_loop")[:, :], start=True, stop=False)
                        for m in range(T):
                            ins = pe.matmul(o, adj_t[:, m, t * P:(t + 1) * P], n2[:, m, :],
                                            start=False, stop=(m == T - 1))
                    ins.then_inc(y_ready.sem, 1)
                run_front_and_main(pe, lambda b, q: fr.tensor(pe, b, q), main)

            @block.scalar
            def _(a):
                def main(b, q, nxt):
                    a.wait_ge(az_ready.sem, az_ready.done(b))
                    a.wait_ge(h1_ready.sem, h1_ready.freed(b))
                    a.activation(mixed[:, :], AZ[:, :], ACT.Copy).then_inc(az_copied.sem, 1)
                    if nxt:
                        fr.scalar(a, *nxt)
                    a.wait_ge(h1_ready.sem, h1_ready.done(b))
                    a.wait_ge(y_ready.sem, y_ready.freed(b))
                    a.activation(h1F[:, :], H1[:, :], ACT.Relu, bias=w("b1")[:, 0:1])\
                        .then_inc(h1_copied.sem, 1)
                    a.wait_ge(n2_ready.sem, n2_ready.done(b))
                    a.activation(n2[:, :, :], N2[:, :].rearrange("p (t d) -> p t d", t=T), ACT.Copy)\
                        .then_inc(n2_copied.sem, 1)
                run_front_and_main(a, lambda b, q: fr.scalar(a, b, q), main)

            @block.vector
            def _(v):
                def front(b, q):
                    fr.vector_stats(v, b, q)
                    fr.vector_apply(v, b, q)

                def main(b, q, nxt):
                    if nxt:
                        fr.vector_stats(v, *nxt)
                        fr.vector_apply(v, *nxt)
                    v.wait_ge(y_ready.sem, y_ready.done(b))
                    bias = res["row_L0_gnn_b2"][:, :]\
                        .unsqueeze(1).broadcast_to([P, T, D])
                    v.tensor_tensor(out[q][:, :, :], Y[q][:, :].rearrange("p (t d) -> p t d", t=T), bias,
                                    ALU.add).then_inc(y_read.sem, 1)
                    v.wait_ge(y_read.sem, y_read.done(b))
                    v.scalar_tensor_tensor(out=out[q][:, :, :], in0=out[q][:, :, :], scalar=0.0,
                                           in1=fr.z[q][:, :, :], op0=ALU.max, op1=ALU.add)\
                        .then_inc(y_rectified.sem, 1)
                    v.wait_ge(y_rectified.sem, y_rectified.done(b))
                    v.scalar_tensor_tensor(out=X[:, b, :, :], in0=out[q][:, :, :], scalar=0.5,
                                           in1=X[:, b, :, :], op0=ALU.mult, op1=ALU.add)\
                        .then_inc(x_done.sem, 1)
                run_front_and_main(v, front, main)

            @block.gpsimd
            def _(g):
                credit(g, ctx)

                def main(b, q, nxt):
                    if nxt:
                        fr.gpsimd(g, *nxt)
                run_front_and_main(g, lambda b, q: fr.gpsimd(g, b, q), main)



class Router:

    def __init__(self, ctx, nc, res, tag, bank, w_gate, bias, rule, guard):
        sb = lambda n, s, dt=F32: ctx.enter_context(nc.sbuf_tensor(tag + n, s, dt))
        c = lambda n, **k: Count(ctx, nc, tag + n, **k)
        self.bank, self.w, self.bias, self.rule, self.guard = bank, w_gate, bias, rule, guard
        self.res, self.iota, self.ident = res, res["iota"], res["ident"]
        self.lg, self.sub, self.ex = sb("lg", [P, T, E]), sb("sub", [P, T, E]), sb("ex", [P, T, E])
        self.probs, self.top = sb("probs", [P, T, E]), sb("top", [P, T, E])
        self.idx, self.idxf = sb("idx", [P, T, E], U32), sb("idxf", [P, T, E])
        self.s1, self.s2, self.w2 = sb("s1", [P, T]), sb("s2", [P, T]), sb("w2", [P, T, 2])
        self.hot = sb("hot", [P, T, 2, E])
        self.c = [sb(f"c{i}", [P, T, E]) for i in range(2)]
        self.cF = [sb(f"cF{i}", [E, N]) for i in range(2)]
        self.lg_ready, self.lg_read = c("lg_ready"), c("lg_read")
        self.sub_ready, self.ex_ready, self.c_ready = c("sub_ready"), c("ex_ready"), c("c_ready")
        self.c_turned, self.cF_ready = c("c_turned"), c("cF_ready")
        self.chain = Chain(ctx, nc, tag + "route_chain",
                           (11 if rule == "probs" else 8) + (bias is not None))

    def tensor_logits(self, pe, fr, b, q):
        pe.wait_ge(fr.zF_ready.sem, fr.zF_ready.done(b))
        for t in range(T):
            ins = pe.matmul(self.bank[:, t * E:(t + 1) * E], fr.zF[q][:, t * P:(t + 1) * P],
                            self.w[:, :], start=True, stop=True)
        ins.then_inc(self.lg_ready.sem, 1)

    def tensor_turn(self, pe, b, q):
        pe.wait_ge(self.c_ready.sem, self.c_ready.done(b))
        for t in range(T):
            ins = pe.transpose(self.bank[0:E, t * P:(t + 1) * P], self.c[q][:, t, :], self.ident[:, :])
        ins.then_inc(self.c_turned.sem, 1)

    def scalar_exp(self, a, b, q):
        a.wait_ge(self.sub_ready.sem, self.sub_ready.done(b))
        k = E if self.rule == "probs" else 2
        a.activation(self.ex[:, :, 0:k], self.sub[:, :, 0:k], ACT.Exp).then_inc(self.ex_ready.sem, 1)

    def scalar_cF(self, a, b, q):
        a.wait_ge(self.c_turned.sem, self.c_turned.done(b))
        a.activation(self.cF[q][:, :], self.bank[0:E, :], ACT.Copy).then_inc(self.cF_ready.sem, 1)

    def vector_before_exp(self, v, b, q):
        ch = self.chain
        ch.begin(b)
        v.wait_ge(self.lg_ready.sem, self.lg_ready.done(b))
        lg = self.bank[:, 0:T * E].rearrange("p (t e) -> p t e", t=T)
        if self.bias is None:
            ch.link(v, v.tensor_copy(self.lg[:, :, :], lg))
        else:
            ch.link(v, v.tensor_tensor(self.lg[:, :, :], lg,
                                       self.bias[0][:, :].unsqueeze(1).broadcast_to([P, T, E]), ALU.add))
            ch.link(v, v.tensor_tensor(self.lg[:, :, :], self.lg[:, :, :],
                                       self.bias[1][:, :].unsqueeze(1).broadcast_to([P, T, E]), ALU.add))
        hold(v, self.res)
        for t in range(T):
            ins = v.max(self.top[:, t, :], self.lg[:, t, :])
        ch.link(v, ins)
        k = E if self.rule == "probs" else 2
        src = self.lg if self.rule == "probs" else self.top
        v.tensor_tensor(self.sub[:, :, 0:k], src[:, :, 0:k],
                        self.top[:, :, 0:1].broadcast_to([P, T, k]), ALU.subtract)\
            .then_inc(self.sub_ready.sem, 1)

    def vector_after_exp(self, v, b, q):
        ch = self.chain
        v.wait_ge(self.ex_ready.sem, self.ex_ready.done(b))
        k = E if self.rule == "probs" else 2
        ch.link(v, v.tensor_reduce(self.s1[:, :], self.ex[:, :, 0:k], AX, ALU.add))
        ch.link(v, v.reciprocal(self.s2[:, :], self.s1[:, :]))
        r = self.s2[:, :].unsqueeze(2)
        if self.rule == "probs":
            ch.link(v, v.tensor_tensor(self.probs[:, :, :], self.ex[:, :, :],
                                       r.broadcast_to([P, T, E]), ALU.mult))
            hold(v, self.res)
            for t in range(T):
                ins = v.max(self.top[:, t, :], self.probs[:, t, :])
            ch.link(v, ins)
            v.tensor_tensor(self.s1[:, :], self.top[:, :, 0], self.top[:, :, 1], ALU.add)
            for t in range(T):
                ins = v.max_index(self.idx[:, t, :], self.top[:, t, :], self.probs[:, t, :])
            ch.link(v, ins)
            op, number = self.guard
            v.tensor_copy(self.idxf[:, :, :], self.idx[:, :, :])
            ch.link(v, v.tensor_scalar(self.s1[:, :], self.s1[:, :], number, None, op))
            ch.link(v, v.reciprocal(self.s2[:, :], self.s1[:, :]))
            v.tensor_tensor(self.w2[:, :, :], self.top[:, :, 0:2], r.broadcast_to([P, T, 2]), ALU.mult)
        else:
            hold(v, self.res)
            for t in range(T):
                ins = v.max_index(self.idx[:, t, :], self.top[:, t, :], self.lg[:, t, :])
            ch.link(v, v.tensor_tensor(self.w2[:, :, :], self.ex[:, :, 0:2],
                                       r.broadcast_to([P, T, 2]), ALU.mult))
            ch.link(v, v.tensor_copy(self.idxf[:, :, :], self.idx[:, :, :]))
        for j in range(2):
            ins = v.tensor_tensor(self.hot[:, :, j, :], self.iota[:, :, :],
                                  self.idxf[:, :, j:j + 1].broadcast_to([P, T, E]), ALU.is_equal)
        ch.link(v, ins)
        for j in range(2):
            ins = v.tensor_tensor(self.hot[:, :, j, :], self.hot[:, :, j, :],
                                  self.w2[:, :, j:j + 1].broadcast_to([P, T, E]), ALU.mult)
        ch.link(v, ins)
        v.tensor_tensor(self.c[q][:, :, :], self.hot[:, :, 0, :], self.hot[:, :, 1, :], ALU.add)\
            .then_inc(self.c_ready.sem, 1)
        ch.end()


def mixture(nc, res, X, tag, w, hidden, act, rule, guard, router_bias, biases, adds_z,
            src=None, kind="layernorm", weight=None):
    src = X if src is None else src
    C = len(hidden)
    gated = "W3" in w
    NC = E * C
    HR = 6 if gated else 2 * C
    with Stage(nc) as ctx:
        bank = res["bank"]
        sb = lambda n, s: ctx.enter_context(nc.sbuf_tensor(tag + n, s, F32))
        c = lambda n, **k: Count(ctx, nc, tag + n, **k)
        fr = Front(ctx, nc, res, src, bank[0], kind=kind, weight=weight, tag=tag)
        ro = Router(ctx, nc, res, tag, bank[1], w["Wg"], router_bias, rule, guard)
        H, Y = bank[2:6], bank[6:8]
        HS = 2 if gated else 4
        hF = [sb(f"hF{i}", [P, N]) for i in range(HR)]
        gate = [sb(f"gate{i}", [P, N]) for i in range(2)] if gated else None
        acc = sb("acc", [P, T, D])
        h_ready = c("h_ready", per=NC)
        gate_ready = c("gate_ready", per=NC) if gated else None
        hF_ready = c("hF_ready", per=NC, credit=HS)
        y_ready = c("y_ready", per=E, credit=2)
        y_added = c("y_added", per=E, credit=2)
        bias_ready = c("bias_ready")
        acc_set, z_added = c("acc_set"), c("z_added")
        acc_last = acc_set if not adds_z else z_added

        with nc.Block() as block:
            @block.tensor
            def _(pe):
                def up(b, q, e):
                    if e == 0:
                        pe.wait_ge(fr.zF_ready.sem, fr.zF_ready.done(b))
                    for j, size in enumerate(hidden):
                        n = e * C + j
                        pe.wait_ge(hF_ready.sem, hF_ready.freed(b, n + 1))
                        cols = slice(j * P, j * P + size)
                        if gated:
                            k = n % HS * 2
                            pe.matmul(H[k][0:size, :], w["W1"][:, e, cols], fr.zF[q][:, :],
                                      start=True, stop=True)
                            ins = pe.matmul(H[k + 1][0:size, :], w["W3"][:, e, cols], fr.zF[q][:, :],
                                            start=True, stop=True)
                        else:
                            ins = pe.matmul(H[n % HS][0:size, :], w["W1"][:, e, cols], fr.zF[q][:, :],
                                            start=True, stop=True)
                        ins.then_inc(h_ready.sem, 1)

                def down(b, q, e):
                    pe.wait_ge(hF_ready.sem, hF_ready.done(b, e * C + C))
                    pe.wait_ge(y_added.sem, y_added.freed(b, e + 1))
                    for t in range(T):
                        for j, size in enumerate(hidden):
                            ins = pe.matmul(Y[e % 2][:, t * P:(t + 1) * P],
                                            hF[e % 2 * C + j][0:size, t * P:(t + 1) * P],
                                            w["W2"][0:size, e, j, :], start=(j == 0), stop=(j == C - 1))
                    ins.then_inc(y_ready.sem, 1)

                def bias(b, q):
                    pe.wait_ge(ro.cF_ready.sem, ro.cF_ready.done(b))
                    for t in range(T):
                        ins = pe.matmul(ro.bank[:, t * P:(t + 1) * P], ro.cF[q][:, t * P:(t + 1) * P],
                                        w["b2"][:, :], start=True, stop=True)
                    ins.then_inc(bias_ready.sem, 1)

                def front(b, q):
                    fr.tensor(pe, b, q)
                    ro.tensor_logits(pe, fr, b, q)
                    if biases:
                        ro.tensor_turn(pe, b, q)
                        bias(b, q)
                    up(b, q, 0)

                def main(b, q, nxt):
                    for e in range(E):
                        if e + 1 < E:
                            up(b, q, e + 1)
                        elif nxt:
                            if biases:
                                bias(*nxt)
                            up(*nxt, 0)
                        down(b, q, e)
                        if nxt and e == 3:
                            fr.tensor(pe, *nxt)
                        if nxt and e == 4:
                            pe.wait_ge(acc_set.sem, acc_set.done(b))
                            ro.tensor_logits(pe, fr, *nxt)
                        if nxt and e == 6 and biases:
                            ro.tensor_turn(pe, *nxt)
                run_front_and_main(pe, front, main)

            @block.scalar
            def _(a):
                def hidden_chunks(b, q, e):
                    for j, size in enumerate(hidden):
                        n = e * C + j
                        a.wait_ge(h_ready.sem, h_ready.done(b, n + 1))
                        if gated:
                            a.wait_ge(hF_ready.sem, hF_ready.freed(b, n + 1))
                            a.activation(gate[n % 2][0:size, :], H[n % HS * 2][0:size, :], act)\
                                .then_inc(gate_ready.sem, 1)
                        else:
                            if j == 0:
                                a.wait_ge(y_ready.sem, y_ready.freed(b, e + 1))
                            a.activation(hF[n % HR][0:size, :], H[n % HS][0:size, :], act,
                                         bias=w["b1"][0:size, e, j:j + 1]).then_inc(hF_ready.sem, 1)

                def front(b, q):
                    fr.scalar(a, b, q)
                    ro.scalar_exp(a, b, q)
                    if biases:
                        ro.scalar_cF(a, b, q)
                    hidden_chunks(b, q, 0)

                def main(b, q, nxt):
                    for e in range(E):
                        if e + 1 < E:
                            hidden_chunks(b, q, e + 1)
                        elif nxt:
                            hidden_chunks(*nxt, 0)
                        if nxt and e == 3:
                            fr.scalar(a, *nxt)
                        if nxt and e == 5:
                            ro.scalar_exp(a, *nxt)
                        if nxt and e == 6 and biases:
                            ro.scalar_cF(a, *nxt)
                run_front_and_main(a, front, main)

            @block.vector
            def _(v):
                def products(b, q, e):
                    for j, size in enumerate(hidden):
                        n = e * C + j
                        v.wait_ge(gate_ready.sem, gate_ready.done(b, n + 1))
                        if j == 0:
                            v.wait_ge(y_ready.sem, y_ready.freed(b, e + 1))
                        v.tensor_tensor(hF[n % HR][0:size, :], H[n % HS * 2 + 1][0:size, :],
                                        gate[n % 2][0:size, :], ALU.mult).then_inc(hF_ready.sem, 1)

                def front(b, q):
                    fr.vector_stats(v, b, q)
                    fr.vector_apply(v, b, q)
                    ro.vector_before_exp(v, b, q)
                    ro.vector_after_exp(v, b, q)
                    if gated:
                        products(b, q, 0)

                def main(b, q, nxt):
                    v.wait_ge(y_added.sem, y_added.done(b, 0))
                    if biases:
                        v.wait_ge(bias_ready.sem, bias_ready.done(b))
                        v.tensor_tensor(acc[:, :, :], ro.bank[:, :].rearrange("p (t d) -> p t d", t=T),
                                        X[:, b, :, :], ALU.add).then_inc(acc_set.sem, 1)
                    else:
                        v.tensor_copy(acc[:, :, :], X[:, b, :, :]).then_inc(acc_set.sem, 1)
                    if adds_z:
                        v.wait_ge(acc_set.sem, acc_set.done(b))
                        v.tensor_tensor(acc[:, :, :], acc[:, :, :], fr.z[q][:, :, :], ALU.add)\
                            .then_inc(z_added.sem, 1)
                    for e in range(E):
                        if gated:
                            if e + 1 < E:
                                products(b, q, e + 1)
                            elif nxt:
                                products(*nxt, 0)
                        v.wait_ge(y_ready.sem, y_ready.done(b, e + 1))
                        if e == 0:
                            v.wait_ge(acc_last.sem, acc_last.done(b))
                        else:
                            v.wait_ge(y_added.sem, y_added.done(b, e))
                        for t in range(T):
                            dst = acc[:, t, :] if e < E - 1 else X[:, b, t, :]
                            ins = v.scalar_tensor_tensor(out=dst, in0=Y[e % 2][:, t * P:(t + 1) * P],
                                                         scalar=ro.c[q][:, t, e:e + 1], in1=acc[:, t, :],
                                                         op0=ALU.mult, op1=ALU.add)
                        ins.then_inc(y_added.sem, 1)
                        if nxt and e == 0:
                            fr.vector_stats(v, *nxt)
                        if nxt and e == 1:
                            fr.vector_apply(v, *nxt)
                        if nxt and e == 4:
                            ro.vector_before_exp(v, *nxt)
                        if nxt and e == 5:
                            ro.vector_after_exp(v, *nxt)
                run_front_and_main(v, front, main)

            @block.gpsimd
            def _(g):
                credit(g, ctx)

                def main(b, q, nxt):
                    if nxt:
                        fr.gpsimd(g, *nxt)
                run_front_and_main(g, lambda b, q: fr.gpsimd(g, b, q), main)



def graph_attention(nc, res, X):
    NEG = -1e16
    with Stage(nc) as ctx:
        bank = res["bank"]
        sb = lambda n, s: ctx.enter_context(nc.sbuf_tensor("g1_" + n, s, F32))
        c = lambda n, **k: Count(ctx, nc, "g1_" + n, **k)
        fr = Front(ctx, nc, res, X, bank[0], tag="g1_")
        HB, S, PT, O = bank[1], bank[2:4], bank[4:6], bank[6]
        SR = 2
        hF = [sb(f"hF{i}", [P, N]) for i in range(2)]
        hT = [sb(f"hT{i}", [P, T, D]) for i in range(2)]
        prod = [sb(f"prod{i}", [P, N]) for i in range(SR)]
        fill = [sb(f"fill{i}", [P, N]) for i in range(SR)]
        prob = [sb(f"prob{i}", [P, N]) for i in range(SR)]
        probT = [sb(f"probT{i}", [P, T, P]) for i in range(SR)]
        top = [sb(f"top{i}", [P, T]) for i in range(2)]
        ntop = [sb(f"ntop{i}", [P, T]) for i in range(2)]
        total = [sb(f"total{i}", [P, T]) for i in range(2)]
        rtotal = [sb(f"rtotal{i}", [P, T]) for i in range(2)]
        out = sb("out", [P, T, D])
        bias = res["row_L1_gnn_b"]
        h_ready, hF_copied = c("h_ready"), c("hF_copied")
        hT_ready, hT_copied = c("hT_ready"), c("hT_copied", credit=1)
        s_ready = c("s_ready", per=T)
        prod_ready = c("prod_ready", per=T, credit=2)
        fill_ready = c("fill_ready", per=T)
        masked = c("masked", per=T)
        ntop_ready = c("ntop_ready", per=T)
        prob_ready = c("prob_ready", per=T, credit=SR)
        turned = c("turned", per=T, credit=SR)
        probT_ready = c("probT_ready", per=T, credit=2)
        o_ready = c("o_ready", per=T, credit=SR)
        r_ready, scaled, x_done = c("r_ready"), c("scaled", credit=1), c("x_done", credit=1)

        with nc.Block() as block:
            @block.tensor
            def _(pe):
                def project(b, q):
                    pe.wait_ge(fr.zF_ready.sem, fr.zF_ready.done(b))
                    pe.wait_ge(hT_copied.sem, hT_copied.freed(b))
                    pe.matmul(HB[:, :], res["L1_gnn_W"][:, :], fr.zF[q][:, :], start=True, stop=True)\
                        .then_inc(h_ready.sem, 1)
                    pe.wait_ge(hF_copied.sem, hF_copied.done(b))
                    for t in range(T):
                        ins = pe.matmul(HB[:, t * P:(t + 1) * P], fr.zF[q][:, t * P:(t + 1) * P],
                                        res["L1_gnn_W"][:, :], start=True, stop=True)
                    ins.then_inc(hT_ready.sem, 1)

                def scores(b, q, t):
                    pe.wait_ge(hF_copied.sem, hF_copied.done(b))
                    pe.wait_ge(prod_ready.sem, prod_ready.freed(b, t + 1))
                    pe.matmul(S[t % 2][:, :], hF[q][:, t * P:(t + 1) * P], hF[q][:, :],
                              start=True, stop=True).then_inc(s_ready.sem, 1)

                def turn(b, q, t):
                    pe.wait_ge(prob_ready.sem, prob_ready.done(b, t + 1))
                    pe.wait_ge(probT_ready.sem, probT_ready.freed(b, t + 1))
                    for m in range(T):
                        ins = pe.transpose(PT[t % 2][:, m * P:(m + 1) * P],
                                           prob[t % SR][:, m * P:(m + 1) * P], res["ident"][:, :])
                    ins.then_inc(turned.sem, 1)

                def attend(b, q, t):
                    if t == 0:
                        pe.wait_ge(hT_copied.sem, hT_copied.done(b))
                        pe.wait_ge(scaled.sem, scaled.freed(b))
                    pe.wait_ge(probT_ready.sem, probT_ready.done(b, t + 1))
                    for m in range(T):
                        ins = pe.matmul(O[:, t * P:(t + 1) * P], probT[t % SR][:, m, :], hT[q][:, m, :],
                                        start=(m == 0), stop=(m == T - 1))
                    ins.then_inc(o_ready.sem, 1)

                def front(b, q):
                    fr.tensor(pe, b, q)
                    project(b, q)
                    scores(b, q, 0)
                    scores(b, q, 1)

                def main(b, q, nxt):
                    scores(b, q, 2)
                    scores(b, q, 3)
                    turn(b, q, 0)
                    turn(b, q, 1)
                    attend(b, q, 0)
                    if nxt:
                        fr.tensor(pe, *nxt)
                    attend(b, q, 1)
                    if nxt:
                        project(*nxt)
                    turn(b, q, 2)
                    turn(b, q, 3)
                    if nxt:
                        scores(*nxt, 0)
                        scores(*nxt, 1)
                    attend(b, q, 2)
                    attend(b, q, 3)
                run_front_and_main(pe, front, main)

            @block.scalar
            def _(a):
                def project(b, q):
                    a.wait_ge(h_ready.sem, h_ready.done(b))
                    a.activation(hF[q][:, :], HB[:, :], ACT.Identity, bias=res["L1_gnn_b_lin"][:, 0:1])\
                        .then_inc(hF_copied.sem, 1)

                def exp(b, q, t):
                    a.wait_ge(ntop_ready.sem, ntop_ready.done(b, t + 1))
                    a.wait_ge(turned.sem, turned.freed(b, t + 1))
                    a.activation(prob[t % SR][:, :], prod[t % SR][:, :], ACT.Exp,
                                 bias=ntop[q][:, t:t + 1], accum_out=total[q][:, t:t + 1])\
                        .then_inc(prob_ready.sem, 1)

                def copy(b, q, t):
                    a.wait_ge(turned.sem, turned.done(b, t + 1))
                    a.wait_ge(o_ready.sem, o_ready.freed(b, t + 1))
                    a.activation(probT[t % SR][:, :, :], PT[t % 2][:, :].rearrange("p (m n) -> p m n", m=T),
                                 ACT.Copy).then_inc(probT_ready.sem, 1)

                def front(b, q):
                    fr.scalar(a, b, q)
                    project(b, q)

                def main(b, q, nxt):
                    exp(b, q, 0)
                    exp(b, q, 1)
                    copy(b, q, 0)
                    copy(b, q, 1)
                    if nxt:
                        fr.scalar(a, *nxt)
                        project(*nxt)
                    exp(b, q, 2)
                    exp(b, q, 3)
                    copy(b, q, 2)
                    copy(b, q, 3)
                run_front_and_main(a, front, main)

            @block.vector
            def _(v):
                def mask(b, q, t):
                    v.wait_ge(s_ready.sem, s_ready.done(b, t + 1))
                    v.wait_ge(prob_ready.sem, prob_ready.freed(b, t + 1))
                    v.tensor_tensor(prod[t % SR][:, :], S[t % 2][:, :], res["adj_n"][:, t, :], ALU.mult)\
                        .then_inc(prod_ready.sem, 1)

                def peaks(b, q, two):
                    for t in two:
                        v.wait_ge(prod_ready.sem, prod_ready.done(b, t + 1))
                        v.tensor_scalar(fill[t % SR][:, :], prod[t % SR][:, :], 0.0, NEG,
                                        ALU.is_equal, ALU.mult).then_inc(fill_ready.sem, 1)
                    for t in two:
                        v.wait_ge(fill_ready.sem, fill_ready.done(b, t + 1))
                        hold(v, res)
                        v.tensor_tensor_reduce(prod[t % SR][:, :], prod[t % SR][:, :],
                                               fill[t % SR][:, :], 1.0, -3e38, ALU.add, ALU.max,
                                               top[q][:, t:t + 1]).then_inc(masked.sem, 1)
                    for t in two:
                        v.wait_ge(masked.sem, masked.done(b, t + 1))
                        v.tensor_scalar(ntop[q][:, t:t + 1], top[q][:, t:t + 1], -1.0, None, ALU.mult)\
                            .then_inc(ntop_ready.sem, 1)

                def front(b, q):
                    fr.vector_stats(v, b, q)
                    fr.vector_apply(v, b, q)
                    bias_h(b, q)
                    mask(b, q, 0)
                    mask(b, q, 1)
                    peaks(b, q, (0, 1))
                    fr.vector_stats(v, 1, 1)

                def bias_h(b, q):
                    v.wait_ge(hT_ready.sem, hT_ready.done(b))
                    v.tensor_tensor(hT[q][:, :, :], HB[:, :].rearrange("p (t d) -> p t d", t=T),
                                    res["row_L1_gnn_b_lin"][:, :].unsqueeze(1).broadcast_to([P, T, D]),
                                    ALU.add).then_inc(hT_copied.sem, 1)

                def main(b, q, nxt):
                    if nxt:
                        fr.vector_apply(v, *nxt)
                    mask(b, q, 2)
                    mask(b, q, 3)
                    peaks(b, q, (2, 3))
                    if nxt:
                        bias_h(*nxt)
                        mask(*nxt, 0)
                        mask(*nxt, 1)
                        peaks(*nxt, (0, 1))
                    if not isinstance(b, int):
                        fr.vector_stats(v, b + 2, q)
                    v.wait_ge(o_ready.sem, o_ready.done(b, T))
                    v.reciprocal(rtotal[q][:, :], total[q][:, :]).then_inc(r_ready.sem, 1)
                    v.wait_ge(r_ready.sem, r_ready.done(b))
                    v.wait_ge(x_done.sem, x_done.freed(b))
                    for t in range(T):
                        ins = v.scalar_tensor_tensor(out=out[:, t, :], in0=O[:, t * P:(t + 1) * P],
                                                     scalar=rtotal[q][:, t:t + 1], in1=bias[:, :],
                                                     op0=ALU.mult, op1=ALU.add)
                    ins.then_inc(scaled.sem, 1)
                    v.wait_ge(scaled.sem, scaled.done(b))
                    v.tensor_tensor(X[:, b, :, :], X[:, b, :, :], out[:, :, :], ALU.add)\
                        .then_inc(x_done.sem, 1)
                run_front_and_main(v, front, main)

            @block.gpsimd
            def _(g):
                credit(g, ctx)

                def main(b, q, nxt):
                    if nxt:
                        fr.gpsimd(g, *nxt)
                run_front_and_main(g, lambda b, q: fr.gpsimd(g, b, q), main)



STEPS = 8


def run_pairs(eng, front, main):
    front(0)
    with eng.Fori(0, B // 2 - 1) as j:
        main(j, j + 1)
    main(B // 2 - 1, None)


def diffusion(nc, res, X):
    DT = 1.0 / STEPS
    with Stage(nc) as ctx:
        bank = res["bank"]
        sb = lambda n, s: ctx.enter_context(nc.sbuf_tensor("g2_" + n, s, F32))
        c = lambda n, **k: Count(ctx, nc, "g2_" + n, **k)
        fr = Front(ctx, nc, res, X, bank[0], tag="g2_")
        FC, R, TB = bank[1], bank[2:4], bank[4:6]
        sig, s_alpha, diag = sb("sig", [P, T]), sb("s_alpha", [P, T]), sb("diag", [P, T])
        A_n, A_t = sb("A_n", [P, T, N]), sb("A_t", [P, T, N])
        dclip, wd, W = sb("dclip", [P, 1]), sb("wd", [P, D]), sb("W", [P, D])
        hF = [sb(f"hF{q}", [P, N]) for q in range(2)]
        hT = [sb(f"hT{q}", [P, T, D]) for q in range(2)]
        dz = [sb(f"dz{q}", [P, N]) for q in range(2)]
        chain = ctx.sem("g2_set_up")
        w_ready, a_turned, a_copied = (ctx.sem("g2_" + n) for n in ("w_ready", "a_turned", "a_copied"))
        two = lambda n, **k: [c(f"{n}{q}", **k) for q in range(2)]
        fc_ready, h0_ready, dz_ready = two("fc_ready"), two("h0_ready", credit=1), two("dz_ready")
        r_ready, h_ready = two("r_ready", per=STEPS), two("h_ready", credit=1, per=STEPS)
        turned, hT_ready = two("turned", credit=1, per=STEPS + 1), two("hT_ready", per=STEPS)
        x_done = two("x_done", credit=1)

        with nc.Block() as block:
            @block.scalar
            def _(a):
                a.activation(sig[:, :], res["alpha"][:, :], ACT.Sigmoid).then_inc(chain, 1)
                for t in range(T):
                    a.wait_ge(a_turned, t + 1)
                    a.activation(A_t[:, :, t * P:(t + 1) * P],
                                 bank[t][:, :].rearrange("p (m n) -> p m n", m=T), ACT.Copy)\
                        .then_inc(a_copied, 1)

            @block.vector
            def _(v):
                v.wait_ge(chain, 1)
                v.tensor_scalar(s_alpha[:, :], sig[:, :], 0.5 * DT, None, ALU.mult).then_inc(chain, 1)
                v.tensor_scalar(dclip[:, :], res["L2_gnn_d"][:, :], 0.0, 1.0, ALU.max, ALU.min)\
                    .then_inc(chain, 1)
                v.wait_ge(chain, 3)
                v.tensor_scalar(diag[:, :], s_alpha[:, :], -1.0, 1.0 - DT, ALU.mult, ALU.add)
                v.tensor_scalar(wd[:, :], res["L2_gnn_wT"][:, :], dclip[:, 0:1], DT, ALU.mult, ALU.mult)
                for t in range(T):
                    ins = v.tensor_scalar(A_n[:, t, :], res["adj_n"][:, t, :], s_alpha[:, t:t + 1], None,
                                          ALU.mult)
                ins.then_inc(chain, 1)
                v.wait_ge(chain, 4)
                for t in range(T):
                    ins = v.scalar_tensor_tensor(out=A_n[:, t, t * P:(t + 1) * P], in0=res["ident"][:, :],
                                                 scalar=diag[:, t:t + 1],
                                                 in1=A_n[:, t, t * P:(t + 1) * P],
                                                 op0=ALU.mult, op1=ALU.add)
                ins.then_inc(chain, 1)
                v.wait_ge(w_ready, 1)
                v.tensor_copy(W[:, :], bank[4][:, 0:P])

            @block.tensor
            def _(pe):
                pe.wait_ge(chain, 5)
                pe.matmul(bank[4][:, 0:P], wd[:, :], res["L2_gnn_wT"][:, :], start=True, stop=True)\
                    .then_inc(w_ready, 1)
                for t in range(T):
                    for m in range(T):
                        ins = pe.transpose(bank[t][:, m * P:(m + 1) * P], A_n[:, t, m * P:(m + 1) * P],
                                           res["ident"][:, :])
                    ins.then_inc(a_turned, 1)

        with nc.Block() as block:
            @block.tensor
            def _(pe):
                def turn(j, q, s):
                    if s == 0:
                        pe.wait_ge(h0_ready[q].sem, h0_ready[q].done(j))
                        pe.wait_ge(x_done[q].sem, x_done[q].freed(j))
                    else:
                        pe.wait_ge(h_ready[q].sem, h_ready[q].done(j, s))
                        pe.wait_ge(hT_ready[q].sem, hT_ready[q].done(j, s))
                    for t in range(T):
                        ins = pe.transpose(TB[q][:, t * P:(t + 1) * P], hF[q][:, t * P:(t + 1) * P],
                                           res["ident"][:, :])
                    ins.then_inc(turned[q].sem, 1)

                def step(j, q, s):
                    if s == 0:
                        pe.wait_ge(h_ready[q].sem, h_ready[q].done(j, 0))
                    pe.matmul(R[q][:, :], W[:, :], hF[q][:, :], start=True, stop=False)
                    pe.wait_ge(hT_ready[q].sem, hT_ready[q].done(j, s + 1))
                    for m in range(T):
                        ins = pe.matmul(R[q][:, :], hT[q][:, m, :], A_t[:, m, :],
                                        start=False, stop=(m == T - 1))
                    ins.then_inc(r_ready[q].sem, 1)

                def front(j):
                    for q in range(2):
                        fr.tensor(pe, j * 2 + q, q)

                def main(j, nxt):
                    for q in range(2):
                        pe.wait_ge(fr.zF_ready.sem, fr.zF_ready.done(j * 2 + q))
                        if q == 1:
                            pe.wait_ge(h0_ready[0].sem, h0_ready[0].done(j))
                        else:
                            pe.wait_ge(h0_ready[1].sem, h0_ready[1].done(j, 0))
                        pe.matmul(FC[:, :], res["fc_in_wT"][:, :], fr.zF[q][:, :], start=True, stop=True)\
                            .then_inc(fc_ready[q].sem, 1)
                    turn(j, 0, 0)
                    for s in range(STEPS):
                        step(j, 0, s)
                        turn(j, 1, s)
                        step(j, 1, s)
                        turn(j, 0, s + 1)
                        if nxt is not None and s in (4, 5):
                            fr.tensor(pe, nxt * 2 + (s - 4), s - 4)
                    turn(j, 1, STEPS)
                run_pairs(pe, front, main)

            @block.scalar
            def _(a):
                def copy(j, q, s):
                    a.wait_ge(turned[q].sem, turned[q].done(j, s + 1))
                    a.activation(hT[q][:, :, :], TB[q][:, :].rearrange("p (t d) -> p t d", t=T), ACT.Copy)\
                        .then_inc(hT_ready[q].sem, 1)

                def front(j):
                    for q in range(2):
                        fr.scalar(a, j * 2 + q, q)

                def main(j, nxt):
                    for q in range(2):
                        a.wait_ge(fc_ready[q].sem, fc_ready[q].done(j))
                        a.wait_ge(turned[q].sem, turned[q].done(j, 0))
                        a.activation(hF[q][:, :], FC[:, :], ACT.Identity,
                                     bias=res["L2_gnn_fc_in_b"][:, 0:1]).then_inc(h0_ready[q].sem, 1)
                    for q in range(2):
                        a.wait_ge(h_ready[q].sem, h_ready[q].done(j, 0))
                        a.activation(dz[q][:, :], fr.zF[q][:, :], ACT.Copy, scale=DT)\
                            .then_inc(dz_ready[q].sem, 1)
                    for s in range(STEPS):
                        for q in range(2):
                            copy(j, q, s)
                        if nxt is not None and s in (4, 5):
                            fr.scalar(a, nxt * 2 + (s - 4), s - 4)
                run_pairs(a, front, main)

            @block.vector
            def _(v):
                def front(j):
                    for q in range(2):
                        fr.vector_stats(v, j * 2 + q, q)
                        fr.vector_apply(v, j * 2 + q, q)

                def main(j, nxt):
                    for s in range(STEPS):
                        for q in range(2):
                            v.wait_ge(r_ready[q].sem, r_ready[q].done(j, s + 1))
                            if s == 0:
                                v.wait_ge(dz_ready[q].sem, dz_ready[q].done(j))
                            v.tensor_tensor(hF[q][:, :], R[q][:, :], dz[q][:, :], ALU.add)\
                                .then_inc(h_ready[q].sem, 1)
                        if nxt is not None and s in (2, 3):
                            fr.vector_stats(v, nxt * 2 + (s - 2), s - 2)
                        if nxt is not None and s in (3, 4):
                            fr.vector_apply(v, nxt * 2 + (s - 3), s - 3)
                    for q in range(2):
                        v.wait_ge(turned[q].sem, turned[q].done(j))
                        v.tensor_tensor(X[:, j * 2 + q, :, :], X[:, j * 2 + q, :, :],
                                        TB[q][:, :].rearrange("p (t d) -> p t d", t=T), ALU.add)\
                            .then_inc(x_done[q].sem, 1)
                run_pairs(v, front, main)

            @block.gpsimd
            def _(g):
                credit(g, ctx)

                def front(j):
                    for q in range(2):
                        fr.gpsimd(g, j * 2 + q, q)

                def main(j, nxt):
                    if nxt is not None:
                        front(nxt)
                run_pairs(g, front, main)



CHUNK = N // B
PIECE = 8


def lstm(nc, res, X):
    with Stage(nc) as ctx:
        G = res["psum"][:, :, :].rearrange("p (a g) n -> p a g n", a=2)
        sb = lambda n, s: ctx.enter_context(nc.sbuf_tensor("l_" + n, s, F32))
        c = lambda n, **k: Count(ctx, nc, "l_" + n, **k)
        seq = sb("seq", [P, N + 1, B])
        bank = lambda i: G[:, i // 4, i % 4, :]

        with Stage(nc) as inner:
            fr = Front(inner, nc, res, X, None, tag="l_")
            fr.z_turned.credit = 2
            turned_read = Count(inner, nc, "l_turned_read", credit=1)
            with nc.Block() as block:
                def each(eng, body):
                    with eng.Fori(0, B // 2) as j:
                        body(j * 2, 0)
                        body(j * 2 + 1, 1)

                @block.vector
                def _(v):
                    def apply(b, q):
                        v.wait_ge(fr.z_turned.sem, fr.z_turned.freed(b))
                        fr.vector_apply(v, b, q)

                    fr.vector_stats(v, 0, 0)
                    with v.Fori(0, B // 2 - 1) as j:
                        fr.vector_stats(v, j * 2 + 1, 1)
                        apply(j * 2, 0)
                        fr.vector_stats(v, j * 2 + 2, 0)
                        apply(j * 2 + 1, 1)
                    fr.vector_stats(v, B - 1, 1)
                    apply(B - 2, 0)
                    apply(B - 1, 1)

                @block.gpsimd
                def _(g):
                    credit(g, inner)
                    each(g, lambda b, q: fr.gpsimd(g, b, q))

                @block.tensor
                def _(pe):
                    def turn(b, q):
                        pe.wait_ge(fr.z_ready.sem, fr.z_ready.done(b))
                        pe.wait_ge(turned_read.sem, turned_read.freed(b))
                        for t in range(T):
                            ins = pe.transpose(bank(q)[:, t * P:(t + 1) * P], fr.z[q][:, t, :],
                                               res["ident"][:, :])
                        ins.then_inc(fr.z_turned.sem, 1)
                    each(pe, turn)

                @block.scalar
                def _(a):
                    def copy(b, q):
                        a.wait_ge(fr.z_turned.sem, fr.z_turned.done(b))
                        a.activation(seq[:, 1:N + 1, b], bank(q), ACT.Copy).then_inc(turned_read.sem, 1)
                    each(a, copy)

        with Stage(nc) as inner:
            sb2 = lambda n, s: inner.enter_context(nc.sbuf_tensor("l_" + n, s, F32))
            sem = lambda n: inner.sem("l_" + n)
            ones = sb2("ones", [1, PIECE * B])
            b_sum = sb2("b_sum", [1, 4 * D])
            zeros = sb2("zeros", [P, P])
            sig_if, gc = sb2("sig_if", [P, 2, B]), sb2("gc", [P, 2, B])
            prods, sig_o, tanh_c = sb2("prods", [P, 2, B]), sb2("sig_o", [P, B]), sb2("tanh_c", [P, B])
            started = sem("started")
            i_f_ready, g_ready, o_ready = sem("i_f_ready"), sem("g_ready"), sem("o_ready")
            if_g_done, tanh_c_done = sem("if_g_done"), sem("tanh_c_done")
            prods_done, c_done, h_done = sem("prods_done"), sem("c_done"), sem("h_done")

            def chunks(eng, step):
                last = N // CHUNK // 2 - 1

                def two(t0, more):
                    for par in range(2):
                        for s in range(CHUNK):
                            step(t0 + par * CHUNK + s, s, par, more or par == 0)
                with eng.Fori(0, last) as j:
                    two(j * (2 * CHUNK), True)
                two(last * 2 * CHUNK, False)

            with nc.Block() as block:
                @block.tensor
                def _(pe):
                    def piece(t, n, par):
                        gate, k, kind = n // 8, n % 8 // 2, n % 2
                        o = G[:, par, gate, k * P:(k + 1) * P]
                        cols = slice(gate * D, (gate + 1) * D)
                        if kind == 0:
                            pe.matmul(o, b_sum[0:1, cols], ones[0:1, :], start=(k == 0), stop=False,
                                      skip_group_check=True)
                        else:
                            pe.matmul(o, res["W_ihT"][:, cols], seq[:, bass.ds(t + k * PIECE + 1, PIECE), :],
                                      start=False, stop=False, skip_group_check=True)

                    def step(t, s, par, more):
                        pe.wait_ge(h_done, t + 1)
                        for gate, ready in ((0, None), (1, i_f_ready), (2, g_ready), (3, o_ready)):
                            ins = pe.matmul(G[:, par, gate, s * B:(s + 1) * B],
                                            res["W_hhT"][:, gate * D:(gate + 1) * D],
                                            seq[:, t, :],
                                            start=False, stop=True, skip_group_check=True)
                            if ready is not None:
                                ins.then_inc(ready, 1)
                        if more:
                            piece(t - s + CHUNK, s, 1 - par)
                        for _ in range(FILLERS):
                            pe.matmul(G[:, 1 - par, s // 8, s % 8 // 2 * P:(s % 8 // 2 + 1) * P],
                                      zeros[:, :], res["W_ihT"][:, 0:P], start=False, stop=False,
                                      skip_group_check=True)

                    pe.wait_ge(started, 4)
                    for n in range(32):
                        piece(0, n, 0)
                    chunks(pe, step)

                @block.scalar
                def _(a):
                    def step(t, s, par, more):
                        cols = slice(s * B, (s + 1) * B)
                        a.wait_ge(i_f_ready, t + 1)
                        a.activation(sig_if[:, :, :], G[:, par, 0:2, cols], ACT.Sigmoid)
                        a.wait_ge(g_ready, t + 1)
                        a.activation(gc[:, 0, :], G[:, par, 2, cols], ACT.Tanh).then_inc(if_g_done, 1)
                        a.wait_ge(o_ready, t + 1)
                        a.activation(sig_o[:, :], G[:, par, 3, cols], ACT.Sigmoid)
                        a.wait_ge(c_done, t + 2)
                        a.activation(tanh_c[:, :], gc[:, 1, :], ACT.Tanh).then_inc(tanh_c_done, 1)
                    chunks(a, step)

                @block.vector
                def _(v):
                    v.memset(seq[:, 0, :], 0.0).then_inc(h_done, 1)
                    v.memset(gc[:, 1, :], 0.0).then_inc(c_done, 1)
                    v.memset(ones[:, :], 1.0).then_inc(started, 1)
                    v.memset(zeros[:, :], 0.0).then_inc(started, 1)
                    v.tensor_tensor(b_sum[:, :], res["b_ih"][:, :], res["b_hh"][:, :], ALU.add)\
                        .then_inc(started, 2)

                    def step(t, s, par, more):
                        v.wait_ge(c_done, t + 1)
                        v.wait_ge(if_g_done, t + 1)
                        v.tensor_tensor(prods[:, :, :], sig_if[:, :, :], gc[:, :, :], ALU.mult)\
                            .then_inc(prods_done, 1)
                        v.wait_ge(prods_done, t + 1)
                        v.tensor_tensor(gc[:, 1, :], prods[:, 0, :], prods[:, 1, :], ALU.add)\
                            .then_inc(c_done, 1)
                        v.wait_ge(tanh_c_done, t + 1)
                        v.tensor_tensor(seq[:, t + 1, :], sig_o[:, :], tanh_c[:, :], ALU.mult)\
                            .then_inc(h_done, 1)
                    chunks(v, step)

        with Stage(nc) as inner:
            sb2 = lambda n, s: inner.enter_context(nc.sbuf_tensor("l_" + n, s, F32))
            c2 = lambda n, **k: Count(inner, nc, "l_" + n, **k)
            wrep, ones = sb2("wrep", [P, 2, P]), sb2("ones_n", [P, N])
            hc, h2 = res["front_zF"], [z[:, :, :].rearrange("p t d -> p (t d)") for z in res["front_z"]]
            l0 = [sb2(f"l0{i}", [P, N]) for i in range(2)]
            g, w, inc, pre = (sb2(n, [P, N]) for n in ("g", "w", "inc", "pre"))
            suf = g
            oF = [sb2(f"oF{i}", [P, N]) for i in range(2)]
            rep = c2("rep", per=1)
            hc_ready, logits_ready, l0_ready = c2("hc_ready"), c2("logits_ready"), c2("l0_ready")
            ch = Chain(inner, nc, "l_sums", 5)
            oF_ready, oF_turned, x_done = c2("oF_ready", credit=1), c2("oF_turned"), c2("x_done", credit=1)
            LG = [[bank(0), bank(1)], [bank(2), bank(3)]]
            OT = [bank(4), bank(5)]
            with nc.Block() as block:
                @block.tensor
                def _(pe):
                    def logits(b, q):
                        pe.wait_ge(hc_ready.sem, hc_ready.done(b))
                        for k in range(2):
                            ins = pe.matmul(LG[q][k], wrep[:, k, :], hc[q][:, :], start=True, stop=True)
                        ins.then_inc(logits_ready.sem, 1)

                    def main(b, q, nxt):
                        if nxt:
                            logits(*nxt)
                        pe.wait_ge(oF_ready.sem, oF_ready.done(b))
                        pe.wait_ge(x_done.sem, x_done.freed(b))
                        for t in range(T):
                            ins = pe.transpose(OT[q][:, t * P:(t + 1) * P], oF[q][:, t * P:(t + 1) * P],
                                               res["ident"][:, :])
                        ins.then_inc(oF_turned.sem, 1)
                    pe.wait_ge(rep.sem, 2)
                    run_front_and_main(pe, logits, main)

                @block.gpsimd
                def _(g):
                    credit(g, inner)

                @block.scalar
                def _(a):
                    def copy(b, q):
                        a.activation(hc[q][:, :], seq[:, 1:N + 1, b], ACT.Copy).then_inc(hc_ready.sem, 1)
                        a.activation(h2[q][:, :], seq[:, 1:N + 1, b], ACT.Copy, scale=2.0)
                        a.wait_ge(logits_ready.sem, logits_ready.done(b))
                        a.activation(l0[q][:, :], LG[q][0], ACT.Identity, bias=res["b_lin"][:, 0:1])\
                            .then_inc(l0_ready.sem, 1)

                    def main(b, q, nxt):
                        if nxt:
                            a.wait_ge(oF_ready.sem, oF_ready.freed(b))
                            copy(*nxt)
                    run_front_and_main(a, copy, main)

                @block.vector
                def _(v):
                    v.memset(ones[:, :], 1.0).then_inc(rep.sem, 1)
                    v.tensor_copy(wrep[:, :, :], res["W_linT"][:, :].unsqueeze(2).broadcast_to([P, 2, P]))\
                        .then_inc(rep.sem, 1)
                    v.wait_ge(rep.sem, 2)

                    def main(b, q, nxt):
                        ch.begin(b)
                        v.wait_ge(l0_ready.sem, l0_ready.done(b))
                        v.wait_ge(oF_ready.sem, oF_ready.freed(b))
                        ch.link(v, v.scalar_tensor_tensor(
                            out=g[:, :], in0=LG[q][1], scalar=res["b_lin"][:, 1:2], in1=l0[q][:, :],
                            op0=ALU.add, op1=ALU.is_gt))
                        ch.link(v, v.tensor_tensor(w[:, :], g[:, :], hc[q][:, :], ALU.mult))
                        ch.link(v, v.tensor_tensor_scan(inc[:, :], ones[:, :], w[:, :], 0.0,
                                                        ALU.mult, ALU.add))
                        v.tensor_scalar(suf[:, :], inc[:, :], inc[:, N - 1:N], -1.0,
                                        ALU.subtract, ALU.mult)
                        ch.link(v, v.tensor_tensor(pre[:, :], inc[:, :], w[:, :], ALU.subtract))
                        ch.link(v, v.scalar_tensor_tensor(
                            out=pre[:, :], in0=pre[:, :], scalar=res["fw_att"][:, 0:1], in1=h2[q][:, :],
                            op0=ALU.mult, op1=ALU.add))
                        v.scalar_tensor_tensor(
                            out=oF[q][:, :], in0=suf[:, :], scalar=res["bw_att"][:, 0:1], in1=pre[:, :],
                            op0=ALU.mult, op1=ALU.add).then_inc(oF_ready.sem, 1)
                        v.wait_ge(oF_turned.sem, oF_turned.done(b))
                        v.tensor_tensor(X[:, b, :, :], X[:, b, :, :],
                                        OT[q].rearrange("p (t d) -> p t d", t=T), ALU.add)\
                            .then_inc(x_done.sem, 1)
                        ch.end()
                    run_front_and_main(v, lambda b, q: None, main)



def window_lstms(nc, res, X):
    STEPS_P = [(p, s) for p in range(1, 5) for s in range(p)]
    gates_of = lambda s: ("i", "g", "o") if s == 0 else ("i", "g", "f", "o")
    at = {"i": 0, "f": 1, "g": 2, "o": 3}
    place = {"i": 0, "g": 1, "o": 2, "f": 3}
    GATES = sum(len(gates_of(s)) for _, s in STEPS_P)
    RAISES = sum(2 + (s > 0) for _, s in STEPS_P)
    with Stage(nc) as ctx:
        G = [res["bank"][0:4], res["bank"][4:8]]
        sb = lambda n, s: ctx.enter_context(nc.sbuf_tensor("w_" + n, s, F32))
        c = lambda n, **k: Count(ctx, nc, "w_" + n, **k)
        two_sb = lambda n, s: [sb(f"{n}{q}", s) for q in range(2)]
        two = lambda n, **k: [c(f"{n}{q}", **k) for q in range(2)]
        fr = Front(ctx, nc, res, X, None, tag="w_")
        bsum = sb("bsum", [P, 4, 4])
        uT, h1F, hF = two_sb("uT", [P, T, D]), two_sb("h1F", [P, N]), two_sb("hF", [P, N])
        gate = {k: two_sb("gate_" + k, [P, N]) for k in "igfo"}
        cell, state = two_sb("cell", [P, N]), two_sb("state", [P, N // 2])
        bsum_ready = c("bsum_ready")
        u_ready, u_copied = two("u_ready", per=2), two("u_copied", per=2)
        c_ready, c_copied = two("c_ready", per=2, credit=1), two("c_copied", per=2)
        gate_ready = two("gate_ready", per=GATES)
        act_done = two("act_done", per=RAISES)
        parts_done = two("parts_done", per=len(STEPS_P) - 4)
        cell_done, h_done = two("cell_done", per=len(STEPS_P)), two("h_done", per=len(STEPS_P))
        h_turned, x_done = two("h_turned"), two("x_done", credit=1)
        windows = lambda p: N // p
        cols = lambda p, s: bass.ds(s, windows(p), p) if p > 1 else slice(0, N)

        def steps():
            g = r = f = 0
            for n, (p, s) in enumerate(STEPS_P):
                yield n, p, s, g, r, f
                g += len(gates_of(s))
                r += 2 + (s > 0)
                f += s > 0

        with nc.Block() as block:
            @block.tensor
            def _(pe):
                def lin(j, q, k):
                    if k == 0:
                        pe.wait_ge(fr.zF_ready.sem, fr.zF_ready.done(j * 2 + q))
                        pe.wait_ge(x_done[q].sem, x_done[q].freed(j))
                    else:
                        pe.wait_ge(c_copied[q].sem, c_copied[q].done(j, 1))
                    src = (fr.zF[q], h1F[q])[k]
                    w = res[("L3_gnn_Wg0", "L3_gnn_Wg1")[k]]
                    for t in range(T):
                        ins = pe.matmul(G[q][3][:, t * P:(t + 1) * P], src[:, t * P:(t + 1) * P], w[:, :],
                                        start=True, stop=True)
                    ins.then_inc(u_ready[q].sem, 1)

                def conv(j, q, k):
                    pe.wait_ge(u_copied[q].sem, u_copied[q].done(j, k + 1))
                    for m in range(T):
                        ins = pe.matmul(G[q][0][:, :], uT[q][:, m, :], res["adj_t"][:, m, :],
                                        start=(m == 0), stop=(m == T - 1))
                    ins.then_inc(c_ready[q].sem, 1)

                def step(j, q, n, p, s):
                    if n == 0:
                        pe.wait_ge(c_copied[q].sem, c_copied[q].done(j, 2))
                    else:
                        pe.wait_ge(h_done[q].sem, h_done[q].done(j, n))
                    nw = windows(p)
                    x = hF[q][:, cols(p, s)]
                    for k in gates_of(s):
                        o = G[q][place[k]][:, 0:nw]
                        wc = slice(at[k] * D, (at[k] + 1) * D)
                        ins = pe.matmul(o, res["WihT"][:, p - 1, wc], x, start=True, stop=(s == 0))
                        if s > 0:
                            ins = pe.matmul(o, res["WhhT"][:, p - 1, wc], state[q][:, 0:nw],
                                            start=False, stop=True)
                        ins.then_inc(gate_ready[q].sem, 1)

                def front(j):
                    for q in range(2):
                        turn_z(j, q)

                def turn_z(j, q):
                    b = j * 2 + q
                    pe.wait_ge(fr.z_ready.sem, fr.z_ready.done(b))
                    for t in range(T):
                        ins = pe.transpose(G[q][3][:, t * P:(t + 1) * P], fr.z[q][:, t, :],
                                           res["ident"][:, :])
                    ins.then_inc(fr.z_turned.sem, 1)

                def main(j, nxt):
                    for k in range(2):
                        for q in range(2):
                            lin(j, q, k)
                        for q in range(2):
                            conv(j, q, k)
                    for n, p, s, *_ in steps():
                        for q in range(2):
                            if n == 2 and nxt is not None:
                                pe.wait_ge(fr.zF_ready.sem, fr.zF_ready.done(nxt * 2 + q))
                            step(j, q, n, p, s)
                        if n == 0 and nxt is not None:
                            front(nxt)
                    for q in range(2):
                        pe.wait_ge(h_done[q].sem, h_done[q].done(j))
                        for t in range(T):
                            ins = pe.transpose(G[q][3][:, t * P:(t + 1) * P], hF[q][:, t * P:(t + 1) * P],
                                               res["ident"][:, :])
                        ins.then_inc(h_turned[q].sem, 1)
                run_pairs(pe, front, main)

            @block.scalar
            def _(a):
                def copy_z(j):
                    for q in range(2):
                        b = j * 2 + q
                        a.wait_ge(fr.z_turned.sem, fr.z_turned.done(b))
                        a.activation(fr.zF[q][:, :], G[q][3][:, :], ACT.Copy).then_inc(fr.zF_ready.sem, 1)

                def main(j, nxt):
                    for k in range(2):
                        for q in range(2):
                            a.wait_ge(c_ready[q].sem, c_ready[q].done(j, k + 1))
                            a.activation((h1F, hF)[k][q][:, :], G[q][0][:, :], ACT.Relu)\
                                .then_inc(c_copied[q].sem, 1)

                    def gates(q, n, p, s, g0):
                        nw = windows(p)
                        for i, k in enumerate(gates_of(s)):
                            a.wait_ge(gate_ready[q].sem, gate_ready[q].done(j, g0 + i + 1))
                            ins = a.activation(gate[k][q][:, 0:nw], G[q][place[k]][:, 0:nw],
                                               ACT.Tanh if k == "g" else ACT.Sigmoid,
                                               bias=bsum[:, p - 1, at[k]:at[k] + 1])
                            if k in "gf":
                                ins.then_inc(act_done[q].sem, 1)

                    def tanh(q, n, p):
                        nw = windows(p)
                        a.wait_ge(cell_done[q].sem, cell_done[q].done(j, n + 1))
                        a.activation(gate["g"][q][:, 0:nw], cell[q][:, 0:nw], ACT.Tanh)\
                            .then_inc(act_done[q].sem, 1)

                    for n, p, s, g0, *_ in steps():
                        gates(0, n, p, s, g0)
                        tanh(0, n, p)
                        gates(1, n, p, s, g0)
                        tanh(1, n, p)
                        if n == 0 and nxt is not None:
                            copy_z(nxt)

                a.wait_ge(bsum_ready.sem, 1)
                run_pairs(a, copy_z, main)

            @block.vector
            def _(v):
                v.tensor_tensor(bsum[:, :, :], res["bih"][:, :, :], res["bhh"][:, :, :], ALU.add)\
                    .then_inc(bsum_ready.sem, 1)

                def front(j):
                    for q in range(2):
                        fr.vector_stats(v, j * 2 + q, q)
                        fr.vector_apply(v, j * 2 + q, q)

                def main(j, nxt):
                    for k in range(2):
                        for q in range(2):
                            v.wait_ge(u_ready[q].sem, u_ready[q].done(j, k + 1))
                            v.wait_ge(c_ready[q].sem, c_ready[q].done(j, k))
                            bias = res[("row_L3_gnn_bg0", "row_L3_gnn_bg1")[k]]
                            v.tensor_tensor(uT[q][:, :, :], G[q][3][:, :].rearrange("p (t d) -> p t d", t=T),
                                            bias[:, :].unsqueeze(1).broadcast_to([P, T, D]), ALU.add)\
                                .then_inc(u_copied[q].sem, 1)
                        if k == 0 and nxt is not None:
                            front(nxt)

                    def cell_of(q, n, p, s, r0, f0):
                        nw = windows(p)
                        i, g, f = (gate[k][q][:, 0:nw] for k in "igf")
                        cc = cell[q][:, 0:nw]
                        v.wait_ge(act_done[q].sem, act_done[q].done(j, r0 + 1))
                        if s == 0:
                            v.tensor_tensor(cc, i, g, ALU.mult).then_inc(cell_done[q].sem, 1)
                        else:
                            v.tensor_tensor(i, i, g, ALU.mult)
                            v.wait_ge(act_done[q].sem, act_done[q].done(j, r0 + 2))
                            v.tensor_tensor(cc, f, cc, ALU.mult).then_inc(parts_done[q].sem, 1)
                            v.wait_ge(parts_done[q].sem, parts_done[q].done(j, f0 + 1))
                            v.tensor_tensor(cc, cc, i, ALU.add).then_inc(cell_done[q].sem, 1)

                    def h_of(q, n, p, s, r0):
                        nw = windows(p)
                        v.wait_ge(act_done[q].sem, act_done[q].done(j, r0 + 2 + (s > 0)))
                        out = hF[q][:, cols(p, s)] if s == p - 1 else state[q][:, 0:nw]
                        v.tensor_tensor(out, gate["o"][q][:, 0:nw], gate["g"][q][:, 0:nw], ALU.mult)\
                            .then_inc(h_done[q].sem, 1)

                    for n, p, s, g0, r0, f0 in steps():
                        for q in range(2):
                            cell_of(q, n, p, s, r0, f0)
                            h_of(q, n, p, s, r0)
                    for q in range(2):
                        v.wait_ge(h_turned[q].sem, h_turned[q].done(j))
                        v.tensor_tensor(X[:, j * 2 + q, :, :], X[:, j * 2 + q, :, :],
                                        G[q][3][:, :].rearrange("p (t d) -> p t d", t=T), ALU.add)\
                            .then_inc(x_done[q].sem, 1)
                run_pairs(v, front, main)

            @block.gpsimd
            def _(g):
                credit(g, ctx)

                def front(j):
                    for q in range(2):
                        fr.gpsimd(g, j * 2 + q, q)

                def main(j, nxt):
                    if nxt is not None:
                        front(nxt)
                run_pairs(g, front, main)



def attention(nc, res, X, X1):
    U = HEADS * T
    SCALE = float(HD) ** -0.5
    with Stage(nc) as ctx:
        bank = res["bank"]
        sb = lambda n, s: ctx.enter_context(nc.sbuf_tensor("a_" + n, s, F32))
        c = lambda n, **k: Count(ctx, nc, "a_" + n, **k)
        two_sb = lambda n, s: [sb(f"{n}{q}", s) for q in range(2)]
        PJ, S, PT, O = bank[0:3], bank[3:5], bank[5:7], bank[7]
        fr = Front(ctx, nc, res, X, None, tag="a_")
        h, ms, ve2 = two_sb("h", [P, T, D]), sb("ms", [P, T]), sb("ve2", [P, T])
        rstd2 = sb("rstd2", [P, T])
        qF, kF, vT = two_sb("qF", [P, N]), two_sb("kF", [P, N]), two_sb("vT", [P, T, 64])
        rot_a, rot_b = sb("rot_a", [P, N]), sb("rot_b", [P, N])
        sm, prob, probT = two_sb("sm", [P, N]), two_sb("prob", [P, N]), two_sb("probT", [P, T, P])
        top, ntop = two_sb("top", [P, U]), two_sb("ntop", [P, U])
        total, rtotal = two_sb("total", [P, U]), sb("rtotal", [P, U])
        y, yF, x1 = sb("y", [P, T, D]), sb("yF", [P, N]), sb("x1", [P, T, D])
        ms_ready, ve2_ready, rstd2_ready = c("ms_ready"), c("ve2_ready"), c("rstd2_ready")
        h_ready, h_turned, hF_ready = c("h_ready"), c("h_turned"), c("hF_ready")
        qk_ready = c("qk_ready", per=4)
        rotated = c("rotated", per=4)
        qk_done = c("qk_done", per=2, credit=1)
        v_ready, v_copied = c("v_ready"), c("v_copied")
        s_ready = c("s_ready", per=U)
        masked = c("masked", per=U, credit=2)
        ntop_ready = c("ntop_ready", per=U)
        prob_ready = c("prob_ready", per=U, credit=2)
        turned = c("turned", per=U, credit=2)
        probT_ready = c("probT_ready", per=U, credit=2)
        o_ready = c("o_ready", per=U, credit=2)
        rtotal_ready, y_ready, y_turned, yF_ready = (c("rtotal_ready"), c("y_ready", credit=1), c("y_turned"),
                                                     c("yF_ready"))
        wo_ready, x1_ready, x_done = c("wo_ready"), c("x1_ready"), c("x_done")

        def run(eng, front, main):
            front(0, 0)
            main(0, 0, (1, 1), None)
            with eng.Fori(0, B // 2 - 1) as j:
                main(j * 2 + 1, 1, (j * 2 + 2, 0), (j * 2, 0))
                main(j * 2 + 2, 0, (j * 2 + 3, 1), (j * 2 + 1, 1))
            main(B - 1, 1, None, (B - 2, 0))
            main(None, None, None, (B - 1, 1))

        with nc.Block() as block:
            @block.tensor
            def _(pe):
                def turn_h(b, q):
                    pe.wait_ge(h_ready.sem, h_ready.done(b))
                    for t in range(T):
                        ins = pe.transpose(PJ[0][:, t * P:(t + 1) * P], h[q][:, t, :], res["ident"][:, :])
                    ins.then_inc(h_turned.sem, 1)

                def project(b, q, k):
                    pe.wait_ge(hF_ready.sem, hF_ready.done(b))
                    if k < 2:
                        if k == 1:
                            pe.wait_ge(rotated.sem, rotated.done(b, 2))
                        for i, w in enumerate((("wqT", "wqrT"), ("wkT", "wkrT"))[k]):
                            pe.matmul(PJ[1 + i][:, :], res[w][:, :], fr.zF[q][:, :], start=True, stop=True)\
                                .then_inc(qk_ready.sem, 1)
                    else:
                        for t in range(T):
                            ins = pe.matmul(PJ[0][:, t * 64:(t + 1) * 64], fr.zF[q][:, t * P:(t + 1) * P],
                                            res["wvT"][:, :], start=True, stop=True)
                        ins.then_inc(v_ready.sem, 1)

                def scores(b, q, u):
                    hd, t = u // T, u % T
                    rows = slice(hd * HD, (hd + 1) * HD)
                    if u == 0:
                        pe.wait_ge(qk_done.sem, qk_done.done(b))
                    pe.wait_ge(masked.sem, masked.freed(b, u + 1))
                    pe.matmul(S[u % 2][:, 0:(t + 1) * P], qF[q][rows, t * P:(t + 1) * P],
                              kF[q][rows, 0:(t + 1) * P], start=True, stop=True).then_inc(s_ready.sem, 1)

                def turn(b, q, u):
                    pe.wait_ge(prob_ready.sem, prob_ready.done(b, u + 1))
                    pe.wait_ge(probT_ready.sem, probT_ready.freed(b, u + 1))
                    for m in range(u % T + 1):
                        ins = pe.transpose(PT[u % 2][:, m * P:(m + 1) * P],
                                           prob[u % 2][:, m * P:(m + 1) * P], res["ident"][:, :])
                    ins.then_inc(turned.sem, 1)

                def attend(b, q, u):
                    hd, t = u // T, u % T
                    kv = hd // 2 * HD
                    if u == 0:
                        pe.wait_ge(v_copied.sem, v_copied.done(b))
                        pe.wait_ge(y_ready.sem, y_ready.freed(b))
                    pe.wait_ge(probT_ready.sem, probT_ready.done(b, u + 1))
                    for m in range(t + 1):
                        ins = pe.matmul(O[:, t * P + hd * HD:t * P + (hd + 1) * HD], probT[u % 2][:, m, :],
                                        vT[q][:, m, kv:kv + HD], start=(m == 0), stop=(m == t))
                    ins.then_inc(o_ready.sem, 1)

                def tail(b, q, k):
                    if k == 0:
                        pe.wait_ge(y_ready.sem, y_ready.done(b))
                        for t in range(T):
                            ins = pe.transpose(PJ[1][:, t * P:(t + 1) * P], y[:, t, :], res["ident"][:, :])
                        ins.then_inc(y_turned.sem, 1)
                    else:
                        pe.wait_ge(yF_ready.sem, yF_ready.done(b))
                        for t in range(T):
                            ins = pe.matmul(PJ[2][:, t * P:(t + 1) * P], yF[:, t * P:(t + 1) * P],
                                            res["woT"][:, :], start=True, stop=True)
                        ins.then_inc(wo_ready.sem, 1)

                def front(b, q):
                    turn_h(b, q)
                    for k in range(3):
                        project(b, q, k)
                    scores(b, q, 0)
                    scores(b, q, 1)

                def main(b, q, nxt, prev):
                    for u in range(U):
                        if prev and u == 0:
                            tail(*prev, 0)
                        if prev and u == 2:
                            tail(*prev, 1)
                        if b is None:
                            continue
                        if u + 2 < U:
                            scores(b, q, u + 2)
                        elif nxt:
                            scores(*nxt, u + 2 - U)
                        if nxt and u == 9:
                            turn_h(*nxt)
                        if nxt and u == 10:
                            if prev:
                                pe.wait_ge(x1_ready.sem, x1_ready.done(prev[0]))
                            project(*nxt, 0)
                        if nxt and u == 12:
                            project(*nxt, 1)
                        if nxt and u == 13:
                            project(*nxt, 2)
                        turn(b, q, u)
                        if u:
                            attend(b, q, u - 1)
                    if b is not None:
                        attend(b, q, U - 1)
                run(pe, front, main)

            @block.scalar
            def _(a):
                def copy_h(b, q):
                    a.wait_ge(h_turned.sem, h_turned.done(b))
                    a.activation(fr.zF[q][:, :], PJ[0][:, :], ACT.Copy, scale=res["ln1_w"][:, 0:1])\
                        .then_inc(hF_ready.sem, 1)

                def copy_v(b, q):
                    a.wait_ge(v_ready.sem, v_ready.done(b))
                    a.activation(vT[q][:, :, :], PJ[0][:, 0:T * 64].rearrange("p (t d) -> p t d", t=T),
                                 ACT.Copy).then_inc(v_copied.sem, 1)

                def exp(b, q, u):
                    w = (u % T + 1) * P
                    a.wait_ge(ntop_ready.sem, ntop_ready.done(b, u + 1))
                    a.wait_ge(turned.sem, turned.freed(b, u + 1))
                    at = u % T * HEADS + u // T
                    a.activation(prob[u % 2][:, 0:w], sm[u % 2][:, 0:w], ACT.Exp, scale=SCALE,
                                 bias=ntop[q][:, u:u + 1], accum_out=total[q][:, at:at + 1])\
                        .then_inc(prob_ready.sem, 1)

                def front(b, q):
                    copy_h(b, q)
                    copy_v(b, q)

                def main(b, q, nxt, prev):
                    for u in range(U):
                        if prev and u == 0:
                            a.wait_ge(y_turned.sem, y_turned.done(prev[0]))
                            a.activation(yF[:, :], PJ[1][:, :], ACT.Copy).then_inc(yF_ready.sem, 1)
                        if b is None:
                            continue
                        exp(b, q, u)
                        if nxt and u == 9:
                            copy_h(*nxt)
                        if nxt and u == 13:
                            copy_v(*nxt)
                run(a, front, main)

            @block.vector
            def _(v):
                def rms(b, q):
                    v.wait_ge(fr.z_ready.sem, fr.z_ready.done(b))
                    for t in range(T):
                        ins = v.tensor_tensor_reduce(h[q][:, t, :], fr.z[q][:, t, :], fr.z[q][:, t, :],
                                                     1.0, 0.0, ALU.mult, ALU.add, ms[:, t:t + 1])
                    ins.then_inc(ms_ready.sem, 1)

                def rms_apply(b, q):
                    v.wait_ge(rstd2_ready.sem, rstd2_ready.done(b))
                    for t in range(T):
                        ins = v.tensor_scalar(h[q][:, t, :], fr.z[q][:, t, :], rstd2[:, t:t + 1],
                                              float(D) ** 0.5, ALU.mult, ALU.mult)
                    ins.then_inc(h_ready.sem, 1)

                def rotate(b, q, k):
                    for i, (out, table) in enumerate(((rot_a, "cos"), (rot_b, "sin"))):
                        v.wait_ge(qk_ready.sem, qk_ready.done(b, 2 * k + i + 1))
                        if i == 0:
                            v.wait_ge(qk_done.sem, qk_done.done(b, k))
                        v.tensor_tensor(out[:, :], PJ[1 + i][:, :], res[table][:, :], ALU.mult)\
                            .then_inc(rotated.sem, 1)
                    v.wait_ge(rotated.sem, rotated.done(b, 2 * k + 2))
                    v.tensor_tensor((qF, kF)[k][q][:, :], rot_a[:, :], rot_b[:, :], ALU.add)\
                        .then_inc(qk_done.sem, 1)

                def mask(b, q, u):
                    w = (u % T + 1) * P
                    v.wait_ge(s_ready.sem, s_ready.done(b, u + 1))
                    v.wait_ge(prob_ready.sem, prob_ready.freed(b, u + 1))
                    hold(v, res)
                    v.tensor_tensor_reduce(sm[u % 2][:, 0:w], S[u % 2][:, 0:w], res["tri"][:, N - w:N],
                                           1.0, -3e38, ALU.add, ALU.max, top[q][:, u:u + 1])\
                        .then_inc(masked.sem, 1)
                    v.wait_ge(masked.sem, masked.done(b, u + 1))
                    v.tensor_scalar(ntop[q][:, u:u + 1], top[q][:, u:u + 1], -SCALE, None, ALU.mult)\
                        .then_inc(ntop_ready.sem, 1)

                def copy(b, q, u):
                    w = (u % T + 1) * P
                    v.wait_ge(turned.sem, turned.done(b, u + 1))
                    v.wait_ge(o_ready.sem, o_ready.freed(b, u + 1))
                    v.tensor_copy(probT[u % 2][:, 0:u % T + 1, :],
                                  PT[u % 2][:, 0:w].rearrange("p (m n) -> p m n", n=P))\
                        .then_inc(probT_ready.sem, 1)

                def finish(b, q):
                    v.wait_ge(o_ready.sem, o_ready.done(b, U))
                    v.reciprocal(rtotal[:, :], total[q][:, :]).then_inc(rtotal_ready.sem, 1)
                    v.wait_ge(rtotal_ready.sem, rtotal_ready.done(b))
                    v.tensor_tensor(y[:, :, :].rearrange("p t (h d) -> p (t h) d", d=HD),
                                    O[:, :].rearrange("p (g d) -> p g d", d=HD),
                                    rtotal[:, :].unsqueeze(2).broadcast_to([P, U, HD]), ALU.mult)\
                        .then_inc(y_ready.sem, 1)

                def tail(b, q):
                    v.wait_ge(wo_ready.sem, wo_ready.done(b))
                    v.tensor_tensor(X1[:, b, :, :], PJ[2][:, :].rearrange("p (t d) -> p t d", t=T),
                                    fr.z[q][:, :, :], ALU.add).then_inc(x1_ready.sem, 1)
                    v.wait_ge(x1_ready.sem, x1_ready.done(b))
                    v.tensor_tensor(X[:, b, :, :], X[:, b, :, :], X1[:, b, :, :], ALU.add)\
                        .then_inc(x_done.sem, 1)

                def front(b, q):
                    fr.vector_stats(v, b, q)
                    fr.vector_apply(v, b, q)
                    rms(b, q)
                    rms_apply(b, q)
                    rotate(b, q, 0)
                    rotate(b, q, 1)
                    mask(b, q, 0)

                def main(b, q, nxt, prev):
                    for u in range(U):
                        if prev and u == 3:
                            tail(*prev)
                        if b is None:
                            continue
                        if u + 1 < U:
                            mask(b, q, u + 1)
                        elif nxt:
                            mask(*nxt, 0)
                        copy(b, q, u)
                        if not nxt:
                            continue
                        if u == 4:
                            fr.vector_stats(v, *nxt)
                        if u == 5:
                            fr.vector_apply(v, *nxt)
                        if u == 6:
                            rms(*nxt)
                        if u == 7:
                            rms_apply(*nxt)
                        if u == 10:
                            rotate(*nxt, 0)
                        if u == 12:
                            rotate(*nxt, 1)
                    if b is not None:
                        finish(b, q)
                run(v, front, main)

            @block.gpsimd
            def _(g):
                credit(g, ctx)

                def front(b, q):
                    fr.gpsimd(g, b, q)
                    g.wait_ge(ms_ready.sem, ms_ready.done(b))
                    g.tensor_tensor(ve2[:, :], ms[:, :], res["eps_rms"][:, :], ALU.add)\
                        .then_inc(ve2_ready.sem, 1)
                    g.wait_ge(ve2_ready.sem, ve2_ready.done(b))
                    g.tensor_tensor(rstd2[:, :], ve2[:, :], res["nhalf"][:, :], ALU.pow)\
                        .then_inc(rstd2_ready.sem, 1)

                def main(b, q, nxt, prev):
                    if nxt:
                        front(*nxt)
                run(g, front, main)



STAGES = ("graph_convolution", "mixture_0", "graph_attention", "mixture_1", "diffusion", "lstm",
          "window_lstms", "attention", "mixture_3")


def program(nc, ap, out, stages=STAGES):
    with ExitStack() as late:
        with ExitStack() as early:
            res = load_all(late, early, nc, ap)
            X = res["X"]
            if "graph_convolution" in stages:
                graph_convolution(nc, res, res["adj_t"], X)
            if "mixture_0" in stages:
                mixture(nc, res, X, "m0_", {k: res["L0_" + k] for k in ("Wg", "W1", "b1", "W2", "b2")},
                        [P, P], ACT.Relu, "logits", None, (res["L0_bg"], res["L0_bias"]), True, False)
            if "graph_attention" in stages:
                graph_attention(nc, res, X)
            if "mixture_1" in stages:
                mixture(nc, res, X, "m1_", {k: res["L1_" + k] for k in ("Wg", "W1", "b1", "W2", "b2")},
                        [P], ACT.Gelu, "probs", (ALU.max, 1e-12), None, True, True)
            if "diffusion" in stages:
                diffusion(nc, res, X)
            if "lstm" in stages:
                lstm(nc, res, X)
        if "window_lstms" in stages:
            window_lstms(nc, res, X)
        X1 = late.enter_context(nc.sbuf_tensor("r_X1", [P, B, T, D], F32))
        if "attention" in stages:
            attention(nc, res, X, X1)
        if "mixture_3" in stages:
            mixture(nc, res, X, "m3_", {k: res["L3_" + k] for k in ("Wg", "W1", "W3", "W2")},
                    [P, P, 341 - 2 * P], ACT.Silu, "probs", (ALU.add, 1e-9), None, False, False,
                    src=X1, kind="rms", weight=res["ln2_w"][:, 0:1])
        y_out = out.rearrange("b (t p) d -> p b t d", p=P)
        with Stage(nc) as ctx, nc.Block() as block:
            out_written = ctx.sem("out_written")

            @block.sync
            def _(sp):
                for b in range(B):
                    sp.dma_start(y_out[:, b, :, :], X[:, b, :, :]).then_inc(out_written, 16)
                sp.wait_ge(out_written, 16 * B)


def layouts(i):
    import numpy as np
    t = lambda a: np.ascontiguousarray(a)
    g = {k: np.asarray(a) for k, a in i.items()}
    d = {}
    for n in ("x", "adj", "L0_gnn_w1_loop", "L0_gnn_w1_neigh", "L0_gnn_b1", "L0_gnn_w2_loop",
              "L0_gnn_w2_neigh", "L0_gnn_b2", "L0_ffn_Wg", "L0_ffn_bg", "L0_ffn_bias", "L0_ffn_W1",
              "L0_ffn_W2", "L0_ffn_b2", "L1_gnn_W", "L1_gnn_b_lin", "L1_gnn_b", "L1_ffn_w1", "L1_ffn_w2",
              "L1_ffn_b2", "L2_gnn_d", "L2_gnn_fc_in_b",
              "L2_ffn_b_ih", "L2_ffn_b_hh", "L2_ffn_b_lin", "L3_gnn_Wg0", "L3_gnn_bg0", "L3_gnn_Wg1",
              "L3_gnn_bg1"):
        d[n] = t(g[n])
    d["alpha"] = t(g["L2_gnn_alpha_train"].reshape(T, P).T)
    d["adj_t"] = t(g["adj"].T)
    d["L2_gnn_wT"] = t(g["L2_gnn_w"].T)
    d["fc_in_wT"] = t(g["L2_gnn_fc_in_w"].T)
    d["fw_att"], d["bw_att"] = t(g["L2_ffn_fw_att"][0]), t(g["L2_ffn_bw_att"][0])
    d["ln1_w"], d["ln2_w"] = t(g["L3_ffn_ln1_w"]), t(g["L3_ffn_ln2_w"])
    d["L0_b1c"] = t(g["L0_ffn_b1"].reshape(E, 2, P).transpose(2, 0, 1))
    d["L1_router_wT"] = t(g["L1_ffn_router_w"].T)
    d["L1_b1c"] = t(g["L1_ffn_b1"].reshape(E, 1, P).transpose(2, 0, 1))
    d["W_ihT"], d["W_hhT"] = t(g["L2_ffn_W_ih"].T), t(g["L2_ffn_W_hh"].T)
    d["W_linT"] = t(g["L2_ffn_W_lin"].T)
    d["WihT"] = t(g["L3_gnn_Wih"].transpose(2, 0, 1))
    d["WhhT"] = t(g["L3_gnn_Whh"].transpose(2, 0, 1))
    d["bihc"] = t(g["L3_gnn_bih"].reshape(4, 4, P).transpose(2, 0, 1))
    d["bhhc"] = t(g["L3_gnn_bhh"].reshape(4, 4, P).transpose(2, 0, 1))
    swap = np.arange(P) ^ (HD // 2)
    wq, wk = g["L3_ffn_wq"], g["L3_ffn_wk"]
    wk = np.repeat(wk.reshape(2, HD, D), 2, axis=0).reshape(P, D)
    d["wqT"], d["wqrT"], d["wkT"], d["wkrT"] = t(wq.T), t(wq[swap].T), t(wk.T), t(wk[swap].T)
    d["wvT"], d["woT"] = t(g["L3_ffn_wv"].T), t(g["L3_ffn_wo"].T)
    freq = 1.0 / 10000.0 ** (np.arange(0, HD, 2, dtype=np.float32) / HD)
    angle = np.outer(np.arange(N, dtype=np.float32), freq)
    angle = np.concatenate([angle, angle], axis=-1).T
    sign = np.where(np.arange(HD) < HD // 2, -1.0, 1.0)[:, None]
    d["cos_table"] = np.tile(np.cos(angle), (HEADS, 1)).astype(np.float32)
    d["sin_table"] = np.tile(np.sin(angle) * sign, (HEADS, 1)).astype(np.float32)
    d["L3_router_wT"] = t(g["L3_ffn_router_w"].T)
    d["L3_w1T"] = t(g["L3_ffn_w1"].transpose(2, 0, 1))
    d["L3_w3T"] = t(g["L3_ffn_w3"].transpose(2, 0, 1))
    d["L3_w2T"] = t(g["L3_ffn_w2"].transpose(0, 2, 1))
    return d


def kernel(**inputs):
    import concourse.bacc as bacc
    from concourse.bass_utils import run_bass_kernel_spmd

    nc = bacc.Bacc("TRN2", target_bir_lowering=False, num_devices=1)
    arrays, ap = {}, {}
    for name, a in layouts(inputs).items():
        arrays["in_" + name] = a
        ap[name] = nc.dram_tensor("in_" + name, a.shape, mybir.dt.from_np(a.dtype), kind="ExternalInput").ap()
    out = nc.dram_tensor("out_x", (B, N, D), F32, kind="ExternalOutput").ap()
    program(nc, ap, out)
    return run_bass_kernel_spmd(nc, [arrays], core_ids=[0]).results[0]["out_x"]
```

```python
from contextlib import ExitStack

import concourse.bass as bass
from concourse import mybir

F32 = mybir.dt.float32
F32R = mybir.dt.float32r
U32 = mybir.dt.uint32
ALU = mybir.AluOpType
ACT = mybir.ActivationFunctionType
AX = mybir.AxisListType.X

P = 128
B, N, D = 16, 512, 128
T = N // P
E = 8
HEADS, HD = 4, 32
FILLERS = 5
EPS_LN = 1e-05
EPS_RMS = 1e-06


class Stage(ExitStack):

    def __init__(self, nc):
        super().__init__()
        self.nc, self.sems, self.counts = nc, [], []

    def sem(self, name):
        self.sems.append(self.nc.alloc_semaphore(name))
        return self.sems[-1]

    def __exit__(self, *what):
        if self.sems and what[0] is None:
            self.nc.clear_and_free_semaphores(self.sems)
            self.nc.all_engine_barrier()
        return super().__exit__(*what)


class Count:

    def __init__(self, ctx, nc, name, per=1, credit=0):
        self.sem = ctx.sem(name)
        ctx.counts.append(self)
        self.per = per
        self.credit = credit
        self.name = name

    def done(self, b, k=None):
        return b * self.per + (self.per if k is None else k) + self.credit

    def freed(self, b, k=None):
        return b * self.per + (self.per if k is None else k)


class Chain:

    def __init__(self, ctx, nc, name, per):
        self.count = Count(ctx, nc, name, per)
        self.k = 0

    def begin(self, b):
        self.b, self.k = b, 0

    def link(self, eng, ins):
        self.k += 1
        ins.then_inc(self.count.sem, 1)
        eng.wait_ge(self.count.sem, self.count.done(self.b, self.k))

    def end(self):
        assert self.k == self.count.per, (self.count.name, self.k)


def hold(eng, res):
    eng.sem_inc(res["holds"], 1)


class Front:

    def __init__(self, ctx, nc, res, src, pt_bank, kind="layernorm", weight=None, tag=""):
        self.res = res
        self.src, self.pt, self.kind, self.weight = src, pt_bank, kind, weight
        self.ident, self.eps, self.nhalf = res["ident"], res["eps_" + kind], res["nhalf"]
        self.z, self.zF, self.st, self.mv, self.ve, self.rstd = (
            res["front_" + n] for n in ("z", "zF", "st", "mv", "ve", "rstd"))
        c = lambda n, **k: Count(ctx, nc, tag + n, **k)
        self.stats = c("ln_stats")
        self.moments = c("ln_moments")
        self.eps_added = c("ln_eps_added")
        self.rstd_ready = c("ln_rstd_ready")
        self.z_ready = c("z_ready")
        self.z_turned = c("z_turned")
        self.zF_ready = c("zF_ready", credit=1)

    def vector_stats(self, v, b, q):
        if self.kind == "layernorm":
            for t in range(T):
                ins = v.bn_stats(self.st[q][:, t, :], self.src[:, b, t, :])
            ins.then_inc(self.stats.sem, 1)
            v.wait_ge(self.stats.sem, self.stats.done(b))
            hold(v, self.res)
            for t in range(T):
                ins = v.bn_aggr(self.mv[q][:, t, :], self.st[q][:, t, :])
            ins.then_inc(self.moments.sem, 1)
        else:
            for t in range(T):
                ins = v.scalar_tensor_tensor(out=self.z[q][:, t, :], in0=self.src[:, b, t, :], scalar=1.0,
                                             in1=self.src[:, b, t, :], op0=ALU.mult, op1=ALU.mult,
                                             accum_out=self.mv[q][:, t, 1:2])
            ins.then_inc(self.moments.sem, 1)

    def gpsimd(self, g, b, q):
        g.wait_ge(self.moments.sem, self.moments.done(b))
        g.tensor_tensor(self.ve[q][:, :], self.mv[q][:, :, 1], self.eps[:, :], ALU.add)\
            .then_inc(self.eps_added.sem, 1)
        g.wait_ge(self.eps_added.sem, self.eps_added.done(b))
        g.tensor_tensor(self.rstd[q][:, :], self.ve[q][:, :], self.nhalf[:, :], ALU.pow)\
            .then_inc(self.rstd_ready.sem, 1)

    def vector_apply(self, v, b, q):
        v.wait_ge(self.rstd_ready.sem, self.rstd_ready.done(b))
        for t in range(T):
            if self.kind == "layernorm":
                ins = v.tensor_scalar(self.z[q][:, t, :], self.src[:, b, t, :], self.mv[q][:, t, 0:1],
                                      self.rstd[q][:, t:t + 1], ALU.subtract, ALU.mult)
            else:
                ins = v.tensor_scalar(self.z[q][:, t, :], self.src[:, b, t, :],
                                      self.rstd[q][:, t:t + 1], float(D) ** 0.5, ALU.mult, ALU.mult)
        ins.then_inc(self.z_ready.sem, 1)

    def tensor(self, pe, b, q):
        pe.wait_ge(self.z_ready.sem, self.z_ready.done(b))
        pe.wait_ge(self.zF_ready.sem, self.zF_ready.freed(b))
        for t in range(T):
            ins = pe.transpose(self.pt[:, t * P:(t + 1) * P], self.z[q][:, t, :], self.ident[:, :])
        ins.then_inc(self.z_turned.sem, 1)

    def scalar(self, a, b, q):
        a.wait_ge(self.z_turned.sem, self.z_turned.done(b))
        if self.weight is None:
            a.activation(self.zF[q][:, :], self.pt[:, :], ACT.Copy).then_inc(self.zF_ready.sem, 1)
        else:
            a.activation(self.zF[q][:, :], self.pt[:, :], ACT.Copy, scale=self.weight)\
                .then_inc(self.zF_ready.sem, 1)


class Halves:

    def __init__(self, ctx, nc, name, shape):
        self.high, self.low = (ctx.enter_context(nc.sbuf_tensor(name + part, shape, F32R))
                               for part in ("_high", "_low"))


def matmul_halves(pe, out, left, right, start, stop):
    pairs = ((left[0], right[0]), (left[1], right[0]), (left[0], right[1]))
    for n, (a, b) in enumerate(pairs):
        ins = pe.matmul(out, a, b, start=(start and n == 0), stop=(stop and n == 2))
    return ins


def run_front_and_main(eng, front, main):
    front(0, 0)
    with eng.Fori(0, B // 2 - 1) as j:
        main(j * 2, 0, (j * 2 + 1, 1))
        main(j * 2 + 1, 1, (j * 2 + 2, 0))
    main(B - 2, 0, (B - 1, 1))
    main(B - 1, 1, None)


def credit(eng, stage):
    for c in stage.counts:
        if c.credit:
            eng.sem_inc(c.sem, c.credit)



X_FIRST = 2


def load_all(late, middle, early, nc, ap):
    res = {"holds": late.enter_context(nc.semaphore("holds"))}

    def sb(name, shape, ctx=late):
        res[name] = ctx.enter_context(nc.sbuf_tensor("r_" + name, shape, F32))
        return res[name]

    res["psum"] = late.enter_context(nc.psum_tensor("psum", [P, 8, N], F32))
    res["bank"] = [res["psum"][:, i, :] for i in range(8)]
    for n, shape in (("z", [P, T, D]), ("zF", [P, N]), ("st", [P, T, 6]), ("mv", [P, T, 2]),
                     ("ve", [P, T]), ("rstd", [P, T])):
        res["front_" + n] = [late.enter_context(nc.sbuf_tensor(f"front_{n}{q}", shape, F32))
                             for q in range(2)]
    X = sb("X", [P, B, T, D])
    ident = sb("ident", [P, P])
    nhalf = sb("nhalf", [P, T])
    eps_ln, eps_rms = sb("eps_layernorm", [P, T]), sb("eps_rms", [P, T])
    iota = sb("iota", [P, T, E])
    tri = sb("tri", [P, N])
    plan = []

    def weight(name, shape, src, ctx=late, plan=plan):
        dst = sb(name, shape, ctx)
        plan.append((dst[(slice(None),) * len(shape)], src))

    row = lambda a, n: a.rearrange("(a d) -> a d", a=1).broadcast_to([P, n])
    fold = lambda a: a.rearrange("(t p) m -> p t m", p=P)
    col = lambda a: a.rearrange("(a p) -> p a", p=P)
    weight("woT", [P, D], ap["woT"])
    for n in ("ln1_w", "ln2_w"):
        weight(n, [P, 1], col(ap[n]))
    for n in ("wqT", "wqrT", "wkT", "wkrT"):
        weight(n, [P, D], ap[n])
    weight("wvT", [P, 64], ap["wvT"])
    weight("cos", [P, N], ap["cos_table"])
    weight("sin", [P, N], ap["sin_table"])
    weight("L3_Wg", [P, E], ap["L3_router_wT"])
    HID = ap["L3_w1T"].shape[2]
    weight("L3_W1", [P, E, HID], ap["L3_w1T"])
    weight("L3_W3", [P, E, HID], ap["L3_w3T"])
    w2 = sb("L3_W2", [P, E, 3, D])
    for e in range(E):
        plan.append((w2[:, e, 0:2, :], ap["L3_w2T"][e, 0:256, :].rearrange("(c p) d -> p c d", p=P)))
        plan.append((w2[0:HID - 256, e, 2, :], ap["L3_w2T"][e, 256:HID, :]))
    adj_t = sb("adj_t", [P, T, N], middle)
    first = [(adj_t[:, :, :], fold(ap["adj_t"]))]
    for n in ("L3_gnn_Wg0", "L3_gnn_Wg1"):
        weight(n, [P, D], ap[n], middle)
    for n in ("L3_gnn_bg0", "L3_gnn_bg1"):
        weight("row_" + n, [P, D], row(ap[n], D), middle)
    weight("WihT", [P, 4, 4 * D], ap["WihT"], middle)
    weight("WhhT", [P, 4, 4 * D], ap["WhhT"], middle)
    weight("bih", [P, 4, 4], ap["bihc"], middle)
    weight("bhh", [P, 4, 4], ap["bhhc"], middle)
    adj_n = sb("adj_n", [P, T, N], early)
    plan.append((adj_n[:, :, :], fold(ap["adj"])))
    for n in ("L0_gnn_w1_loop", "L0_gnn_w1_neigh", "L0_gnn_w2_loop", "L0_gnn_w2_neigh"):
        weight(n, [P, D], ap[n], early, first)
    weight("L0_gnn_b1", [P, 1], col(ap["L0_gnn_b1"]), early, first)
    weight("row_L0_gnn_b2", [P, D], row(ap["L0_gnn_b2"], D), early, first)
    for n in ("L1_gnn_W", "L2_gnn_wT", "fc_in_wT"):
        weight(n, [P, D], ap[n], early)
    for n in ("L1_gnn_b_lin", "L2_gnn_d", "L2_gnn_fc_in_b", "fw_att", "bw_att"):
        weight(n, [P, 1], col(ap[n]), early)
    for n in ("L1_gnn_b_lin", "L1_gnn_b"):
        weight("row_" + n, [P, D], row(ap[n], D), early)
    weight("alpha", [P, T], ap["alpha"], early)
    weight("L0_Wg", [P, E], ap["L0_ffn_Wg"], early)
    for n in ("bg", "bias"):
        weight("L0_" + n, [P, E], row(ap["L0_ffn_" + n], E), early)
    weight("L0_W1", [P, E, 256], ap["L0_ffn_W1"].rearrange("e d h -> d e h"), early)
    weight("L0_b1", [P, E, 2], ap["L0_b1c"], early)
    weight("L0_W2", [P, E, 2, D], ap["L0_ffn_W2"].rearrange("e (c p) d -> p e c d", p=P), early)
    weight("L0_b2", [E, D], ap["L0_ffn_b2"], early)
    weight("L1_Wg", [P, E], ap["L1_router_wT"], early)
    weight("L1_W1", [P, E, D], ap["L1_ffn_w1"].rearrange("e d h -> d e h"), early)
    weight("L1_b1", [P, E, 1], ap["L1_b1c"], early)
    weight("L1_W2", [P, E, 1, D], ap["L1_ffn_w2"].rearrange("e (c p) d -> p e c d", p=P), early)
    weight("L1_b2", [E, D], ap["L1_ffn_b2"], early)
    weight("W_ihT", [P, 4 * D], ap["W_ihT"], early)
    weight("W_hhT", [P, 4 * D], ap["W_hhT"], early)
    weight("b_ih", [1, 4 * D], ap["L2_ffn_b_ih"].rearrange("(a d) -> a d", a=1), early)
    weight("b_hh", [1, 4 * D], ap["L2_ffn_b_hh"].rearrange("(a d) -> a d", a=1), early)
    weight("W_linT", [P, 2], ap["W_linT"], early)
    weight("b_lin", [P, 2], row(ap["L2_ffn_b_lin"], 2), early)

    x_in = ap["x"].rearrange("b (t p) d -> p b t d", p=P)
    with Stage(nc) as ctx, nc.Block() as block:
        x_loaded, w_loaded, const_set = ctx.sem("x_loaded"), ctx.sem("w_loaded"), ctx.sem("const_set")

        @block.sync
        def _(sp):
            for b in range(X_FIRST):
                sp.dma_start(X[:, b, :, :], x_in[:, b, :, :]).then_inc(x_loaded, 16)
            sp.wait_ge(x_loaded, 16 * X_FIRST)
            sp.wait_ge(w_loaded, 16 * len(first))

        @block.scalar
        def _(a):
            for dst, src in first:
                a.dma_start(dst, src).then_inc(w_loaded, 16)

        @block.gpsimd
        def _(g):
            g.memset(ident[:, :], 0.0).then_inc(const_set, 1)
            g.memset(tri[:, :], 0.0).then_inc(const_set, 1)
            g.memset(nhalf[:, :], -0.5)
            g.memset(eps_ln[:, :], EPS_LN)
            g.memset(eps_rms[:, :], EPS_RMS * D)
            g.iota(iota[:, :, :], [[0, T], [1, E]], base=0, channel_multiplier=0,
                   allow_small_or_imprecise_dtypes=True)
            g.wait_ge(const_set, 2)
            g.affine_select(out=ident[:, :], in_=ident[:, :], compare_op=ALU.not_equal, fill=1.0, base=0,
                            pattern=[[-1, P]], channel_multiplier=1)
            g.affine_select(out=tri[:, N - P:N], in_=tri[:, N - P:N], compare_op=ALU.is_ge, fill=-1e30,
                            base=0, pattern=[[-1, P]], channel_multiplier=1)

    def load_rest(sp, x_rest, w_rest):
        for b in range(X_FIRST, B):
            sp.dma_start(X[:, b, :, :], x_in[:, b, :, :]).then_inc(x_rest, 16)
        for dst, src in plan:
            sp.dma_start(dst, src).then_inc(w_rest, 16)
        sp.wait_ge(w_rest, 16 * len(plan))
        sp.wait_ge(x_rest, 16 * (B - X_FIRST))

    res["load_rest"] = load_rest
    return res



def graph_convolution(nc, res, adj_t, X):
    with Stage(nc) as ctx:
        bank = res["bank"]
        sb = lambda n, s: ctx.enter_context(nc.sbuf_tensor("g0_" + n, s, F32))
        c = lambda n, **k: Count(ctx, nc, "g0_" + n, **k)
        fr = Front(ctx, nc, res, X, bank[0])
        mixed, h1F, n2 = sb("mixed", [P, N]), sb("h1F", [P, N]), sb("n2", [P, T, D])
        out = [sb(f"out{i}", [P, T, D]) for i in range(2)]
        az_ready, az_copied = c("az_ready"), c("az_copied", credit=1)
        h1_ready, h1_copied = c("h1_ready", credit=1), c("h1_copied", credit=1)
        n2_ready, n2_copied = c("n2_ready"), c("n2_copied", credit=1)
        y_ready, y_read = c("y_ready", credit=1), c("y_read", credit=1)
        y_rectified, x_done = c("y_rectified"), c("x_done")
        w = lambda n: res["L0_gnn_" + n]
        AZ, H1, N2, Y = bank[1], bank[2], bank[3], [bank[4], bank[5]]
        x_rest, w_rest = ctx.sem("x_rest"), ctx.sem("w_rest")

        with nc.Block() as block:
            @block.sync
            def _(sp):
                res["load_rest"](sp, x_rest, w_rest)

            @block.tensor
            def _(pe):
                def front(b, q):
                    pe.wait_ge(fr.z_ready.sem, fr.z_ready.done(b))
                    pe.wait_ge(az_copied.sem, az_copied.freed(b))
                    for m in range(T):
                        ins = pe.matmul(AZ[:, :], fr.z[q][:, m, :], adj_t[:, m, :],
                                        start=(m == 0), stop=(m == T - 1))
                    ins.then_inc(az_ready.sem, 1)
                    fr.tensor(pe, b, q)

                def main(b, q, nxt):
                    pe.wait_ge(fr.zF_ready.sem, fr.zF_ready.done(b))
                    pe.wait_ge(h1_copied.sem, h1_copied.freed(b))
                    pe.matmul(H1[:, :], w("w1_loop")[:, :], fr.zF[q][:, :], start=True, stop=False)
                    pe.wait_ge(az_copied.sem, az_copied.done(b))
                    pe.matmul(H1[:, :], w("w1_neigh")[:, :], mixed[:, :], start=False, stop=True)\
                        .then_inc(h1_ready.sem, 1)
                    pe.wait_ge(h1_copied.sem, h1_copied.done(b))
                    pe.wait_ge(n2_copied.sem, n2_copied.freed(b))
                    for t in range(T):
                        ins = pe.matmul(N2[:, t * P:(t + 1) * P], h1F[:, t * P:(t + 1) * P],
                                        w("w2_neigh")[:, :], start=True, stop=True)
                    ins.then_inc(n2_ready.sem, 1)
                    if nxt:
                        front(*nxt)
                    pe.wait_ge(n2_copied.sem, n2_copied.done(b))
                    pe.wait_ge(y_read.sem, y_read.freed(b))
                    for t in range(T):
                        o = Y[q][:, t * P:(t + 1) * P]
                        pe.matmul(o, h1F[:, t * P:(t + 1) * P], w("w2_loop")[:, :], start=True, stop=False)
                        for m in range(T):
                            ins = pe.matmul(o, adj_t[:, m, t * P:(t + 1) * P], n2[:, m, :],
                                            start=False, stop=(m == T - 1))
                    ins.then_inc(y_ready.sem, 1)
                run_front_and_main(pe, front, main)

            @block.scalar
            def _(a):
                def front(b, q):
                    a.wait_ge(az_ready.sem, az_ready.done(b))
                    a.wait_ge(h1_ready.sem, h1_ready.freed(b))
                    a.activation(mixed[:, :], AZ[:, :], ACT.Copy).then_inc(az_copied.sem, 1)
                    fr.scalar(a, b, q)

                def main(b, q, nxt):
                    a.wait_ge(h1_ready.sem, h1_ready.done(b))
                    a.wait_ge(y_ready.sem, y_ready.freed(b))
                    a.activation(h1F[:, :], H1[:, :], ACT.Relu, bias=w("b1")[:, 0:1])\
                        .then_inc(h1_copied.sem, 1)
                    a.wait_ge(n2_ready.sem, n2_ready.done(b))
                    a.activation(n2[:, :, :], N2[:, :].rearrange("p (t d) -> p t d", t=T), ACT.Copy)\
                        .then_inc(n2_copied.sem, 1)
                    if nxt:
                        front(*nxt)
                run_front_and_main(a, front, main)

            @block.vector
            def _(v):
                def front(b, q):
                    for k in range(2):
                        fr.vector_stats(v, k, k)
                        fr.vector_apply(v, k, k)
                    v.wait_ge(x_rest, 16 * (B - X_FIRST))

                def main(b, q, nxt):
                    follows = not isinstance(b, int)
                    if follows:
                        fr.vector_stats(v, b + 2, q)
                    v.wait_ge(y_ready.sem, y_ready.done(b))
                    bias = res["row_L0_gnn_b2"][:, :]\
                        .unsqueeze(1).broadcast_to([P, T, D])
                    v.tensor_tensor(out[q][:, :, :], Y[q][:, :].rearrange("p (t d) -> p t d", t=T), bias,
                                    ALU.add).then_inc(y_read.sem, 1)
                    v.wait_ge(y_read.sem, y_read.done(b))
                    v.scalar_tensor_tensor(out=out[q][:, :, :], in0=out[q][:, :, :], scalar=0.0,
                                           in1=fr.z[q][:, :, :], op0=ALU.max, op1=ALU.add)\
                        .then_inc(y_rectified.sem, 1)
                    v.wait_ge(y_rectified.sem, y_rectified.done(b))
                    if follows:
                        fr.vector_apply(v, b + 2, q)
                    v.scalar_tensor_tensor(out=X[:, b, :, :], in0=out[q][:, :, :], scalar=0.5,
                                           in1=X[:, b, :, :], op0=ALU.mult, op1=ALU.add)\
                        .then_inc(x_done.sem, 1)
                run_front_and_main(v, front, main)

            @block.gpsimd
            def _(g):
                credit(g, ctx)

                def front(b, q):
                    fr.gpsimd(g, 0, 0)
                    fr.gpsimd(g, 1, 1)

                def main(b, q, nxt):
                    if not isinstance(b, int):
                        fr.gpsimd(g, b + 2, q)
                run_front_and_main(g, front, main)



class Router:

    def __init__(self, ctx, nc, res, tag, bank, w_gate, bias, rule, guard):
        sb = lambda n, s, dt=F32: ctx.enter_context(nc.sbuf_tensor(tag + n, s, dt))
        c = lambda n, **k: Count(ctx, nc, tag + n, **k)
        self.bank, self.w, self.bias, self.rule, self.guard = bank, w_gate, bias, rule, guard
        self.res, self.iota, self.ident = res, res["iota"], res["ident"]
        self.lg, self.sub, self.ex = sb("lg", [P, T, E]), sb("sub", [P, T, E]), sb("ex", [P, T, E])
        self.probs, self.top = sb("probs", [P, T, E]), sb("top", [P, T, E])
        self.idx, self.idxf = sb("idx", [P, T, E], U32), sb("idxf", [P, T, E])
        self.s1, self.s2, self.w2 = sb("s1", [P, T]), sb("s2", [P, T]), sb("w2", [P, T, 2])
        self.hot = sb("hot", [P, T, 2, E])
        self.c = [sb(f"c{i}", [P, T, E]) for i in range(2)]
        self.cF = [sb(f"cF{i}", [E, N]) for i in range(2)]
        self.lg_ready, self.lg_read = c("lg_ready"), c("lg_read")
        self.sub_ready, self.ex_ready, self.c_ready = c("sub_ready"), c("ex_ready"), c("c_ready")
        self.c_turned, self.cF_ready = c("c_turned"), c("cF_ready")
        self.chain = Chain(ctx, nc, tag + "route_chain",
                           (11 if rule == "probs" else 8) + (bias is not None))

    def tensor_logits(self, pe, fr, b, q):
        pe.wait_ge(fr.zF_ready.sem, fr.zF_ready.done(b))
        for t in range(T):
            ins = pe.matmul(self.bank[:, t * E:(t + 1) * E], fr.zF[q][:, t * P:(t + 1) * P],
                            self.w[:, :], start=True, stop=True)
        ins.then_inc(self.lg_ready.sem, 1)

    def tensor_turn(self, pe, b, q):
        pe.wait_ge(self.c_ready.sem, self.c_ready.done(b))
        for t in range(T):
            ins = pe.transpose(self.bank[0:E, t * P:(t + 1) * P], self.c[q][:, t, :], self.ident[:, :])
        ins.then_inc(self.c_turned.sem, 1)

    def scalar_exp(self, a, b, q):
        a.wait_ge(self.sub_ready.sem, self.sub_ready.done(b))
        k = E if self.rule == "probs" else 2
        a.activation(self.ex[:, :, 0:k], self.sub[:, :, 0:k], ACT.Exp).then_inc(self.ex_ready.sem, 1)

    def scalar_cF(self, a, b, q):
        a.wait_ge(self.c_turned.sem, self.c_turned.done(b))
        a.activation(self.cF[q][:, :], self.bank[0:E, :], ACT.Copy).then_inc(self.cF_ready.sem, 1)

    def vector_before_exp(self, v, b, q):
        ch = self.chain
        ch.begin(b)
        v.wait_ge(self.lg_ready.sem, self.lg_ready.done(b))
        lg = self.bank[:, 0:T * E].rearrange("p (t e) -> p t e", t=T)
        if self.bias is None:
            ch.link(v, v.tensor_copy(self.lg[:, :, :], lg))
        else:
            ch.link(v, v.tensor_tensor(self.lg[:, :, :], lg,
                                       self.bias[0][:, :].unsqueeze(1).broadcast_to([P, T, E]), ALU.add))
            ch.link(v, v.tensor_tensor(self.lg[:, :, :], self.lg[:, :, :],
                                       self.bias[1][:, :].unsqueeze(1).broadcast_to([P, T, E]), ALU.add))
        hold(v, self.res)
        for t in range(T):
            ins = v.max(self.top[:, t, :], self.lg[:, t, :])
        ch.link(v, ins)
        k = E if self.rule == "probs" else 2
        src = self.lg if self.rule == "probs" else self.top
        v.tensor_tensor(self.sub[:, :, 0:k], src[:, :, 0:k],
                        self.top[:, :, 0:1].broadcast_to([P, T, k]), ALU.subtract)\
            .then_inc(self.sub_ready.sem, 1)

    def vector_sum(self, v, b, q):
        ch = self.chain
        v.wait_ge(self.ex_ready.sem, self.ex_ready.done(b))
        k = E if self.rule == "probs" else 2
        ch.link(v, v.tensor_reduce(self.s1[:, :], self.ex[:, :, 0:k], AX, ALU.add))
        ch.link(v, v.reciprocal(self.s2[:, :], self.s1[:, :]))

    def vector_best(self, v, b, q):
        ch = self.chain
        r = self.s2[:, :].unsqueeze(2)
        if self.rule == "probs":
            ch.link(v, v.tensor_tensor(self.probs[:, :, :], self.ex[:, :, :],
                                       r.broadcast_to([P, T, E]), ALU.mult))
            hold(v, self.res)
            for t in range(T):
                ins = v.max(self.top[:, t, :], self.probs[:, t, :])
            ch.link(v, ins)
            v.tensor_tensor(self.s1[:, :], self.top[:, :, 0], self.top[:, :, 1], ALU.add)
            for t in range(T):
                ins = v.max_index(self.idx[:, t, :], self.top[:, t, :], self.probs[:, t, :])
            ch.link(v, ins)
            op, number = self.guard
            v.tensor_copy(self.idxf[:, :, :], self.idx[:, :, :])
            ch.link(v, v.tensor_scalar(self.s1[:, :], self.s1[:, :], number, None, op))
            ch.link(v, v.reciprocal(self.s2[:, :], self.s1[:, :]))
            v.tensor_tensor(self.w2[:, :, :], self.top[:, :, 0:2], r.broadcast_to([P, T, 2]), ALU.mult)
        else:
            hold(v, self.res)
            for t in range(T):
                ins = v.max_index(self.idx[:, t, :], self.top[:, t, :], self.lg[:, t, :])
            ch.link(v, v.tensor_tensor(self.w2[:, :, :], self.ex[:, :, 0:2],
                                       r.broadcast_to([P, T, 2]), ALU.mult))
            ch.link(v, v.tensor_copy(self.idxf[:, :, :], self.idx[:, :, :]))

    def vector_combine(self, v, b, q):
        ch = self.chain
        for j in range(2):
            ins = v.tensor_tensor(self.hot[:, :, j, :], self.iota[:, :, :],
                                  self.idxf[:, :, j:j + 1].broadcast_to([P, T, E]), ALU.is_equal)
        ch.link(v, ins)
        for j in range(2):
            ins = v.tensor_tensor(self.hot[:, :, j, :], self.hot[:, :, j, :],
                                  self.w2[:, :, j:j + 1].broadcast_to([P, T, E]), ALU.mult)
        ch.link(v, ins)
        v.tensor_tensor(self.c[q][:, :, :], self.hot[:, :, 0, :], self.hot[:, :, 1, :], ALU.add)\
            .then_inc(self.c_ready.sem, 1)
        ch.end()


SCHEDULE = {1: (0, 1, 2, 3, 3, 4, 5, 6),
            2: (1, 3, 4, 5, 5, 5, 5, 6),
            3: (1, 3, 4, 5, 5, 6, 7, None)}


def mixture(nc, res, X, tag, w, hidden, act, rule, guard, router_bias, biases, adds_z,
            src=None, kind="layernorm", weight=None, halves=True, x_out=None):
    src = X if src is None else src
    C = len(hidden)
    gated = "W3" in w
    NC = E * C
    HR = 6 if gated else 2 * C
    with Stage(nc) as ctx:
        bank = res["bank"]
        sb = lambda n, s: ctx.enter_context(nc.sbuf_tensor(tag + n, s, F32))
        c = lambda n, **k: Count(ctx, nc, tag + n, **k)
        fr = Front(ctx, nc, res, src, bank[0], kind=kind, weight=weight, tag=tag)
        ro = Router(ctx, nc, res, tag, bank[1], w["Wg"], router_bias, rule, guard)
        H, Y = bank[2:6], bank[6:8]
        HS = 2 if gated else 4
        hF = [sb(f"hF{i}", [P, N]) for i in range(HR)]
        gate = [sb(f"gate{i}", [P, N]) for i in range(2)] if gated else None
        acc = sb("acc", [P, T, D])
        ups = [n for n in ("W1", "W3") if n in w]
        APPLY_AT, Z_AT, LOGITS_AT, EXP_AT, SUM_AT, BEST_AT, COMBINE_AT, TURN_AT = SCHEDULE[C]
        if halves:
            zs = [Halves(ctx, nc, f"{tag}z{i}", [P, N]) for i in range(2)]
            ws = {n: Halves(ctx, nc, tag + n, [P, E, sum(hidden)]) for n in ups}
            w_high, w_low = ctx.sem(tag + "w_high"), ctx.sem(tag + "w_low")
            z_high, z_low = c("z_high"), c("z_low")
        h_ready = c("h_ready", per=NC)
        gate_ready = c("gate_ready", per=NC) if gated else None
        hF_ready = c("hF_ready", per=NC, credit=HS)
        y_ready = c("y_ready", per=E, credit=2)
        y_added = c("y_added", per=E, credit=2)
        bias_ready = c("bias_ready")
        acc_set = c("acc_set")
        if adds_z:
            xz, xz_ready = sb("xz", [P, T, D]), c("xz_ready")
        out_written = ctx.sem("out_written") if x_out is not None else None

        with nc.Block() as block:
            if x_out is not None:
                @block.sync
                def _(sp):
                    def store(b):
                        sp.wait_ge(y_added.sem, y_added.done(b))
                        sp.dma_start(x_out[:, b, :, :], X[:, b, :, :]).then_inc(out_written, 16)
                    with sp.Fori(0, B) as b:
                        store(b)
                    sp.wait_ge(out_written, 16 * B)

            @block.tensor
            def _(pe):
                def up(b, q, e, chunks=range(C)):
                    if e == 0 and chunks[0] == 0:
                        pe.wait_ge(fr.zF_ready.sem, fr.zF_ready.done(b))
                        if halves:
                            pe.wait_ge(z_high.sem, z_high.done(b))
                            pe.wait_ge(z_low.sem, z_low.done(b))
                    for j in chunks:
                        n, size = e * C + j, hidden[j]
                        pe.wait_ge(hF_ready.sem, hF_ready.freed(b, n + 1))
                        cols = slice(j * P, j * P + size)
                        for i, name in enumerate(ups):
                            o = H[n % HS * len(ups) + i][0:size, :]
                            if halves:
                                ins = matmul_halves(pe, o, (ws[name].high[:, e, cols],
                                                            ws[name].low[:, e, cols]),
                                                    (zs[q].high[:, :], zs[q].low[:, :]), True, True)
                            else:
                                ins = pe.matmul(o, w[name][:, e, cols], fr.zF[q][:, :],
                                                start=True, stop=True)
                        ins.then_inc(h_ready.sem, 1)

                def down(b, q, e, tiles=range(T)):
                    pe.wait_ge(hF_ready.sem, hF_ready.done(b, e * C + C))
                    pe.wait_ge(y_added.sem, y_added.freed(b, e + 1))
                    for t in tiles:
                        for j, size in enumerate(hidden):
                            ins = pe.matmul(Y[e % 2][:, t * P:(t + 1) * P],
                                            hF[e % 2 * C + j][0:size, t * P:(t + 1) * P],
                                            w["W2"][0:size, e, j, :], start=(j == 0), stop=(j == C - 1))
                    if tiles[-1] == T - 1:
                        ins.then_inc(y_ready.sem, 1)

                def bias(b, q):
                    pe.wait_ge(ro.cF_ready.sem, ro.cF_ready.done(b))
                    for t in range(T):
                        ins = pe.matmul(ro.bank[:, t * P:(t + 1) * P], ro.cF[q][:, t * P:(t + 1) * P],
                                        w["b2"][:, :], start=True, stop=True)
                    ins.then_inc(bias_ready.sem, 1)

                def front(b, q):
                    fr.tensor(pe, b, q)
                    ro.tensor_logits(pe, fr, b, q)
                    if biases:
                        ro.tensor_turn(pe, b, q)
                    if halves:
                        pe.wait_ge(w_high, len(ups))
                        pe.wait_ge(w_low, len(ups))
                    up(b, q, 0)

                def main(b, q, nxt):
                    for e in range(E):
                        ahead = (b, q, e + 1) if e + 1 < E else (*nxt, 0) if nxt else None
                        if gated and ahead:
                            up(*ahead, range(C - 1))
                            down(b, q, e, range(T // 2))
                            up(*ahead, range(C - 1, C))
                            down(b, q, e, range(T // 2, T))
                        else:
                            if ahead:
                                up(*ahead)
                            if e == 0 and biases:
                                bias(b, q)
                            down(b, q, e)
                        if nxt and e == Z_AT:
                            fr.tensor(pe, *nxt)
                        if nxt and e == LOGITS_AT:
                            pe.wait_ge(acc_set.sem, acc_set.done(b))
                            ro.tensor_logits(pe, fr, *nxt)
                        if nxt and e == TURN_AT:
                            ro.tensor_turn(pe, *nxt)
                run_front_and_main(pe, front, main)

            @block.scalar
            def _(a):
                def hidden_chunks(b, q, e):
                    for j, size in enumerate(hidden):
                        n = e * C + j
                        a.wait_ge(h_ready.sem, h_ready.done(b, n + 1))
                        if gated:
                            a.wait_ge(hF_ready.sem, hF_ready.freed(b, n + 1))
                            a.activation(gate[n % 2][0:size, :], H[n % HS * 2][0:size, :], act)\
                                .then_inc(gate_ready.sem, 1)
                        else:
                            if j == 0:
                                a.wait_ge(y_ready.sem, y_ready.freed(b, e + 1))
                            a.activation(hF[n % HR][0:size, :], H[n % HS][0:size, :], act,
                                         bias=w["b1"][0:size, e, j:j + 1]).then_inc(hF_ready.sem, 1)

                def split(b, q):
                    if halves:
                        a.wait_ge(fr.zF_ready.sem, fr.zF_ready.done(b))
                        a.activation(zs[q].high[:, :], fr.zF[q][:, :], ACT.Copy).then_inc(z_high.sem, 1)

                def front(b, q):
                    if halves:
                        for n in ups:
                            a.activation(ws[n].high[:, :, :], w[n][:, :, :], ACT.Copy).then_inc(w_high, 1)
                    fr.scalar(a, b, q)
                    split(b, q)
                    ro.scalar_exp(a, b, q)
                    if biases:
                        ro.scalar_cF(a, b, q)
                    hidden_chunks(b, q, 0)

                def main(b, q, nxt):
                    for e in range(E):
                        if e + 1 < E:
                            hidden_chunks(b, q, e + 1)
                        elif nxt:
                            hidden_chunks(*nxt, 0)
                        if nxt and e == Z_AT:
                            fr.scalar(a, *nxt)
                            split(*nxt)
                        if nxt and e == EXP_AT:
                            ro.scalar_exp(a, *nxt)
                        if nxt and e == TURN_AT:
                            ro.scalar_cF(a, *nxt)
                run_front_and_main(a, front, main)

            @block.vector
            def _(v):
                def products(b, q, e):
                    for j, size in enumerate(hidden):
                        n = e * C + j
                        v.wait_ge(gate_ready.sem, gate_ready.done(b, n + 1))
                        if j == 0:
                            v.wait_ge(y_ready.sem, y_ready.freed(b, e + 1))
                        v.tensor_tensor(hF[n % HR][0:size, :], H[n % HS * 2 + 1][0:size, :],
                                        gate[n % 2][0:size, :], ALU.mult).then_inc(hF_ready.sem, 1)

                def split(b, q):
                    if halves:
                        v.wait_ge(z_high.sem, z_high.done(b))
                        v.tensor_tensor(zs[q].low[:, :], fr.zF[q][:, :], zs[q].high[:, :], ALU.subtract)\
                            .then_inc(z_low.sem, 1)

                def front(b, q):
                    fr.vector_stats(v, b, q)
                    fr.vector_apply(v, b, q)
                    ro.vector_before_exp(v, b, q)
                    ro.vector_sum(v, b, q)
                    ro.vector_best(v, b, q)
                    ro.vector_combine(v, b, q)
                    fr.vector_stats(v, 1, 1)
                    split(b, q)
                    if halves:
                        for i, n in enumerate(ups):
                            v.wait_ge(w_high, i + 1)
                            v.tensor_tensor(ws[n].low[:, :, :], w[n][:, :, :], ws[n].high[:, :, :],
                                            ALU.subtract).then_inc(w_low, 1)
                    if gated:
                        products(b, q, 0)

                def main(b, q, nxt):
                    follows = not isinstance(b, int)
                    v.wait_ge(y_added.sem, y_added.done(b, 0))
                    if biases:
                        v.wait_ge(bias_ready.sem, bias_ready.done(b))
                        if adds_z:
                            v.wait_ge(xz_ready.sem, xz_ready.done(b))
                        v.tensor_tensor(acc[:, :, :], ro.bank[:, :].rearrange("p (t d) -> p t d", t=T),
                                        xz[:, :, :] if adds_z else X[:, b, :, :], ALU.add)\
                            .then_inc(acc_set.sem, 1)
                    else:
                        v.tensor_copy(acc[:, :, :], X[:, b, :, :]).then_inc(acc_set.sem, 1)
                    for e in range(E):
                        if gated:
                            if e + 1 < E:
                                products(b, q, e + 1)
                            elif nxt:
                                products(*nxt, 0)
                        v.wait_ge(y_ready.sem, y_ready.done(b, e + 1))
                        if e == 0:
                            v.wait_ge(acc_set.sem, acc_set.done(b))
                        else:
                            v.wait_ge(y_added.sem, y_added.done(b, e))
                        for t in range(T):
                            dst = acc[:, t, :] if e < E - 1 else X[:, b, t, :]
                            ins = v.scalar_tensor_tensor(out=dst, in0=Y[e % 2][:, t * P:(t + 1) * P],
                                                         scalar=ro.c[q][:, t, e:e + 1], in1=acc[:, t, :],
                                                         op0=ALU.mult, op1=ALU.add)
                        ins.then_inc(y_added.sem, 1)
                        if nxt and e == APPLY_AT:
                            fr.vector_apply(v, *nxt)
                        if follows and e == APPLY_AT + 1:
                            fr.vector_stats(v, b + 2, q)
                        if nxt and e == LOGITS_AT:
                            split(*nxt)
                            ro.vector_before_exp(v, *nxt)
                        if nxt and e == SUM_AT:
                            ro.vector_sum(v, *nxt)
                        if nxt and e == BEST_AT:
                            ro.vector_best(v, *nxt)
                        if nxt and e == COMBINE_AT:
                            ro.vector_combine(v, *nxt)
                run_front_and_main(v, front, main)

            @block.gpsimd
            def _(g):
                credit(g, ctx)

                def add_z(b, q):
                    if adds_z:
                        g.wait_ge(fr.z_ready.sem, fr.z_ready.done(b))
                        g.tensor_tensor(xz[:, :, :], X[:, b, :, :], fr.z[q][:, :, :], ALU.add)\
                            .then_inc(xz_ready.sem, 1)

                def front(b, q):
                    fr.gpsimd(g, 0, 0)
                    add_z(0, 0)
                    fr.gpsimd(g, 1, 1)

                def main(b, q, nxt):
                    if nxt and adds_z:
                        g.wait_ge(acc_set.sem, acc_set.done(b))
                        add_z(*nxt)
                    if not isinstance(b, int):
                        fr.gpsimd(g, b + 2, q)
                run_front_and_main(g, front, main)



def graph_attention(nc, res, X):
    NEG = -1e16
    with Stage(nc) as ctx:
        bank = res["bank"]
        sb = lambda n, s: ctx.enter_context(nc.sbuf_tensor("g1_" + n, s, F32))
        c = lambda n, **k: Count(ctx, nc, "g1_" + n, **k)
        fr = Front(ctx, nc, res, X, bank[0], tag="g1_")
        HB, S, PT, O = bank[1], bank[2:4], bank[4:6], bank[6]
        SR = 2
        hF = [sb(f"hF{i}", [P, N]) for i in range(2)]
        hT = [sb(f"hT{i}", [P, T, D]) for i in range(2)]
        prod = [sb(f"prod{i}", [P, N]) for i in range(SR)]
        fill = [sb(f"fill{i}", [P, N]) for i in range(SR)]
        prob = [sb(f"prob{i}", [P, N]) for i in range(SR)]
        probT = [sb(f"probT{i}", [P, T, P]) for i in range(SR)]
        top = [sb(f"top{i}", [P, T]) for i in range(2)]
        ntop = [sb(f"ntop{i}", [P, T]) for i in range(2)]
        total = [sb(f"total{i}", [P, T]) for i in range(2)]
        rtotal = [sb(f"rtotal{i}", [P, T]) for i in range(2)]
        out = sb("out", [P, T, D])
        bias = res["row_L1_gnn_b"]
        h_ready, hF_copied = c("h_ready"), c("hF_copied")
        hT_ready, hT_copied = c("hT_ready"), c("hT_copied", credit=1)
        s_ready = c("s_ready", per=T)
        prod_ready = c("prod_ready", per=T, credit=2)
        fill_ready = c("fill_ready", per=T)
        masked = c("masked", per=T)
        ntop_ready = c("ntop_ready", per=T)
        prob_ready = c("prob_ready", per=T, credit=SR)
        turned = c("turned", per=T, credit=SR)
        probT_ready = c("probT_ready", per=T, credit=2)
        o_ready = c("o_ready", per=T, credit=SR)
        r_ready, scaled, x_done = c("r_ready"), c("scaled", credit=1), c("x_done", credit=1)

        with nc.Block() as block:
            @block.tensor
            def _(pe):
                def project(b, q):
                    pe.wait_ge(fr.zF_ready.sem, fr.zF_ready.done(b))
                    pe.wait_ge(hT_copied.sem, hT_copied.freed(b))
                    pe.matmul(HB[:, :], res["L1_gnn_W"][:, :], fr.zF[q][:, :], start=True, stop=True)\
                        .then_inc(h_ready.sem, 1)
                    pe.wait_ge(hF_copied.sem, hF_copied.done(b))
                    for t in range(T):
                        ins = pe.matmul(HB[:, t * P:(t + 1) * P], fr.zF[q][:, t * P:(t + 1) * P],
                                        res["L1_gnn_W"][:, :], start=True, stop=True)
                    ins.then_inc(hT_ready.sem, 1)

                def scores(b, q, t):
                    pe.wait_ge(hF_copied.sem, hF_copied.done(b))
                    pe.wait_ge(prod_ready.sem, prod_ready.freed(b, t + 1))
                    pe.matmul(S[t % 2][:, :], hF[q][:, t * P:(t + 1) * P], hF[q][:, :],
                              start=True, stop=True).then_inc(s_ready.sem, 1)

                def turn(b, q, t):
                    pe.wait_ge(prob_ready.sem, prob_ready.done(b, t + 1))
                    pe.wait_ge(probT_ready.sem, probT_ready.freed(b, t + 1))
                    for m in range(T):
                        ins = pe.transpose(PT[t % 2][:, m * P:(m + 1) * P],
                                           prob[t % SR][:, m * P:(m + 1) * P], res["ident"][:, :])
                    ins.then_inc(turned.sem, 1)

                def attend(b, q, t):
                    if t == 0:
                        pe.wait_ge(hT_copied.sem, hT_copied.done(b))
                        pe.wait_ge(scaled.sem, scaled.freed(b))
                    pe.wait_ge(probT_ready.sem, probT_ready.done(b, t + 1))
                    for m in range(T):
                        ins = pe.matmul(O[:, t * P:(t + 1) * P], probT[t % SR][:, m, :], hT[q][:, m, :],
                                        start=(m == 0), stop=(m == T - 1))
                    ins.then_inc(o_ready.sem, 1)

                def front(b, q):
                    fr.tensor(pe, b, q)
                    project(b, q)
                    scores(b, q, 0)
                    scores(b, q, 1)

                def main(b, q, nxt):
                    scores(b, q, 2)
                    scores(b, q, 3)
                    turn(b, q, 0)
                    turn(b, q, 1)
                    attend(b, q, 0)
                    if nxt:
                        fr.tensor(pe, *nxt)
                    attend(b, q, 1)
                    if nxt:
                        project(*nxt)
                    turn(b, q, 2)
                    turn(b, q, 3)
                    if nxt:
                        scores(*nxt, 0)
                        scores(*nxt, 1)
                    attend(b, q, 2)
                    attend(b, q, 3)
                run_front_and_main(pe, front, main)

            @block.scalar
            def _(a):
                def project(b, q):
                    a.wait_ge(h_ready.sem, h_ready.done(b))
                    a.activation(hF[q][:, :], HB[:, :], ACT.Identity, bias=res["L1_gnn_b_lin"][:, 0:1])\
                        .then_inc(hF_copied.sem, 1)

                def exp(b, q, t):
                    a.wait_ge(ntop_ready.sem, ntop_ready.done(b, t + 1))
                    a.wait_ge(turned.sem, turned.freed(b, t + 1))
                    a.activation(prob[t % SR][:, :], prod[t % SR][:, :], ACT.Exp,
                                 bias=ntop[q][:, t:t + 1], accum_out=total[q][:, t:t + 1])\
                        .then_inc(prob_ready.sem, 1)

                def copy(b, q, t):
                    a.wait_ge(turned.sem, turned.done(b, t + 1))
                    a.wait_ge(o_ready.sem, o_ready.freed(b, t + 1))
                    a.activation(probT[t % SR][:, :, :], PT[t % 2][:, :].rearrange("p (m n) -> p m n", m=T),
                                 ACT.Copy).then_inc(probT_ready.sem, 1)

                def front(b, q):
                    fr.scalar(a, b, q)
                    project(b, q)

                def main(b, q, nxt):
                    exp(b, q, 0)
                    exp(b, q, 1)
                    copy(b, q, 0)
                    copy(b, q, 1)
                    if nxt:
                        fr.scalar(a, *nxt)
                        project(*nxt)
                    exp(b, q, 2)
                    exp(b, q, 3)
                    copy(b, q, 2)
                    copy(b, q, 3)
                run_front_and_main(a, front, main)

            @block.vector
            def _(v):
                def mask(b, q, t):
                    v.wait_ge(s_ready.sem, s_ready.done(b, t + 1))
                    v.wait_ge(prob_ready.sem, prob_ready.freed(b, t + 1))
                    v.tensor_tensor(prod[t % SR][:, :], S[t % 2][:, :], res["adj_n"][:, t, :], ALU.mult)\
                        .then_inc(prod_ready.sem, 1)

                def peaks(b, q, two):
                    for t in two:
                        v.wait_ge(prod_ready.sem, prod_ready.done(b, t + 1))
                        v.tensor_scalar(fill[t % SR][:, :], prod[t % SR][:, :], 0.0, NEG,
                                        ALU.is_equal, ALU.mult).then_inc(fill_ready.sem, 1)
                    for t in two:
                        v.wait_ge(fill_ready.sem, fill_ready.done(b, t + 1))
                        hold(v, res)
                        v.tensor_tensor_reduce(prod[t % SR][:, :], prod[t % SR][:, :],
                                               fill[t % SR][:, :], 1.0, -3e38, ALU.add, ALU.max,
                                               top[q][:, t:t + 1]).then_inc(masked.sem, 1)
                    for t in two:
                        v.wait_ge(masked.sem, masked.done(b, t + 1))
                        v.tensor_scalar(ntop[q][:, t:t + 1], top[q][:, t:t + 1], -1.0, None, ALU.mult)\
                            .then_inc(ntop_ready.sem, 1)

                def front(b, q):
                    fr.vector_stats(v, b, q)
                    fr.vector_apply(v, b, q)
                    bias_h(b, q)
                    mask(b, q, 0)
                    mask(b, q, 1)
                    peaks(b, q, (0, 1))
                    fr.vector_stats(v, 1, 1)

                def bias_h(b, q):
                    v.wait_ge(hT_ready.sem, hT_ready.done(b))
                    v.tensor_tensor(hT[q][:, :, :], HB[:, :].rearrange("p (t d) -> p t d", t=T),
                                    res["row_L1_gnn_b_lin"][:, :].unsqueeze(1).broadcast_to([P, T, D]),
                                    ALU.add).then_inc(hT_copied.sem, 1)

                def main(b, q, nxt):
                    if nxt:
                        fr.vector_apply(v, *nxt)
                    mask(b, q, 2)
                    mask(b, q, 3)
                    peaks(b, q, (2, 3))
                    if nxt:
                        bias_h(*nxt)
                        mask(*nxt, 0)
                        mask(*nxt, 1)
                        peaks(*nxt, (0, 1))
                    if not isinstance(b, int):
                        fr.vector_stats(v, b + 2, q)
                    v.wait_ge(o_ready.sem, o_ready.done(b, T))
                    v.reciprocal(rtotal[q][:, :], total[q][:, :]).then_inc(r_ready.sem, 1)
                    v.wait_ge(r_ready.sem, r_ready.done(b))
                    v.wait_ge(x_done.sem, x_done.freed(b))
                    for t in range(T):
                        ins = v.scalar_tensor_tensor(out=out[:, t, :], in0=O[:, t * P:(t + 1) * P],
                                                     scalar=rtotal[q][:, t:t + 1], in1=bias[:, :],
                                                     op0=ALU.mult, op1=ALU.add)
                    ins.then_inc(scaled.sem, 1)
                    v.wait_ge(scaled.sem, scaled.done(b))
                    v.tensor_tensor(X[:, b, :, :], X[:, b, :, :], out[:, :, :], ALU.add)\
                        .then_inc(x_done.sem, 1)
                run_front_and_main(v, front, main)

            @block.gpsimd
            def _(g):
                credit(g, ctx)

                def main(b, q, nxt):
                    if nxt:
                        fr.gpsimd(g, *nxt)
                run_front_and_main(g, lambda b, q: fr.gpsimd(g, b, q), main)



STEPS = 8


def run_pairs(eng, front, main):
    front(0)
    with eng.Fori(0, B // 2 - 1) as j:
        main(j, j + 1)
    main(B // 2 - 1, None)


def diffusion(nc, res, X):
    DT = 1.0 / STEPS
    with Stage(nc) as ctx:
        bank = res["bank"]
        sb = lambda n, s: ctx.enter_context(nc.sbuf_tensor("g2_" + n, s, F32))
        c = lambda n, **k: Count(ctx, nc, "g2_" + n, **k)
        fr = Front(ctx, nc, res, X, bank[0], tag="g2_")
        FC, R, TB = bank[1], bank[2:4], bank[4:6]
        sig, s_alpha, diag = sb("sig", [P, T]), sb("s_alpha", [P, T]), sb("diag", [P, T])
        A_n, A_t = sb("A_n", [P, T, N]), Halves(ctx, nc, "g2_A_t", [P, T, N])
        dclip, wd, W = sb("dclip", [P, 1]), sb("wd", [P, D]), Halves(ctx, nc, "g2_W", [P, D])
        hF = [sb(f"hF{q}", [P, N]) for q in range(2)]
        hF_parts = [Halves(ctx, nc, f"g2_hF{q}", [P, N]) for q in range(2)]
        hT_parts = [Halves(ctx, nc, f"g2_hT{q}", [P, T, D]) for q in range(2)]
        dz = [sb(f"dz{q}", [P, N]) for q in range(2)]
        chain = ctx.sem("g2_set_up")
        w_ready, a_turned, a_copied = (ctx.sem("g2_" + n) for n in ("w_ready", "a_turned", "a_copied"))
        two = lambda n, **k: [c(f"{n}{q}", **k) for q in range(2)]
        fc_ready, h0_ready, dz_ready = two("fc_ready"), two("h0_ready", credit=1), two("dz_ready")
        r_ready, h_ready = two("r_ready", per=STEPS), two("h_ready", credit=1, per=STEPS)
        turned = two("turned", credit=1, per=STEPS + 1)
        hF_high, hF_low = two("hF_high", per=STEPS), two("hF_low", per=STEPS)
        hT_high, hT_low = two("hT_high", per=STEPS), two("hT_low", per=STEPS)
        x_done = two("x_done", credit=1)

        with nc.Block() as block:
            @block.scalar
            def _(a):
                a.activation(sig[:, :], res["alpha"][:, :], ACT.Sigmoid).then_inc(chain, 1)
                for t in range(T):
                    a.wait_ge(a_turned, t + 1)
                    a.activation(A_t.high[:, :, t * P:(t + 1) * P],
                                 bank[t][:, :].rearrange("p (m n) -> p m n", m=T), ACT.Copy)\
                        .then_inc(a_copied, 1)
                a.wait_ge(w_ready, 1)
                a.activation(W.high[:, :], bank[4][:, 0:P], ACT.Copy).then_inc(a_copied, 1)

            @block.vector
            def _(v):
                v.wait_ge(chain, 1)
                v.tensor_scalar(s_alpha[:, :], sig[:, :], 0.5 * DT, None, ALU.mult).then_inc(chain, 1)
                v.tensor_scalar(dclip[:, :], res["L2_gnn_d"][:, :], 0.0, 1.0, ALU.max, ALU.min)\
                    .then_inc(chain, 1)
                v.wait_ge(chain, 3)
                v.tensor_scalar(diag[:, :], s_alpha[:, :], -1.0, 1.0 - DT, ALU.mult, ALU.add)
                v.tensor_scalar(wd[:, :], res["L2_gnn_wT"][:, :], dclip[:, 0:1], DT, ALU.mult, ALU.mult)
                for t in range(T):
                    ins = v.tensor_scalar(A_n[:, t, :], res["adj_n"][:, t, :], s_alpha[:, t:t + 1], None,
                                          ALU.mult)
                ins.then_inc(chain, 1)
                v.wait_ge(chain, 4)
                for t in range(T):
                    ins = v.scalar_tensor_tensor(out=A_n[:, t, t * P:(t + 1) * P], in0=res["ident"][:, :],
                                                 scalar=diag[:, t:t + 1],
                                                 in1=A_n[:, t, t * P:(t + 1) * P],
                                                 op0=ALU.mult, op1=ALU.add)
                ins.then_inc(chain, 1)
                for t in range(T):
                    v.wait_ge(a_copied, t + 1)
                    v.tensor_tensor(A_t.low[:, :, t * P:(t + 1) * P],
                                    bank[t][:, :].rearrange("p (m n) -> p m n", m=T),
                                    A_t.high[:, :, t * P:(t + 1) * P], ALU.subtract)
                v.wait_ge(a_copied, T + 1)
                v.tensor_tensor(W.low[:, :], bank[4][:, 0:P], W.high[:, :], ALU.subtract)

            @block.tensor
            def _(pe):
                pe.wait_ge(chain, 5)
                pe.matmul(bank[4][:, 0:P], wd[:, :], res["L2_gnn_wT"][:, :], start=True, stop=True)\
                    .then_inc(w_ready, 1)
                for t in range(T):
                    for m in range(T):
                        ins = pe.transpose(bank[t][:, m * P:(m + 1) * P], A_n[:, t, m * P:(m + 1) * P],
                                           res["ident"][:, :])
                    ins.then_inc(a_turned, 1)

        with nc.Block() as block:
            @block.tensor
            def _(pe):
                def turn(j, q, s):
                    if s == 0:
                        pe.wait_ge(h0_ready[q].sem, h0_ready[q].done(j))
                        pe.wait_ge(x_done[q].sem, x_done[q].freed(j))
                    else:
                        pe.wait_ge(h_ready[q].sem, h_ready[q].done(j, s))
                        pe.wait_ge(hT_low[q].sem, hT_low[q].done(j, s))
                    for t in range(T):
                        ins = pe.transpose(TB[q][:, t * P:(t + 1) * P], hF[q][:, t * P:(t + 1) * P],
                                           res["ident"][:, :])
                    ins.then_inc(turned[q].sem, 1)

                def step_high(j, q, s):
                    if s == 0:
                        pe.wait_ge(h_ready[q].sem, h_ready[q].done(j, 0))
                    pe.wait_ge(hF_high[q].sem, hF_high[q].done(j, s + 1))
                    pe.wait_ge(hF_low[q].sem, hF_low[q].done(j, s + 1))
                    matmul_halves(pe, R[q][:, :], (W.high[:, :], W.low[:, :]),
                                  (hF_parts[q].high[:, :], hF_parts[q].low[:, :]), True, False)
                    pe.wait_ge(hT_high[q].sem, hT_high[q].done(j, s + 1))
                    for m in range(T):
                        pe.matmul(R[q][:, :], hT_parts[q].high[:, m, :], A_t.high[:, m, :],
                                  start=False, stop=False)
                        pe.matmul(R[q][:, :], hT_parts[q].high[:, m, :], A_t.low[:, m, :],
                                  start=False, stop=False)

                def step_low(j, q, s):
                    pe.wait_ge(hT_low[q].sem, hT_low[q].done(j, s + 1))
                    for m in range(T):
                        ins = pe.matmul(R[q][:, :], hT_parts[q].low[:, m, :], A_t.high[:, m, :],
                                        start=False, stop=(m == T - 1))
                    ins.then_inc(r_ready[q].sem, 1)

                def front(j):
                    for q in range(2):
                        fr.tensor(pe, j * 2 + q, q)

                def main(j, nxt):
                    for q in range(2):
                        pe.wait_ge(fr.zF_ready.sem, fr.zF_ready.done(j * 2 + q))
                        if q == 1:
                            pe.wait_ge(h0_ready[0].sem, h0_ready[0].done(j))
                        else:
                            pe.wait_ge(h0_ready[1].sem, h0_ready[1].done(j, 0))
                        pe.matmul(FC[:, :], res["fc_in_wT"][:, :], fr.zF[q][:, :], start=True, stop=True)\
                            .then_inc(fc_ready[q].sem, 1)
                    turn(j, 0, 0)
                    for s in range(STEPS):
                        step_high(j, 0, s)
                        turn(j, 1, s)
                        step_low(j, 0, s)
                        step_high(j, 1, s)
                        turn(j, 0, s + 1)
                        step_low(j, 1, s)
                        if nxt is not None and s in (4, 5):
                            fr.tensor(pe, nxt * 2 + (s - 4), s - 4)
                    turn(j, 1, STEPS)
                run_pairs(pe, front, main)

            @block.scalar
            def _(a):
                def turned_high(j, q, s):
                    a.wait_ge(turned[q].sem, turned[q].done(j, s + 1))
                    a.activation(hT_parts[q].high[:, :, :],
                                 TB[q][:, :].rearrange("p (t d) -> p t d", t=T), ACT.Copy)\
                        .then_inc(hT_high[q].sem, 1)

                def high(j, q, s):
                    a.wait_ge(*((h0_ready[q].sem, h0_ready[q].done(j)) if s == 0 else
                                (h_ready[q].sem, h_ready[q].done(j, s))))
                    a.activation(hF_parts[q].high[:, :], hF[q][:, :], ACT.Copy).then_inc(hF_high[q].sem, 1)

                def front(j):
                    for q in range(2):
                        fr.scalar(a, j * 2 + q, q)

                def main(j, nxt):
                    for q in range(2):
                        a.wait_ge(fc_ready[q].sem, fc_ready[q].done(j))
                        a.wait_ge(turned[q].sem, turned[q].done(j, 0))
                        a.activation(hF[q][:, :], FC[:, :], ACT.Identity,
                                     bias=res["L2_gnn_fc_in_b"][:, 0:1]).then_inc(h0_ready[q].sem, 1)
                        high(j, q, 0)
                    turned_high(j, 0, 0)
                    for q in range(2):
                        a.wait_ge(h_ready[q].sem, h_ready[q].done(j, 0))
                        a.activation(dz[q][:, :], fr.zF[q][:, :], ACT.Copy, scale=DT)\
                            .then_inc(dz_ready[q].sem, 1)
                    for s in range(STEPS):
                        turned_high(j, 1, s)
                        if s + 1 < STEPS:
                            high(j, 0, s + 1)
                            turned_high(j, 0, s + 1)
                            high(j, 1, s + 1)
                        if nxt is not None and s in (4, 5):
                            fr.scalar(a, nxt * 2 + (s - 4), s - 4)
                run_pairs(a, front, main)

            @block.vector
            def _(v):
                def front(j):
                    for q in range(2):
                        fr.vector_stats(v, j * 2 + q, q)
                        fr.vector_apply(v, j * 2 + q, q)

                def add(j, q, s):
                    v.wait_ge(r_ready[q].sem, r_ready[q].done(j, s + 1))
                    if s == 0:
                        v.wait_ge(dz_ready[q].sem, dz_ready[q].done(j))
                    v.tensor_tensor(hF[q][:, :], R[q][:, :], dz[q][:, :], ALU.add)\
                        .then_inc(h_ready[q].sem, 1)

                def low(j, q, s):
                    v.wait_ge(hF_high[q].sem, hF_high[q].done(j, s + 1))
                    v.tensor_tensor(hF_parts[q].low[:, :], hF[q][:, :], hF_parts[q].high[:, :],
                                    ALU.subtract).then_inc(hF_low[q].sem, 1)

                def turned_low(j, q, s):
                    v.wait_ge(hT_high[q].sem, hT_high[q].done(j, s + 1))
                    v.tensor_tensor(hT_parts[q].low[:, :, :],
                                    TB[q][:, :].rearrange("p (t d) -> p t d", t=T),
                                    hT_parts[q].high[:, :, :], ALU.subtract).then_inc(hT_low[q].sem, 1)

                def main(j, nxt):
                    low(j, 0, 0)
                    low(j, 1, 0)
                    turned_low(j, 0, 0)
                    for s in range(STEPS):
                        add(j, 0, s)
                        turned_low(j, 1, s)
                        if s + 1 < STEPS:
                            low(j, 0, s + 1)
                        add(j, 1, s)
                        if s + 1 < STEPS:
                            turned_low(j, 0, s + 1)
                            low(j, 1, s + 1)
                        if nxt is not None and s in (2, 3):
                            fr.vector_stats(v, nxt * 2 + (s - 2), s - 2)
                        if nxt is not None and s in (3, 4):
                            fr.vector_apply(v, nxt * 2 + (s - 3), s - 3)
                    for q in range(2):
                        v.wait_ge(turned[q].sem, turned[q].done(j))
                        v.tensor_tensor(X[:, j * 2 + q, :, :], X[:, j * 2 + q, :, :],
                                        TB[q][:, :].rearrange("p (t d) -> p t d", t=T), ALU.add)\
                            .then_inc(x_done[q].sem, 1)
                run_pairs(v, front, main)

            @block.gpsimd
            def _(g):
                credit(g, ctx)

                def front(j):
                    for q in range(2):
                        fr.gpsimd(g, j * 2 + q, q)

                def main(j, nxt):
                    if nxt is not None:
                        front(nxt)
                run_pairs(g, front, main)



CHUNK = N // B
PIECE = 8


def lstm(nc, res, X):
    with Stage(nc) as ctx:
        G = res["psum"][:, :, :].rearrange("p (a g) n -> p a g n", a=2)
        sb = lambda n, s: ctx.enter_context(nc.sbuf_tensor("l_" + n, s, F32))
        c = lambda n, **k: Count(ctx, nc, "l_" + n, **k)
        seq = sb("seq", [P, N + 1, B])
        bank = lambda i: G[:, i // 4, i % 4, :]

        with Stage(nc) as inner:
            fr = Front(inner, nc, res, X, None, tag="l_")
            fr.z_turned.credit = 2
            turned_read = Count(inner, nc, "l_turned_read", credit=1)
            with nc.Block() as block:
                def each(eng, body):
                    with eng.Fori(0, B // 2) as j:
                        body(j * 2, 0)
                        body(j * 2 + 1, 1)

                @block.vector
                def _(v):
                    def apply(b, q):
                        v.wait_ge(fr.z_turned.sem, fr.z_turned.freed(b))
                        fr.vector_apply(v, b, q)

                    fr.vector_stats(v, 0, 0)
                    with v.Fori(0, B // 2 - 1) as j:
                        fr.vector_stats(v, j * 2 + 1, 1)
                        apply(j * 2, 0)
                        fr.vector_stats(v, j * 2 + 2, 0)
                        apply(j * 2 + 1, 1)
                    fr.vector_stats(v, B - 1, 1)
                    apply(B - 2, 0)
                    apply(B - 1, 1)

                @block.gpsimd
                def _(g):
                    credit(g, inner)
                    each(g, lambda b, q: fr.gpsimd(g, b, q))

                @block.tensor
                def _(pe):
                    def turn(b, q):
                        pe.wait_ge(fr.z_ready.sem, fr.z_ready.done(b))
                        pe.wait_ge(turned_read.sem, turned_read.freed(b))
                        for t in range(T):
                            ins = pe.transpose(bank(q)[:, t * P:(t + 1) * P], fr.z[q][:, t, :],
                                               res["ident"][:, :])
                        ins.then_inc(fr.z_turned.sem, 1)
                    each(pe, turn)

                @block.scalar
                def _(a):
                    def copy(b, q):
                        a.wait_ge(fr.z_turned.sem, fr.z_turned.done(b))
                        a.activation(seq[:, 1:N + 1, b], bank(q), ACT.Copy).then_inc(turned_read.sem, 1)
                    each(a, copy)

        with Stage(nc) as inner:
            sb2 = lambda n, s: inner.enter_context(nc.sbuf_tensor("l_" + n, s, F32))
            sem = lambda n: inner.sem("l_" + n)
            ones = sb2("ones", [1, PIECE * B])
            b_sum = sb2("b_sum", [1, 4 * D])
            zeros = sb2("zeros", [P, P])
            sig_if, gc = sb2("sig_if", [P, 2, B]), sb2("gc", [P, 2, B])
            prods, sig_o, tanh_c = sb2("prods", [P, 2, B]), sb2("sig_o", [P, B]), sb2("tanh_c", [P, B])
            started = sem("started")
            i_f_ready, g_ready, o_ready = sem("i_f_ready"), sem("g_ready"), sem("o_ready")
            if_g_done, tanh_c_done = sem("if_g_done"), sem("tanh_c_done")
            prods_done, c_done, h_done = sem("prods_done"), sem("c_done"), sem("h_done")

            def chunks(eng, step):
                last = N // CHUNK // 2 - 1

                def two(t0, more):
                    for par in range(2):
                        for s in range(CHUNK):
                            step(t0 + par * CHUNK + s, s, par, more or par == 0)
                with eng.Fori(0, last) as j:
                    two(j * (2 * CHUNK), True)
                two(last * 2 * CHUNK, False)

            with nc.Block() as block:
                @block.tensor
                def _(pe):
                    def piece(t, n, par):
                        gate, k, kind = n // 8, n % 8 // 2, n % 2
                        o = G[:, par, gate, k * P:(k + 1) * P]
                        cols = slice(gate * D, (gate + 1) * D)
                        if kind == 0:
                            pe.matmul(o, b_sum[0:1, cols], ones[0:1, :], start=(k == 0), stop=False,
                                      skip_group_check=True)
                        else:
                            pe.matmul(o, res["W_ihT"][:, cols], seq[:, bass.ds(t + k * PIECE + 1, PIECE), :],
                                      start=False, stop=False, skip_group_check=True)

                    def fill(n, s, par):
                        for _ in range(n):
                            pe.matmul(G[:, par, s // 8, s % 8 // 2 * P:(s % 8 // 2 + 1) * P],
                                      zeros[:, :], res["W_ihT"][:, 0:P], start=False, stop=False,
                                      skip_group_check=True)

                    def step(t, s, par, more):
                        pe.wait_ge(h_done, t + 1)
                        for gate, ready in ((0, None), (1, i_f_ready), (2, g_ready), (3, o_ready)):
                            ins = pe.matmul(G[:, par, gate, s * B:(s + 1) * B],
                                            res["W_hhT"][:, gate * D:(gate + 1) * D],
                                            seq[:, t, :],
                                            start=False, stop=True, skip_group_check=True)
                            if ready is not None:
                                ins.then_inc(ready, 1)
                        if more:
                            piece(t - s + CHUNK, s, 1 - par)
                        fill(FILLERS, s, 1 - par)

                    pe.wait_ge(started, 4)
                    for n in range(32):
                        piece(0, n, 0)
                    fill(16, 31, 0)
                    chunks(pe, step)

                @block.scalar
                def _(a):
                    def step(t, s, par, more):
                        cols = slice(s * B, (s + 1) * B)
                        a.wait_ge(i_f_ready, t + 1)
                        a.activation(sig_if[:, :, :], G[:, par, 0:2, cols], ACT.Sigmoid)
                        a.wait_ge(g_ready, t + 1)
                        a.activation(gc[:, 0, :], G[:, par, 2, cols], ACT.Tanh).then_inc(if_g_done, 1)
                        a.wait_ge(o_ready, t + 1)
                        a.activation(sig_o[:, :], G[:, par, 3, cols], ACT.Sigmoid)
                        a.wait_ge(c_done, t + 2)
                        a.activation(tanh_c[:, :], gc[:, 1, :], ACT.Tanh).then_inc(tanh_c_done, 1)
                    chunks(a, step)

                @block.vector
                def _(v):
                    v.memset(seq[:, 0, :], 0.0).then_inc(h_done, 1)
                    v.memset(gc[:, 1, :], 0.0).then_inc(c_done, 1)
                    v.memset(ones[:, :], 1.0).then_inc(started, 1)
                    v.memset(zeros[:, :], 0.0).then_inc(started, 1)
                    v.tensor_tensor(b_sum[:, :], res["b_ih"][:, :], res["b_hh"][:, :], ALU.add)\
                        .then_inc(started, 2)

                    def step(t, s, par, more):
                        v.wait_ge(c_done, t + 1)
                        v.wait_ge(if_g_done, t + 1)
                        v.tensor_tensor(prods[:, :, :], sig_if[:, :, :], gc[:, :, :], ALU.mult)\
                            .then_inc(prods_done, 1)
                        v.wait_ge(prods_done, t + 1)
                        v.tensor_tensor(gc[:, 1, :], prods[:, 0, :], prods[:, 1, :], ALU.add)\
                            .then_inc(c_done, 1)
                        v.wait_ge(tanh_c_done, t + 1)
                        v.tensor_tensor(seq[:, t + 1, :], sig_o[:, :], tanh_c[:, :], ALU.mult)\
                            .then_inc(h_done, 1)
                    chunks(v, step)

        with Stage(nc) as inner:
            sb2 = lambda n, s: inner.enter_context(nc.sbuf_tensor("l_" + n, s, F32))
            c2 = lambda n, **k: Count(inner, nc, "l_" + n, **k)
            wrep, ones = sb2("wrep", [P, 2, P]), sb2("ones_n", [P, N])
            hc, h2 = res["front_zF"], [z[:, :, :].rearrange("p t d -> p (t d)") for z in res["front_z"]]
            l0 = [sb2(f"l0{i}", [P, N]) for i in range(2)]
            g, w, inc, pre = (sb2(n, [P, N]) for n in ("g", "w", "inc", "pre"))
            suf = g
            oF = [sb2(f"oF{i}", [P, N]) for i in range(2)]
            rep = c2("rep", per=1)
            hc_ready, logits_ready, l0_ready = c2("hc_ready"), c2("logits_ready"), c2("l0_ready")
            ch = Chain(inner, nc, "l_sums", 5)
            oF_ready, oF_turned, x_done = c2("oF_ready", credit=1), c2("oF_turned"), c2("x_done", credit=1)
            LG = [[bank(0), bank(1)], [bank(2), bank(3)]]
            OT = [bank(4), bank(5)]
            with nc.Block() as block:
                @block.tensor
                def _(pe):
                    def logits(b, q):
                        pe.wait_ge(hc_ready.sem, hc_ready.done(b))
                        for k in range(2):
                            ins = pe.matmul(LG[q][k], wrep[:, k, :], hc[q][:, :], start=True, stop=True)
                        ins.then_inc(logits_ready.sem, 1)

                    def main(b, q, nxt):
                        if nxt:
                            logits(*nxt)
                        pe.wait_ge(oF_ready.sem, oF_ready.done(b))
                        pe.wait_ge(x_done.sem, x_done.freed(b))
                        for t in range(T):
                            ins = pe.transpose(OT[q][:, t * P:(t + 1) * P], oF[q][:, t * P:(t + 1) * P],
                                               res["ident"][:, :])
                        ins.then_inc(oF_turned.sem, 1)
                    pe.wait_ge(rep.sem, 2)
                    run_front_and_main(pe, logits, main)

                @block.gpsimd
                def _(g):
                    credit(g, inner)

                @block.scalar
                def _(a):
                    def copy(b, q):
                        a.activation(hc[q][:, :], seq[:, 1:N + 1, b], ACT.Copy).then_inc(hc_ready.sem, 1)
                        a.activation(h2[q][:, :], seq[:, 1:N + 1, b], ACT.Copy, scale=2.0)
                        a.wait_ge(logits_ready.sem, logits_ready.done(b))
                        a.activation(l0[q][:, :], LG[q][0], ACT.Identity, bias=res["b_lin"][:, 0:1])\
                            .then_inc(l0_ready.sem, 1)

                    def main(b, q, nxt):
                        if nxt:
                            a.wait_ge(oF_ready.sem, oF_ready.freed(b))
                            copy(*nxt)
                    run_front_and_main(a, copy, main)

                @block.vector
                def _(v):
                    v.memset(ones[:, :], 1.0).then_inc(rep.sem, 1)
                    v.tensor_copy(wrep[:, :, :], res["W_linT"][:, :].unsqueeze(2).broadcast_to([P, 2, P]))\
                        .then_inc(rep.sem, 1)
                    v.wait_ge(rep.sem, 2)

                    def main(b, q, nxt):
                        ch.begin(b)
                        v.wait_ge(l0_ready.sem, l0_ready.done(b))
                        v.wait_ge(oF_ready.sem, oF_ready.freed(b))
                        ch.link(v, v.scalar_tensor_tensor(
                            out=g[:, :], in0=LG[q][1], scalar=res["b_lin"][:, 1:2], in1=l0[q][:, :],
                            op0=ALU.add, op1=ALU.is_gt))
                        ch.link(v, v.tensor_tensor(w[:, :], g[:, :], hc[q][:, :], ALU.mult))
                        ch.link(v, v.tensor_tensor_scan(inc[:, :], ones[:, :], w[:, :], 0.0,
                                                        ALU.mult, ALU.add))
                        v.tensor_scalar(suf[:, :], inc[:, :], inc[:, N - 1:N], -1.0,
                                        ALU.subtract, ALU.mult)
                        ch.link(v, v.tensor_tensor(pre[:, :], inc[:, :], w[:, :], ALU.subtract))
                        ch.link(v, v.scalar_tensor_tensor(
                            out=pre[:, :], in0=pre[:, :], scalar=res["fw_att"][:, 0:1], in1=h2[q][:, :],
                            op0=ALU.mult, op1=ALU.add))
                        v.scalar_tensor_tensor(
                            out=oF[q][:, :], in0=suf[:, :], scalar=res["bw_att"][:, 0:1], in1=pre[:, :],
                            op0=ALU.mult, op1=ALU.add).then_inc(oF_ready.sem, 1)
                        v.wait_ge(oF_turned.sem, oF_turned.done(b))
                        v.tensor_tensor(X[:, b, :, :], X[:, b, :, :],
                                        OT[q].rearrange("p (t d) -> p t d", t=T), ALU.add)\
                            .then_inc(x_done.sem, 1)
                        ch.end()
                    run_front_and_main(v, lambda b, q: None, main)



def window_lstms(nc, res, X):
    STEPS_P = [(p, s) for p in range(1, 5) for s in range(p)]
    gates_of = lambda s: ("i", "g", "o") if s == 0 else ("i", "g", "f", "o")
    at = {"i": 0, "f": 1, "g": 2, "o": 3}
    place = {"i": 0, "g": 1, "o": 2, "f": 3}
    GATES = sum(len(gates_of(s)) for _, s in STEPS_P)
    RAISES = sum(2 + (s > 0) for _, s in STEPS_P)
    with Stage(nc) as ctx:
        G = [res["bank"][0:4], res["bank"][4:8]]
        sb = lambda n, s: ctx.enter_context(nc.sbuf_tensor("w_" + n, s, F32))
        c = lambda n, **k: Count(ctx, nc, "w_" + n, **k)
        two_sb = lambda n, s: [sb(f"{n}{q}", s) for q in range(2)]
        two = lambda n, **k: [c(f"{n}{q}", **k) for q in range(2)]
        fr = Front(ctx, nc, res, X, None, tag="w_")
        bsum = sb("bsum", [P, 4, 4])
        uT, h1F, hF = two_sb("uT", [P, T, D]), two_sb("h1F", [P, N]), two_sb("hF", [P, N])
        gate = {k: two_sb("gate_" + k, [P, N]) for k in "igfo"}
        cell, state = two_sb("cell", [P, N]), two_sb("state", [P, N // 2])
        bsum_ready = c("bsum_ready")
        u_ready, u_copied = two("u_ready", per=2), two("u_copied", per=2)
        c_ready, c_copied = two("c_ready", per=2, credit=1), two("c_copied", per=2)
        gate_ready = two("gate_ready", per=GATES)
        act_done = two("act_done", per=RAISES)
        parts_done = two("parts_done", per=len(STEPS_P) - 4)
        cell_done, h_done = two("cell_done", per=len(STEPS_P)), two("h_done", per=len(STEPS_P))
        h_turned, x_done = two("h_turned"), two("x_done", credit=1)
        windows = lambda p: N // p
        cols = lambda p, s: bass.ds(s, windows(p), p) if p > 1 else slice(0, N)

        def steps():
            g = r = f = 0
            for n, (p, s) in enumerate(STEPS_P):
                yield n, p, s, g, r, f
                g += len(gates_of(s))
                r += 2 + (s > 0)
                f += s > 0

        with nc.Block() as block:
            @block.tensor
            def _(pe):
                def lin(j, q, k):
                    if k == 0:
                        pe.wait_ge(fr.zF_ready.sem, fr.zF_ready.done(j * 2 + q))
                        pe.wait_ge(x_done[q].sem, x_done[q].freed(j))
                    else:
                        pe.wait_ge(c_copied[q].sem, c_copied[q].done(j, 1))
                    src = (fr.zF[q], h1F[q])[k]
                    w = res[("L3_gnn_Wg0", "L3_gnn_Wg1")[k]]
                    for t in range(T):
                        ins = pe.matmul(G[q][3][:, t * P:(t + 1) * P], src[:, t * P:(t + 1) * P], w[:, :],
                                        start=True, stop=True)
                    ins.then_inc(u_ready[q].sem, 1)

                def conv(j, q, k):
                    pe.wait_ge(u_copied[q].sem, u_copied[q].done(j, k + 1))
                    for m in range(T):
                        ins = pe.matmul(G[q][0][:, :], uT[q][:, m, :], res["adj_t"][:, m, :],
                                        start=(m == 0), stop=(m == T - 1))
                    ins.then_inc(c_ready[q].sem, 1)

                def step(j, q, n, p, s):
                    if n == 0:
                        pe.wait_ge(c_copied[q].sem, c_copied[q].done(j, 2))
                    else:
                        pe.wait_ge(h_done[q].sem, h_done[q].done(j, n))
                    nw = windows(p)
                    x = hF[q][:, cols(p, s)]
                    for k in gates_of(s):
                        o = G[q][place[k]][:, 0:nw]
                        wc = slice(at[k] * D, (at[k] + 1) * D)
                        ins = pe.matmul(o, res["WihT"][:, p - 1, wc], x, start=True, stop=(s == 0))
                        if s > 0:
                            ins = pe.matmul(o, res["WhhT"][:, p - 1, wc], state[q][:, 0:nw],
                                            start=False, stop=True)
                        ins.then_inc(gate_ready[q].sem, 1)

                def front(j):
                    for q in range(2):
                        turn_z(j, q)

                def turn_z(j, q):
                    b = j * 2 + q
                    pe.wait_ge(fr.z_ready.sem, fr.z_ready.done(b))
                    for t in range(T):
                        ins = pe.transpose(G[q][3][:, t * P:(t + 1) * P], fr.z[q][:, t, :],
                                           res["ident"][:, :])
                    ins.then_inc(fr.z_turned.sem, 1)

                def main(j, nxt):
                    for k in range(2):
                        for q in range(2):
                            lin(j, q, k)
                        for q in range(2):
                            conv(j, q, k)
                    for n, p, s, *_ in steps():
                        for q in range(2):
                            if n == 2 and nxt is not None:
                                pe.wait_ge(fr.zF_ready.sem, fr.zF_ready.done(nxt * 2 + q))
                            step(j, q, n, p, s)
                        if n == 0 and nxt is not None:
                            front(nxt)
                    for q in range(2):
                        pe.wait_ge(h_done[q].sem, h_done[q].done(j))
                        for t in range(T):
                            ins = pe.transpose(G[q][3][:, t * P:(t + 1) * P], hF[q][:, t * P:(t + 1) * P],
                                               res["ident"][:, :])
                        ins.then_inc(h_turned[q].sem, 1)
                run_pairs(pe, front, main)

            @block.scalar
            def _(a):
                def copy_z(j):
                    for q in range(2):
                        b = j * 2 + q
                        a.wait_ge(fr.z_turned.sem, fr.z_turned.done(b))
                        a.activation(fr.zF[q][:, :], G[q][3][:, :], ACT.Copy).then_inc(fr.zF_ready.sem, 1)

                def main(j, nxt):
                    for k in range(2):
                        for q in range(2):
                            a.wait_ge(c_ready[q].sem, c_ready[q].done(j, k + 1))
                            a.activation((h1F, hF)[k][q][:, :], G[q][0][:, :], ACT.Relu)\
                                .then_inc(c_copied[q].sem, 1)

                    def gates(q, n, p, s, g0):
                        nw = windows(p)
                        for i, k in enumerate(gates_of(s)):
                            a.wait_ge(gate_ready[q].sem, gate_ready[q].done(j, g0 + i + 1))
                            ins = a.activation(gate[k][q][:, 0:nw], G[q][place[k]][:, 0:nw],
                                               ACT.Tanh if k == "g" else ACT.Sigmoid,
                                               bias=bsum[:, p - 1, at[k]:at[k] + 1])
                            if k in "gf":
                                ins.then_inc(act_done[q].sem, 1)

                    def tanh(q, n, p):
                        nw = windows(p)
                        a.wait_ge(cell_done[q].sem, cell_done[q].done(j, n + 1))
                        a.activation(gate["g"][q][:, 0:nw], cell[q][:, 0:nw], ACT.Tanh)\
                            .then_inc(act_done[q].sem, 1)

                    for n, p, s, g0, *_ in steps():
                        gates(0, n, p, s, g0)
                        tanh(0, n, p)
                        gates(1, n, p, s, g0)
                        tanh(1, n, p)
                        if n == 0 and nxt is not None:
                            copy_z(nxt)

                a.wait_ge(bsum_ready.sem, 1)
                run_pairs(a, copy_z, main)

            @block.vector
            def _(v):
                v.tensor_tensor(bsum[:, :, :], res["bih"][:, :, :], res["bhh"][:, :, :], ALU.add)\
                    .then_inc(bsum_ready.sem, 1)

                def front(j):
                    for q in range(2):
                        fr.vector_stats(v, j * 2 + q, q)
                        fr.vector_apply(v, j * 2 + q, q)

                def main(j, nxt):
                    for k in range(2):
                        for q in range(2):
                            v.wait_ge(u_ready[q].sem, u_ready[q].done(j, k + 1))
                            v.wait_ge(c_ready[q].sem, c_ready[q].done(j, k))
                            bias = res[("row_L3_gnn_bg0", "row_L3_gnn_bg1")[k]]
                            v.tensor_tensor(uT[q][:, :, :], G[q][3][:, :].rearrange("p (t d) -> p t d", t=T),
                                            bias[:, :].unsqueeze(1).broadcast_to([P, T, D]), ALU.add)\
                                .then_inc(u_copied[q].sem, 1)
                        if k == 0 and nxt is not None:
                            front(nxt)

                    def cell_of(q, n, p, s, r0, f0):
                        nw = windows(p)
                        i, g, f = (gate[k][q][:, 0:nw] for k in "igf")
                        cc = cell[q][:, 0:nw]
                        v.wait_ge(act_done[q].sem, act_done[q].done(j, r0 + 1))
                        if s == 0:
                            v.tensor_tensor(cc, i, g, ALU.mult).then_inc(cell_done[q].sem, 1)
                        else:
                            v.tensor_tensor(i, i, g, ALU.mult)
                            v.wait_ge(act_done[q].sem, act_done[q].done(j, r0 + 2))
                            v.tensor_tensor(cc, f, cc, ALU.mult).then_inc(parts_done[q].sem, 1)
                            v.wait_ge(parts_done[q].sem, parts_done[q].done(j, f0 + 1))
                            v.tensor_tensor(cc, cc, i, ALU.add).then_inc(cell_done[q].sem, 1)

                    def h_of(q, n, p, s, r0):
                        nw = windows(p)
                        v.wait_ge(act_done[q].sem, act_done[q].done(j, r0 + 2 + (s > 0)))
                        out = hF[q][:, cols(p, s)] if s == p - 1 else state[q][:, 0:nw]
                        v.tensor_tensor(out, gate["o"][q][:, 0:nw], gate["g"][q][:, 0:nw], ALU.mult)\
                            .then_inc(h_done[q].sem, 1)

                    for n, p, s, g0, r0, f0 in steps():
                        for q in range(2):
                            cell_of(q, n, p, s, r0, f0)
                            h_of(q, n, p, s, r0)
                    for q in range(2):
                        v.wait_ge(h_turned[q].sem, h_turned[q].done(j))
                        v.tensor_tensor(X[:, j * 2 + q, :, :], X[:, j * 2 + q, :, :],
                                        G[q][3][:, :].rearrange("p (t d) -> p t d", t=T), ALU.add)\
                            .then_inc(x_done[q].sem, 1)
                run_pairs(v, front, main)

            @block.gpsimd
            def _(g):
                credit(g, ctx)

                def front(j):
                    for q in range(2):
                        fr.gpsimd(g, j * 2 + q, q)

                def main(j, nxt):
                    if nxt is not None:
                        front(nxt)
                run_pairs(g, front, main)



def attention(nc, res, X, X1):
    U = HEADS * T
    SCALE = float(HD) ** -0.5
    with Stage(nc) as ctx:
        bank = res["bank"]
        sb = lambda n, s: ctx.enter_context(nc.sbuf_tensor("a_" + n, s, F32))
        c = lambda n, **k: Count(ctx, nc, "a_" + n, **k)
        two_sb = lambda n, s: [sb(f"{n}{q}", s) for q in range(2)]
        PJ, S, PT, O = bank[0:3], bank[3:5], bank[5:7], bank[7]
        fr = Front(ctx, nc, res, X, None, tag="a_")
        h, ms, ve2 = two_sb("h", [P, T, D]), sb("ms", [P, T]), sb("ve2", [P, T])
        rstd2 = sb("rstd2", [P, T])
        qF, kF, vT = two_sb("qF", [P, N]), two_sb("kF", [P, N]), two_sb("vT", [P, T, 64])
        rot_a, rot_b = sb("rot_a", [P, N]), sb("rot_b", [P, N])
        sm, prob, probT = two_sb("sm", [P, N]), two_sb("prob", [P, N]), two_sb("probT", [P, T, P])
        top, ntop = two_sb("top", [P, U]), two_sb("ntop", [P, U])
        total, rtotal = two_sb("total", [P, U]), sb("rtotal", [P, U])
        rsums, rsumsF, yF = sb("rsums", [P, T, D]), sb("rsumsF", [P, N]), sb("yF", [P, N])
        ms_ready, ve2_ready, rstd2_ready = c("ms_ready"), c("ve2_ready"), c("rstd2_ready")
        h_ready, h_turned, hF_ready = c("h_ready"), c("h_turned"), c("hF_ready")
        qk_ready = c("qk_ready", per=4)
        rotated = c("rotated", per=4)
        qk_done = c("qk_done", per=2, credit=1)
        v_ready, v_copied = c("v_ready"), c("v_copied")
        s_ready = c("s_ready", per=U)
        masked = c("masked", per=U, credit=2)
        ntop_ready = c("ntop_ready", per=U)
        prob_ready = c("prob_ready", per=U, credit=2)
        turned = c("turned", per=U, credit=2)
        probT_ready = c("probT_ready", per=U, credit=2)
        o_ready = c("o_ready", per=U, credit=2)
        rtotal_ready, rsums_ready, rsums_turned = c("rtotal_ready"), c("rsums_ready"), c("rsums_turned")
        rsumsF_ready, y_scaled = c("rsumsF_ready"), c("y_scaled", credit=1)
        wo_ready, x1_ready, x_done = c("wo_ready"), c("x1_ready"), c("x_done")

        def run(eng, front, main):
            front(0, 0)
            main(0, 0, (1, 1), None)
            with eng.Fori(0, B // 2 - 1) as j:
                main(j * 2 + 1, 1, (j * 2 + 2, 0), (j * 2, 0))
                main(j * 2 + 2, 0, (j * 2 + 3, 1), (j * 2 + 1, 1))
            main(B - 1, 1, None, (B - 2, 0))
            main(None, None, None, (B - 1, 1))

        with nc.Block() as block:
            @block.tensor
            def _(pe):
                def turn_h(b, q):
                    pe.wait_ge(h_ready.sem, h_ready.done(b))
                    for t in range(T):
                        ins = pe.transpose(PJ[0][:, t * P:(t + 1) * P], h[q][:, t, :], res["ident"][:, :])
                    ins.then_inc(h_turned.sem, 1)

                def project(b, q, k):
                    pe.wait_ge(hF_ready.sem, hF_ready.done(b))
                    if k < 2:
                        if k == 1:
                            pe.wait_ge(rotated.sem, rotated.done(b, 2))
                        for i, w in enumerate((("wqT", "wqrT"), ("wkT", "wkrT"))[k]):
                            pe.matmul(PJ[1 + i][:, :], res[w][:, :], fr.zF[q][:, :], start=True, stop=True)\
                                .then_inc(qk_ready.sem, 1)
                    else:
                        for t in range(T):
                            ins = pe.matmul(PJ[0][:, t * 64:(t + 1) * 64], fr.zF[q][:, t * P:(t + 1) * P],
                                            res["wvT"][:, :], start=True, stop=True)
                        ins.then_inc(v_ready.sem, 1)

                def scores(b, q, u):
                    hd, t = u // T, u % T
                    rows = slice(hd * HD, (hd + 1) * HD)
                    if u == 0:
                        pe.wait_ge(qk_done.sem, qk_done.done(b))
                    pe.wait_ge(masked.sem, masked.freed(b, u + 1))
                    pe.matmul(S[u % 2][:, 0:(t + 1) * P], qF[q][rows, t * P:(t + 1) * P],
                              kF[q][rows, 0:(t + 1) * P], start=True, stop=True).then_inc(s_ready.sem, 1)

                def turn(b, q, u):
                    pe.wait_ge(prob_ready.sem, prob_ready.done(b, u + 1))
                    pe.wait_ge(probT_ready.sem, probT_ready.freed(b, u + 1))
                    for m in range(u % T + 1):
                        ins = pe.transpose(PT[u % 2][:, m * P:(m + 1) * P],
                                           prob[u % 2][:, m * P:(m + 1) * P], res["ident"][:, :])
                    ins.then_inc(turned.sem, 1)

                def attend(b, q, u):
                    hd, t = u // T, u % T
                    kv = hd // 2 * HD
                    if u == 0:
                        pe.wait_ge(v_copied.sem, v_copied.done(b))
                        pe.wait_ge(y_scaled.sem, y_scaled.freed(b))
                    pe.wait_ge(probT_ready.sem, probT_ready.done(b, u + 1))
                    for m in range(t + 1):
                        ins = pe.matmul(O[hd * HD:(hd + 1) * HD, t * P:(t + 1) * P],
                                        vT[q][:, m, kv:kv + HD], probT[u % 2][:, m, :],
                                        start=(m == 0), stop=(m == t))
                    ins.then_inc(o_ready.sem, 1)

                def tail(b, q, k):
                    if k == 0:
                        pe.wait_ge(rsums_ready.sem, rsums_ready.done(b))
                        for t in range(T):
                            ins = pe.transpose(PJ[1][:, t * P:(t + 1) * P], rsums[:, t, :],
                                               res["ident"][:, :])
                        ins.then_inc(rsums_turned.sem, 1)
                    else:
                        pe.wait_ge(y_scaled.sem, y_scaled.done(b))
                        for t in range(T):
                            ins = pe.matmul(PJ[2][:, t * P:(t + 1) * P], yF[:, t * P:(t + 1) * P],
                                            res["woT"][:, :], start=True, stop=True)
                        ins.then_inc(wo_ready.sem, 1)

                def front(b, q):
                    turn_h(b, q)
                    for k in range(3):
                        project(b, q, k)
                    scores(b, q, 0)
                    scores(b, q, 1)

                def main(b, q, nxt, prev):
                    for u in range(U):
                        if prev and u == 0:
                            tail(*prev, 0)
                        if prev and u == 2:
                            tail(*prev, 1)
                        if b is None:
                            continue
                        if u + 2 < U:
                            scores(b, q, u + 2)
                        elif nxt:
                            scores(*nxt, u + 2 - U)
                        if nxt and u == 9:
                            turn_h(*nxt)
                        if nxt and u == 10:
                            if prev:
                                pe.wait_ge(x1_ready.sem, x1_ready.done(prev[0]))
                            project(*nxt, 0)
                        if nxt and u == 12:
                            project(*nxt, 1)
                        if nxt and u == 13:
                            project(*nxt, 2)
                        turn(b, q, u)
                        if u:
                            attend(b, q, u - 1)
                    if b is not None:
                        attend(b, q, U - 1)
                run(pe, front, main)

            @block.scalar
            def _(a):
                def copy_h(b, q):
                    a.wait_ge(h_turned.sem, h_turned.done(b))
                    a.activation(fr.zF[q][:, :], PJ[0][:, :], ACT.Copy, scale=res["ln1_w"][:, 0:1])\
                        .then_inc(hF_ready.sem, 1)

                def copy_v(b, q):
                    a.wait_ge(v_ready.sem, v_ready.done(b))
                    a.activation(vT[q][:, :, :], PJ[0][:, 0:T * 64].rearrange("p (t d) -> p t d", t=T),
                                 ACT.Copy).then_inc(v_copied.sem, 1)

                def copy(b, q, u):
                    w = (u % T + 1) * P
                    a.wait_ge(turned.sem, turned.done(b, u + 1))
                    a.wait_ge(o_ready.sem, o_ready.freed(b, u + 1))
                    a.activation(probT[u % 2][:, 0:u % T + 1, :],
                                 PT[u % 2][:, 0:w].rearrange("p (m n) -> p m n", n=P), ACT.Copy)\
                        .then_inc(probT_ready.sem, 1)

                def exp(b, q, u):
                    w = (u % T + 1) * P
                    a.wait_ge(ntop_ready.sem, ntop_ready.done(b, u + 1))
                    a.wait_ge(turned.sem, turned.freed(b, u + 1))
                    at = u % T * HEADS + u // T
                    a.activation(prob[u % 2][:, 0:w], sm[u % 2][:, 0:w], ACT.Exp, scale=SCALE,
                                 bias=ntop[q][:, u:u + 1], accum_out=total[q][:, at:at + 1])\
                        .then_inc(prob_ready.sem, 1)

                def front(b, q):
                    copy_h(b, q)
                    copy_v(b, q)

                def main(b, q, nxt, prev):
                    for u in range(U):
                        if prev and u == 0:
                            a.wait_ge(rsums_turned.sem, rsums_turned.done(prev[0]))
                            a.activation(rsumsF[:, :], PJ[1][:, :], ACT.Copy)\
                                .then_inc(rsumsF_ready.sem, 1)
                        if b is None:
                            continue
                        exp(b, q, u)
                        if u:
                            copy(b, q, u - 1)
                        if nxt and u == 9:
                            copy_h(*nxt)
                        if nxt and u == 13:
                            copy_v(*nxt)
                    if b is not None:
                        copy(b, q, U - 1)
                run(a, front, main)

            @block.vector
            def _(v):
                def rms(b, q):
                    v.wait_ge(fr.z_ready.sem, fr.z_ready.done(b))
                    for t in range(T):
                        ins = v.tensor_tensor_reduce(h[q][:, t, :], fr.z[q][:, t, :], fr.z[q][:, t, :],
                                                     1.0, 0.0, ALU.mult, ALU.add, ms[:, t:t + 1])
                    ins.then_inc(ms_ready.sem, 1)

                def rms_apply(b, q):
                    v.wait_ge(rstd2_ready.sem, rstd2_ready.done(b))
                    for t in range(T):
                        ins = v.tensor_scalar(h[q][:, t, :], fr.z[q][:, t, :], rstd2[:, t:t + 1],
                                              float(D) ** 0.5, ALU.mult, ALU.mult)
                    ins.then_inc(h_ready.sem, 1)

                def rotate(b, q, k):
                    for i, (out, table) in enumerate(((rot_a, "cos"), (rot_b, "sin"))):
                        v.wait_ge(qk_ready.sem, qk_ready.done(b, 2 * k + i + 1))
                        if i == 0:
                            v.wait_ge(qk_done.sem, qk_done.done(b, k))
                        v.tensor_tensor(out[:, :], PJ[1 + i][:, :], res[table][:, :], ALU.mult)\
                            .then_inc(rotated.sem, 1)

                def mask(b, q, u):
                    w = (u % T + 1) * P
                    v.wait_ge(s_ready.sem, s_ready.done(b, u + 1))
                    v.wait_ge(prob_ready.sem, prob_ready.freed(b, u + 1))
                    hold(v, res)
                    v.tensor_tensor_reduce(sm[u % 2][:, 0:w], S[u % 2][:, 0:w], res["tri"][:, N - w:N],
                                           1.0, -3e38, ALU.add, ALU.max, top[q][:, u:u + 1])\
                        .then_inc(masked.sem, 1)
                    v.wait_ge(masked.sem, masked.done(b, u + 1))
                    v.tensor_scalar(ntop[q][:, u:u + 1], top[q][:, u:u + 1], -SCALE, None, ALU.mult)\
                        .then_inc(ntop_ready.sem, 1)

                def finish(b, q):
                    v.wait_ge(prob_ready.sem, prob_ready.done(b, U))
                    v.reciprocal(rtotal[:, :], total[q][:, :]).then_inc(rtotal_ready.sem, 1)
                    v.wait_ge(rtotal_ready.sem, rtotal_ready.done(b))
                    v.tensor_copy(rsums[:, :, :].rearrange("p t (h d) -> p (t h) d", d=HD),
                                  rtotal[:, :].unsqueeze(2).broadcast_to([P, U, HD]))\
                        .then_inc(rsums_ready.sem, 1)

                def scale(b):
                    v.wait_ge(rsumsF_ready.sem, rsumsF_ready.done(b))
                    v.wait_ge(o_ready.sem, o_ready.done(b, U))
                    v.tensor_tensor(yF[:, :], O[:, :], rsumsF[:, :], ALU.mult).then_inc(y_scaled.sem, 1)

                def tail(b, q):
                    v.wait_ge(wo_ready.sem, wo_ready.done(b))
                    v.tensor_tensor(X1[:, b, :, :], PJ[2][:, :].rearrange("p (t d) -> p t d", t=T),
                                    fr.z[q][:, :, :], ALU.add).then_inc(x1_ready.sem, 1)

                def front(b, q):
                    fr.vector_stats(v, b, q)
                    fr.vector_apply(v, b, q)
                    rms(b, q)
                    rms_apply(b, q)
                    rotate(b, q, 0)
                    rotate(b, q, 1)
                    mask(b, q, 0)

                def main(b, q, nxt, prev):
                    for u in range(U):
                        if prev and u == 3:
                            tail(*prev)
                        if b is None:
                            if u == 0:
                                scale(prev[0])
                            continue
                        if u + 1 < U:
                            mask(b, q, u + 1)
                        elif nxt:
                            mask(*nxt, 0)
                        if prev and u == 0:
                            scale(prev[0])
                        if not nxt:
                            continue
                        if u == 3:
                            fr.vector_stats(v, *nxt)
                        if u == 5:
                            fr.vector_apply(v, *nxt)
                        if u == 6:
                            rms(*nxt)
                        if u == 8:
                            rms_apply(*nxt)
                        if u == 10:
                            rotate(*nxt, 0)
                        if u == 12:
                            rotate(*nxt, 1)
                    if b is not None:
                        finish(b, q)
                run(v, front, main)

            @block.gpsimd
            def _(g):
                credit(g, ctx)

                def rotate(b, q, k):
                    g.wait_ge(rotated.sem, rotated.done(b, 2 * k + 2))
                    g.tensor_tensor((qF, kF)[k][q][:, :], rot_a[:, :], rot_b[:, :], ALU.add)\
                        .then_inc(qk_done.sem, 1)

                def front(b, q):
                    fr.gpsimd(g, b, q)
                    g.wait_ge(ms_ready.sem, ms_ready.done(b))
                    g.tensor_tensor(ve2[:, :], ms[:, :], res["eps_rms"][:, :], ALU.add)\
                        .then_inc(ve2_ready.sem, 1)
                    g.wait_ge(ve2_ready.sem, ve2_ready.done(b))
                    g.tensor_tensor(rstd2[:, :], ve2[:, :], res["nhalf"][:, :], ALU.pow)\
                        .then_inc(rstd2_ready.sem, 1)

                    rotate(b, q, 0)
                    rotate(b, q, 1)

                def main(b, q, nxt, prev):
                    if prev:
                        b0 = prev[0]
                        g.wait_ge(x1_ready.sem, x1_ready.done(b0))
                        g.tensor_tensor(X[:, b0, :, :], X[:, b0, :, :], X1[:, b0, :, :], ALU.add)\
                            .then_inc(x_done.sem, 1)
                    if nxt:
                        front(*nxt)
                run(g, front, main)



def program(nc, ap, out):
    with ExitStack() as late:
        with ExitStack() as middle:
            with ExitStack() as early:
                res = load_all(late, middle, early, nc, ap)
                X = res["X"]
                graph_convolution(nc, res, res["adj_t"], X)
                mixture(nc, res, X, "m0_", {k: res["L0_" + k] for k in ("Wg", "W1", "b1", "W2", "b2")},
                        [P, P], ACT.Relu, "logits", None, (res["L0_bg"], res["L0_bias"]), True, False)
                graph_attention(nc, res, X)
                mixture(nc, res, X, "m1_", {k: res["L1_" + k] for k in ("Wg", "W1", "b1", "W2", "b2")},
                        [P], ACT.Gelu, "probs", (ALU.max, 1e-12), None, True, True, halves=False)
                diffusion(nc, res, X)
                lstm(nc, res, X)
            window_lstms(nc, res, X)
        X1 = late.enter_context(nc.sbuf_tensor("r_X1", [P, B, T, D], F32))
        attention(nc, res, X, X1)
        mixture(nc, res, X, "m3_", {k: res["L3_" + k] for k in ("Wg", "W1", "W3", "W2")},
                [P, P, 341 - 2 * P], ACT.Silu, "probs", (ALU.add, 1e-9), None, False, False,
                src=X1, kind="rms", weight=res["ln2_w"][:, 0:1],
                x_out=out.rearrange("b (t p) d -> p b t d", p=P))


def layouts(i):
    import numpy as np
    t = lambda a: np.ascontiguousarray(a)
    g = {k: np.asarray(a) for k, a in i.items()}
    d = {}
    for n in ("x", "adj", "L0_gnn_w1_loop", "L0_gnn_w1_neigh", "L0_gnn_b1", "L0_gnn_w2_loop",
              "L0_gnn_w2_neigh", "L0_gnn_b2", "L0_ffn_Wg", "L0_ffn_bg", "L0_ffn_bias", "L0_ffn_W1",
              "L0_ffn_W2", "L0_ffn_b2", "L1_gnn_W", "L1_gnn_b_lin", "L1_gnn_b", "L1_ffn_w1", "L1_ffn_w2",
              "L1_ffn_b2", "L2_gnn_d", "L2_gnn_fc_in_b",
              "L2_ffn_b_ih", "L2_ffn_b_hh", "L2_ffn_b_lin", "L3_gnn_Wg0", "L3_gnn_bg0", "L3_gnn_Wg1",
              "L3_gnn_bg1"):
        d[n] = t(g[n])
    d["alpha"] = t(g["L2_gnn_alpha_train"].reshape(T, P).T)
    d["adj_t"] = t(g["adj"].T)
    d["L2_gnn_wT"] = t(g["L2_gnn_w"].T)
    d["fc_in_wT"] = t(g["L2_gnn_fc_in_w"].T)
    d["fw_att"], d["bw_att"] = t(g["L2_ffn_fw_att"][0]), t(g["L2_ffn_bw_att"][0])
    d["ln1_w"], d["ln2_w"] = t(g["L3_ffn_ln1_w"]), t(g["L3_ffn_ln2_w"])
    d["L0_b1c"] = t(g["L0_ffn_b1"].reshape(E, 2, P).transpose(2, 0, 1))
    d["L1_router_wT"] = t(g["L1_ffn_router_w"].T)
    d["L1_b1c"] = t(g["L1_ffn_b1"].reshape(E, 1, P).transpose(2, 0, 1))
    d["W_ihT"], d["W_hhT"] = t(g["L2_ffn_W_ih"].T), t(g["L2_ffn_W_hh"].T)
    d["W_linT"] = t(g["L2_ffn_W_lin"].T)
    d["WihT"] = t(g["L3_gnn_Wih"].transpose(2, 0, 1))
    d["WhhT"] = t(g["L3_gnn_Whh"].transpose(2, 0, 1))
    d["bihc"] = t(g["L3_gnn_bih"].reshape(4, 4, P).transpose(2, 0, 1))
    d["bhhc"] = t(g["L3_gnn_bhh"].reshape(4, 4, P).transpose(2, 0, 1))
    swap = np.arange(P) ^ (HD // 2)
    wq, wk = g["L3_ffn_wq"], g["L3_ffn_wk"]
    wk = np.repeat(wk.reshape(2, HD, D), 2, axis=0).reshape(P, D)
    d["wqT"], d["wqrT"], d["wkT"], d["wkrT"] = t(wq.T), t(wq[swap].T), t(wk.T), t(wk[swap].T)
    d["wvT"], d["woT"] = t(g["L3_ffn_wv"].T), t(g["L3_ffn_wo"].T)
    freq = 1.0 / 10000.0 ** (np.arange(0, HD, 2, dtype=np.float32) / HD)
    angle = np.outer(np.arange(N, dtype=np.float32), freq)
    angle = np.concatenate([angle, angle], axis=-1).T
    sign = np.where(np.arange(HD) < HD // 2, -1.0, 1.0)[:, None]
    d["cos_table"] = np.tile(np.cos(angle), (HEADS, 1)).astype(np.float32)
    d["sin_table"] = np.tile(np.sin(angle) * sign, (HEADS, 1)).astype(np.float32)
    d["L3_router_wT"] = t(g["L3_ffn_router_w"].T)
    d["L3_w1T"] = t(g["L3_ffn_w1"].transpose(2, 0, 1))
    d["L3_w3T"] = t(g["L3_ffn_w3"].transpose(2, 0, 1))
    d["L3_w2T"] = t(g["L3_ffn_w2"].transpose(0, 2, 1))
    return d


def kernel(**inputs):
    import concourse.bacc as bacc
    from concourse.bass_utils import run_bass_kernel_spmd

    nc = bacc.Bacc("TRN2", target_bir_lowering=False, num_devices=1)
    arrays, ap = {}, {}
    for name, a in layouts(inputs).items():
        arrays["in_" + name] = a
        ap[name] = nc.dram_tensor("in_" + name, a.shape, mybir.dt.from_np(a.dtype), kind="ExternalInput").ap()
    out = nc.dram_tensor("out_x", (B, N, D), F32, kind="ExternalOutput").ap()
    program(nc, ap, out)
    return run_bass_kernel_spmd(nc, [arrays], core_ids=[0]).results[0]["out_x"]
```
